# Optimizing a Trainium2 kernel written in Bass

```python
import numpy as np
import jax
import jax.numpy as jnp

def _softmax(x, axis=-1):
    return jax.nn.softmax(x, axis=axis)

def _gelu(x):
    return jax.nn.gelu(x, approximate=True)

def _silu(x):
    return jax.nn.silu(x)

def _sigmoid(x):
    return jax.nn.sigmoid(x)

def _layernorm(x, axis=-1, eps=1e-05):
    m = jnp.mean(x, axis=axis, keepdims=True)
    v = jnp.var(x, axis=axis, keepdims=True)
    return (x - m) / jnp.sqrt(v + eps)

def _scatter_add(tgt, idx, src, axis=0):
    return tgt.at[idx].add(src)

def _segment_sum(src, seg, n):
    return jax.ops.segment_sum(src, seg, n)
kernel_name = 'mk_gps_d1_gnn_r8_869160'

def setup_inputs(seed: int=0):
    np.random.seed(seed)
    _w = jnp.asarray

    def _rec_inputs():
        import jax
        import jax.numpy as jnp
        _gk = jax.random.key(seed)
        x = -8.776e-05 + 1 * jax.random.normal(jax.random.fold_in(_gk, 1), (6250, 256), jnp.float32)
        src = jax.random.randint(jax.random.fold_in(_gk, 2), (100000,), 0, 6250, jnp.int32)
        dst = jnp.minimum((6250 * jax.random.uniform(jax.random.fold_in(_gk, 3), (100000,)) ** 2.0).astype(jnp.int32), 49999)
        _o = jnp.argsort(dst, stable=True)
        src = src[_o]
        dst = dst[_o]
        edge_attr_64 = 0.000279952 + 1.00013 * jax.random.normal(jax.random.fold_in(_gk, 11), (100000, 64), jnp.float32)
        return (x, src, dst, edge_attr_64)
    x, src, dst, edge_attr_64 = _rec_inputs()

    def _L0_gnn_setup():
        import jax, jax.numpy as jnp
        import numpy as np
        N, E = (2500, 40000)
        IN_CH, EDGE_DIM = (256, 64)
        HEADS, OUT_CH = (8, 32)
        HC = HEADS * OUT_CH
        key = jax.random.key(seed)
        ks = jax.random.split(key, 12)
        s_in = 1.0 / np.sqrt(IN_CH)
        s_e = 1.0 / np.sqrt(EDGE_DIM)
        return {'x': jax.random.normal(ks[0], (N, IN_CH), dtype=jnp.float32), 'edge_index': jax.random.randint(ks[1], (2, E), 0, N, dtype=jnp.int64), 'edge_attr': jax.random.normal(ks[2], (E, EDGE_DIM), dtype=jnp.float32), 'Wq': jax.random.uniform(ks[3], (HC, IN_CH), jnp.float32, -s_in, s_in), 'bq': jnp.zeros((HC,), jnp.float32), 'Wk': jax.random.uniform(ks[4], (HC, IN_CH), jnp.float32, -s_in, s_in), 'bk': jnp.zeros((HC,), jnp.float32), 'Wv': jax.random.uniform(ks[5], (HC, IN_CH), jnp.float32, -s_in, s_in), 'bv': jnp.zeros((HC,), jnp.float32), 'We': jax.random.uniform(ks[6], (HC, EDGE_DIM), jnp.float32, -s_e, s_e), 'Wskip': jax.random.uniform(ks[7], (HC, IN_CH), jnp.float32, -s_in, s_in), 'bskip': jnp.zeros((HC,), jnp.float32)}
    _L0_gnn_all = _L0_gnn_setup()
    _L0_gnn_in = {k: v for k, v in _L0_gnn_all.items() if k in ('Wq', 'bq', 'Wk', 'bk', 'Wv', 'bv', 'We', 'Wskip', 'bskip')}
    del _L0_gnn_all

    def _L0_mix_setup():
        import jax, jax.numpy as jnp
        import numpy as np
        D_MODEL = 256
        NHEAD = 8
        D_HEAD = D_MODEL // NHEAD
        DIM_FF = 1024
        B, L = (4, 2048)
        LN_EPS = 1e-05

        def _layernorm(x, g, b):
            mu = jnp.mean(x, axis=-1, keepdims=True)
            var = jnp.mean((x - mu) ** 2, axis=-1, keepdims=True)
            return (x - mu) * jax.lax.rsqrt(var + LN_EPS) * g + b

        def _phi(x):
            return jnp.where(x > 0, x + 1.0, jnp.exp(x))
        key = jax.random.key(seed)
        ks = jax.random.split(key, 16)
        s_in = 1.0 / np.sqrt(D_MODEL)
        s_ff = 1.0 / np.sqrt(DIM_FF)
        inp = {'x': jax.random.normal(ks[0], (B, L, D_MODEL), dtype=jnp.float32), 'Wq': jax.random.normal(ks[1], (D_MODEL, D_MODEL), dtype=jnp.float32) * s_in, 'bq': jnp.zeros((D_MODEL,), jnp.float32), 'Wk': jax.random.normal(ks[2], (D_MODEL, D_MODEL), dtype=jnp.float32) * s_in, 'bk': jnp.zeros((D_MODEL,), jnp.float32), 'Wv': jax.random.normal(ks[3], (D_MODEL, D_MODEL), dtype=jnp.float32) * s_in, 'bv': jnp.zeros((D_MODEL,), jnp.float32), 'Wo': jax.random.normal(ks[4], (D_MODEL, D_MODEL), dtype=jnp.float32) * s_in, 'bo': jnp.zeros((D_MODEL,), jnp.float32), 'W1': jax.random.normal(ks[5], (D_MODEL, DIM_FF), dtype=jnp.float32) * s_in, 'b1': jnp.zeros((DIM_FF,), jnp.float32), 'W2': jax.random.normal(ks[6], (DIM_FF, D_MODEL), dtype=jnp.float32) * s_ff, 'b2': jnp.zeros((D_MODEL,), jnp.float32), 'ln1_g': jnp.ones((D_MODEL,), jnp.float32), 'ln1_b': jnp.zeros((D_MODEL,), jnp.float32), 'ln2_g': jnp.ones((D_MODEL,), jnp.float32), 'ln2_b': jnp.zeros((D_MODEL,), jnp.float32)}
        return inp
    _L0_mix_all = _L0_mix_setup()
    _L0_mix_in = {k: v for k, v in _L0_mix_all.items() if k in ('Wq', 'bq', 'Wk', 'bk', 'Wv', 'bv', 'Wo', 'bo', 'W1', 'b1', 'W2', 'b2', 'ln1_g', 'ln1_b', 'ln2_g', 'ln2_b')}
    del _L0_mix_all

    def _L0_ffn_setup():
        import jax, jax.numpy as jnp
        import numpy as np
        BN_EPS = 0.001

        def _bn(h, g, b, m, v):
            return g * (h - m) * jax.lax.rsqrt(v + BN_EPS) + b
        key = jax.random.key(seed)
        ks = jax.random.split(key, 8)
        B, F, Df = (256, 64, 256)
        E, H, D = (8, 256, 256)
        s1 = 1.0 / np.sqrt(Df)
        s2 = 1.0 / np.sqrt(H)
        return {'x': jax.random.normal(ks[0], (B, F, Df), jnp.float32), 'Wr': jax.random.normal(ks[1], (Df, E), jnp.float32) * s1, 'br': jnp.zeros((E,), jnp.float32), 'W1': jax.random.normal(ks[2], (E, Df, H), jnp.float32) * s1, 'b1': jnp.zeros((E, H), jnp.float32), 'g1': jnp.ones((E, H), jnp.float32), 'be1': jnp.zeros((E, H), jnp.float32), 'm1': jnp.zeros((E, H), jnp.float32), 'v1': jnp.ones((E, H), jnp.float32), 'W2': jax.random.normal(ks[3], (E, H, H), jnp.float32) * s2, 'b2': jnp.zeros((E, H), jnp.float32), 'g2': jnp.ones((E, H), jnp.float32), 'be2': jnp.zeros((E, H), jnp.float32), 'm2': jnp.zeros((E, H), jnp.float32), 'v2': jnp.ones((E, H), jnp.float32), 'Wo': jax.random.normal(ks[4], (E, H, D), jnp.float32) * s2, 'bo': jnp.zeros((E, D), jnp.float32)}
    _L0_ffn_all = _L0_ffn_setup()
    _L0_ffn_in = {k: v for k, v in _L0_ffn_all.items() if k in ('Wr', 'br', 'W1', 'b1', 'g1', 'be1', 'm1', 'v1', 'W2', 'b2', 'g2', 'be2', 'm2', 'v2', 'Wo', 'bo')}
    del _L0_ffn_all
    return {'x': x, 'src': src, 'dst': dst, 'edge_attr_64': edge_attr_64, 'L0_gnn_Wq': _L0_gnn_in['Wq'], 'L0_gnn_bq': _L0_gnn_in['bq'], 'L0_gnn_Wk': _L0_gnn_in['Wk'], 'L0_gnn_bk': _L0_gnn_in['bk'], 'L0_gnn_Wv': _L0_gnn_in['Wv'], 'L0_gnn_bv': _L0_gnn_in['bv'], 'L0_gnn_We': _L0_gnn_in['We'], 'L0_gnn_Wskip': _L0_gnn_in['Wskip'], 'L0_gnn_bskip': _L0_gnn_in['bskip'], 'L0_mix_Wq': _L0_mix_in['Wq'], 'L0_mix_bq': _L0_mix_in['bq'], 'L0_mix_Wk': _L0_mix_in['Wk'], 'L0_mix_bk': _L0_mix_in['bk'], 'L0_mix_Wv': _L0_mix_in['Wv'], 'L0_mix_bv': _L0_mix_in['bv'], 'L0_mix_Wo': _L0_mix_in['Wo'], 'L0_mix_bo': _L0_mix_in['bo'], 'L0_mix_W1': _L0_mix_in['W1'], 'L0_mix_b1': _L0_mix_in['b1'], 'L0_mix_W2': _L0_mix_in['W2'], 'L0_mix_b2': _L0_mix_in['b2'], 'L0_mix_ln1_g': _L0_mix_in['ln1_g'], 'L0_mix_ln1_b': _L0_mix_in['ln1_b'], 'L0_mix_ln2_g': _L0_mix_in['ln2_g'], 'L0_mix_ln2_b': _L0_mix_in['ln2_b'], 'L0_ffn_Wr': _L0_ffn_in['Wr'], 'L0_ffn_br': _L0_ffn_in['br'], 'L0_ffn_W1': _L0_ffn_in['W1'], 'L0_ffn_b1': _L0_ffn_in['b1'], 'L0_ffn_g1': _L0_ffn_in['g1'], 'L0_ffn_be1': _L0_ffn_in['be1'], 'L0_ffn_m1': _L0_ffn_in['m1'], 'L0_ffn_v1': _L0_ffn_in['v1'], 'L0_ffn_W2': _L0_ffn_in['W2'], 'L0_ffn_b2': _L0_ffn_in['b2'], 'L0_ffn_g2': _L0_ffn_in['g2'], 'L0_ffn_be2': _L0_ffn_in['be2'], 'L0_ffn_m2': _L0_ffn_in['m2'], 'L0_ffn_v2': _L0_ffn_in['v2'], 'L0_ffn_Wo': _L0_ffn_in['Wo'], 'L0_ffn_bo': _L0_ffn_in['bo']}

def reference(x, src, dst, edge_attr_64, L0_gnn_Wq, L0_gnn_bq, L0_gnn_Wk, L0_gnn_bk, L0_gnn_Wv, L0_gnn_bv, L0_gnn_We, L0_gnn_Wskip, L0_gnn_bskip, L0_mix_Wq, L0_mix_bq, L0_mix_Wk, L0_mix_bk, L0_mix_Wv, L0_mix_bv, L0_mix_Wo, L0_mix_bo, L0_mix_W1, L0_mix_b1, L0_mix_W2, L0_mix_b2, L0_mix_ln1_g, L0_mix_ln1_b, L0_mix_ln2_g, L0_mix_ln2_b, L0_ffn_Wr, L0_ffn_br, L0_ffn_W1, L0_ffn_b1, L0_ffn_g1, L0_ffn_be1, L0_ffn_m1, L0_ffn_v1, L0_ffn_W2, L0_ffn_b2, L0_ffn_g2, L0_ffn_be2, L0_ffn_m2, L0_ffn_v2, L0_ffn_Wo, L0_ffn_bo):
    import jax
    import jax.numpy as jnp

    def _L0_gnn_ref(x, edge_index, edge_attr, Wq, bq, Wk, bk, Wv, bv, We, Wskip, bskip):
        import jax, jax.numpy as jnp
        import numpy as np
        N, E = (2500, 40000)
        IN_CH, EDGE_DIM = (256, 64)
        HEADS, OUT_CH = (8, 32)
        HC = HEADS * OUT_CH
        n = x.shape[0]
        src, dst = (edge_index[0], edge_index[1])
        q = (x @ Wq.T + bq).reshape(n, HEADS, OUT_CH)
        k = (x @ Wk.T + bk).reshape(n, HEADS, OUT_CH)
        v = (x @ Wv.T + bv).reshape(n, HEADS, OUT_CH)
        e = (edge_attr @ We.T).reshape(-1, HEADS, OUT_CH)
        k_e = k[src] + e
        v_e = v[src] + e
        alpha = jnp.einsum('ehc,ehc->eh', q[dst], k_e) / jnp.sqrt(jnp.float32(OUT_CH))
        m = jax.ops.segment_max(alpha, dst, num_segments=n)
        m = jnp.where(jnp.isfinite(m), m, 0.0)
        p = jnp.exp(alpha - m[dst])
        s = jax.ops.segment_sum(p, dst, num_segments=n)
        w = p / (s[dst] + 1e-16)
        out = jax.ops.segment_sum(v_e * w[:, :, None], dst, num_segments=n)
        out = out.reshape(n, HC) + (x @ Wskip.T + bskip)
        return out

    def _L0_mix_ref(x, Wq, bq, Wk, bk, Wv, bv, Wo, bo, W1, b1, W2, b2, ln1_g, ln1_b, ln2_g, ln2_b):
        import jax, jax.numpy as jnp
        import numpy as np
        D_MODEL = 256
        NHEAD = 8
        D_HEAD = D_MODEL // NHEAD
        DIM_FF = 1024
        B, L = (4, 2048)
        LN_EPS = 1e-05

        def _layernorm(x, g, b):
            mu = jnp.mean(x, axis=-1, keepdims=True)
            var = jnp.mean((x - mu) ** 2, axis=-1, keepdims=True)
            return (x - mu) * jax.lax.rsqrt(var + LN_EPS) * g + b

        def _phi(x):
            return jnp.where(x > 0, x + 1.0, jnp.exp(x))
        Bq, Lq, _ = x.shape
        q = (x @ Wq + bq).reshape(Bq, Lq, NHEAD, D_HEAD)
        k = (x @ Wk + bk).reshape(Bq, Lq, NHEAD, D_HEAD)
        v = (x @ Wv + bv).reshape(Bq, Lq, NHEAD, D_HEAD)
        q_phi = _phi(q)
        k_phi = _phi(k)
        kv = jnp.einsum('blhd,blhe->bhde', k_phi, v)
        k_sum = k_phi.sum(axis=1)
        z = 1.0 / (jnp.einsum('blhd,bhd->blh', q_phi, k_sum) + 1e-06)
        out = jnp.einsum('blhd,bhde,blh->blhe', q_phi, kv, z)
        out = out.reshape(Bq, Lq, D_MODEL) @ Wo + bo
        x = _layernorm(x + out, ln1_g, ln1_b)
        ff = jax.nn.relu(x @ W1 + b1) @ W2 + b2
        x = _layernorm(x + ff, ln2_g, ln2_b)
        return x

    def _L0_ffn_ref(x, Wr, br, W1, b1, g1, be1, m1, v1, W2, b2, g2, be2, m2, v2, Wo, bo):
        import jax, jax.numpy as jnp
        import numpy as np
        BN_EPS = 0.001

        def _bn(h, g, b, m, v):
            return g * (h - m) * jax.lax.rsqrt(v + BN_EPS) + b
        feat = jnp.mean(x, axis=0)
        w = jax.nn.softmax(feat @ Wr + br, axis=-1)
        h = jnp.einsum('bfd,edh->bfeh', x, W1) + b1
        h = jax.nn.relu(_bn(h, g1, be1, m1, v1))
        h = jnp.einsum('bfeh,ehk->bfek', h, W2) + b2
        h = jax.nn.relu(_bn(h, g2, be2, m2, v2))
        y = jnp.einsum('bfeh,ehd->bfed', h, Wo) + bo
        return jnp.einsum('bfed,fe->bfd', y, w)
    edge_index = jnp.stack([src, dst])
    xn = _layernorm(x, axis=-1)
    x = x + _L0_gnn_ref(xn, edge_index, edge_attr_64, L0_gnn_Wq, L0_gnn_bq, L0_gnn_Wk, L0_gnn_bk, L0_gnn_Wv, L0_gnn_bv, L0_gnn_We, L0_gnn_Wskip, L0_gnn_bskip) + _L0_mix_ref(xn[None], L0_mix_Wq, L0_mix_bq, L0_mix_Wk, L0_mix_bk, L0_mix_Wv, L0_mix_bv, L0_mix_Wo, L0_mix_bo, L0_mix_W1, L0_mix_b1, L0_mix_W2, L0_mix_b2, L0_mix_ln1_g, L0_mix_ln1_b, L0_mix_ln2_g, L0_mix_ln2_b)[0]
    x = x + _L0_ffn_ref(_layernorm(x, axis=-1)[None], L0_ffn_Wr, L0_ffn_br, L0_ffn_W1, L0_ffn_b1, L0_ffn_g1, L0_ffn_be1, L0_ffn_m1, L0_ffn_v1, L0_ffn_W2, L0_ffn_b2, L0_ffn_g2, L0_ffn_be2, L0_ffn_m2, L0_ffn_v2, L0_ffn_Wo, L0_ffn_bo)[0]
    return x

_drawn_inputs = setup_inputs


def setup_inputs(seed=0):
    import zlib

    import numpy as np

    out = dict(_drawn_inputs(seed))
    spreads = {'L0_gnn_bq': (0.0, 0.753),
     'L0_gnn_bk': (0.0, 0.8),
     'L0_gnn_bv': (0.0, 0.1),
     'L0_gnn_bskip': (0.0, 0.1),
     'L0_mix_bq': (0.0, 0.8),
     'L0_mix_bk': (0.0, 0.8),
     'L0_mix_bv': (0.0, 0.1),
     'L0_mix_bo': (0.0, 0.1),
     'L0_mix_b1': (0.0, 0.275),
     'L0_mix_b2': (0.0, 0.1),
     'L0_mix_ln1_g': (1.0, 0.2),
     'L0_mix_ln1_b': (0.0, 0.1),
     'L0_mix_ln2_g': (1.0, 0.2),
     'L0_mix_ln2_b': (0.0, 0.1),
     'L0_ffn_br': (0.0, 0.459),
     'L0_ffn_b1': (0.0, 0.636),
     'L0_ffn_g1': (1.0, 0.6),
     'L0_ffn_be1': (0.0, 0.656),
     'L0_ffn_m1': (0.0, 0.638),
     'L0_ffn_v1': (1.0, 0.6),
     'L0_ffn_b2': (0.0, 0.457),
     'L0_ffn_g2': (1.0, 0.587),
     'L0_ffn_be2': (0.0, 0.484),
     'L0_ffn_m2': (0.0, 0.469),
     'L0_ffn_v2': (1.0, 0.6),
     'L0_ffn_bo': (0.0, 0.34)}
    factors = {'L0_mix_Wq': 8.0, 'L0_mix_Wk': 8.0, 'L0_mix_Wv': 8.0}
    for name, (base, spread) in spreads.items():
        noise = np.random.default_rng([zlib.crc32(name.encode()), seed]).standard_normal(out[name].shape)
        drawn = base * np.exp(spread * noise) if base else spread * noise
        out[name] = jnp.asarray(drawn.astype(out[name].dtype))
    for name, factor in factors.items():
        out[name] = (out[name] * factor).astype(out[name].dtype)
    return out
```

```python
from contextlib import ExitStack

import numpy as np

import concourse.bass as bass
from concourse import mybir

F32 = mybir.dt.float32
I32 = mybir.dt.int32
ALU = mybir.AluOpType
ACT = mybir.ActivationFunctionType
AX = mybir.AxisListType.X

N, E_, D, ED = 6250, 100000, 256, 64
H, C = 8, 32
T = 125
NT, ET = N // T, E_ // T
BN = 2 * T
NB = N // BN
FF = 1024
NX = 8
LN_EPS, BN_EPS, Z_EPS, S_EPS = 1e-5, 1e-3, 1e-6, 1e-16
G = 4
GPI = ET // G // NB
RB = 4
CH = 16
CE = E_ // CH
CT = ET // CH
SU = 8
STEPS = ET + NT - 1
SI = -(-STEPS // SU)
SP_ = SI * SU
RW = H + 2
PV = D + H
WALK = SP_ + 8
LAG = 2
BIG = 1.0e30
SCALE = float(C) ** -0.5
RD = 4
R_GNN, R_MKV, R_BO, R_B2, R_G1, R_E1, R_G2, R_E2, R_BR = 0, 1024, 1536, 1792, 2048, 2304, 2560, 2816, 3072
ROWS = 3080
C_BQ, C_B1, C_FF = 0, 2, 10
COLS = 10 + 10 * 16


def wait(eng, sem, value):
    if isinstance(value, int) and value <= 0:
        return
    eng.wait_ge(sem, value)


class Order:

    def __init__(self, eng, sem):
        self.eng, self.sem, self.n = eng, sem, 0

    def __call__(self, ins):
        self.n += 1
        ins.then_inc(self.sem, 1)
        self.eng.wait_ge(self.sem, self.n)

    def reset(self):
        self.eng.sem_clear(self.sem)
        self.n = 0


def build(nc, a, out):
    ctx = ExitStack()
    with ctx:
        def sb(name, shape, dt=F32):
            return ctx.enter_context(nc.sbuf_tensor(name, shape, dt))

        def sem(name):
            return ctx.enter_context(nc.semaphore(name))

        def dram(name, shape, dt=F32):
            return nc.dram_tensor(name, shape, dt).ap()

        q_tab, k_tab, v_tab = dram("q_tab", (N, D)), dram("k_tab", (N, D)), dram("v_tab", (N, D))
        xn_d, xnt_d = dram("xn_d", (N, D)), dram("xnt_d", (2, 128, N))
        skip_d, res_d = dram("skip_d", (N, D)), dram("res_d", (N, D))
        walk_d, jb_d = dram("walk_d", (3, SP_), I32), dram("jb_d", (SI, SU))
        fence_d = dram("fence_d", (4, 128))

        region_x = sb("region_x", [128, NT * PV])
        region_s = sb("region_s", [128, 11400])
        weights = sb("weights", [128, 12288])
        rec = sb("rec", [T, ET, RW])
        rows = sb("rows", [T, ROWS])
        cols = sb("cols", [128, COLS])
        bns = sb("bns", [128, 2, 2, 16])
        ident = sb("ident", [128, 128])
        blockm = sb("blockm", [128, 128])
        iota = sb("iota", [T, T])
        we = sb("we", [ED, D])
        src_t, dst_t = sb("src_t", [T, ET], I32), sb("dst_t", [T, ET], I32)
        idx = sb("idx", [T, 2, 2, 16], I32)
        walk_i = sb("walk_i", [SI, 3, SU], I32)
        walk_s = sb("walk_s", [SI, 6, SU])
        kvbd = sb("kvbd", [128, 2, 128])
        ksbd = sb("ksbd", [128, 2, 128])
        wr = sb("wr", [128, 2, NX])
        bo_e = sb("bo_e", [NX, D])
        ends = sb("ends", [128, 8])
        fence = sb("fence", [H, 10, CH])
        stats = sb("stats", [T, 2, 16])
        ksum = sb("ksum", [128, 2])
        fsm = sb("fsm", [T, 2, 32])

        wcat = weights[:, 0:2048].rearrange("p (c n) -> p c n", c=2)
        wmkv = weights[:, 2048:3072].rearrange("p (c n) -> p c n", c=2)
        wmq = weights[:, 3072:3584].rearrange("p (c n) -> p c n", c=2)
        wmo = weights[:, 3584:4096].rearrange("p (c n) -> p c n", c=2)
        wm1 = weights[:, 4096:6144].rearrange("p (c n) -> p c n", c=2)
        wm2 = weights[:, 6144:8192].rearrange("p (c n) -> p c n", c=8)
        wx = [weights[:, 4096 * i:4096 * (i + 1)].rearrange("p (e c n) -> p e c n", e=NX, c=2) for i in range(3)]

        used = [0]

        def carve(start, *shape, parts=128):
            size = int(np.prod(shape))
            if start is not None:
                used[0] = start
            at = used[0]
            used[0] += size
            assert used[0] <= 11400, used
            flat = region_s[0:parts, at:at + size]
            if len(shape) == 1:
                return flat
            names = "abcd"[:len(shape)]
            return flat.rearrange(f"p ({' '.join(names)}) -> p {' '.join(names)}",
                                  **{n: s for n, s in zip(names[:-1], shape[:-1])})

        x_all = region_x[0:T, 0:NT * D].rearrange("p (t d) -> p t d", t=NT)
        xstat = sb("xstat", [T, NT, 4])
        xsix = sb("xsix", [T, 10, 6])
        xn = carve(0, 2, D, parts=T)
        xnt = carve(None, 2, 2, T)
        qkv = carve(None, 2, 3 * D, parts=T)
        skp = carve(None, 2, D, parts=T)
        kt = carve(None, 2, D, parts=T)
        kmin = carve(None, 2, D, parts=T)
        kexp = carve(None, 2, D, parts=T)
        kphi = carve(None, 2, D, parts=T)
        vone = carve(None, 2, 2, 129, parts=T)
        zero = carve(None, 129)
        assert used[0] <= 8200
        mxt = carve(0, 2, 2, BN)
        mxn = carve(None, 2, 2, D, parts=T)
        mres = carve(None, 2, 2, D, parts=T)
        mq = carve(None, 2, BN)
        mqn = carve(None, 2, BN)
        mqe = carve(None, 2, BN)
        mqp = carve(None, 2, BN)
        mz = carve(None, 2, BN)
        mat = carve(None, 2, BN)
        my = carve(None, 2, D, parts=T)
        mx1 = carve(None, 2, D, parts=T)
        mx1t = carve(None, 2, BN)
        mh = carve(None, 8, BN)
        my2 = carve(None, 2, D, parts=T)
        mout = carve(None, 2, D, parts=T)
        qg = region_x[0:T, 0:RB * G * D].rearrange("p (r g d) -> p r g d", r=RB, g=G)
        kg = region_x[0:T, RB * G * D:2 * RB * G * D].rearrange("p (r g d) -> p r g d", r=RB, g=G)
        atg = region_x[0:ED, 2 * RB * G * D:2 * RB * G * D + RB * G * T].rearrange("p (r n) -> p r n", r=RB)
        wf, wl = region_s[0:SI, 8200:8200 + ET], region_s[0:SI, 9000:9000 + ET]
        wz, wi = region_s[0:SI, 9800:9800 + ET].bitcast(I32), region_s[0:SI, 10600:10600 + ET].bitcast(I32)
        walk_k = sb("walk_k", [SI, 2 * SU], I32)
        scores = rec[:, :, :].rearrange("p e m -> p (e m)")[:, 0:ET * H]
        sc_a = region_x[:, 0:CE]
        sc_m = region_x[:, CE:2 * CE + 1]
        sc_f = region_s[:, 0:CE]
        sc_di = sc_f.bitcast(I32)
        jb_all = region_s[0:T, 6400:6400 + SP_]
        walk = region_s[0:1, 7400:7400 + 3 * WALK].bitcast(I32).rearrange("p (w n) -> p w n", w=3)
        acc = region_x[0:T, :].rearrange("p (t f) -> p t f", t=NT)
        vg = carve(0, RD, D, parts=T)
        pv = carve(None, RD, D + RW, parts=T)
        hot = carve(None, RD, T, parts=T)
        att = carve(None, RD, T, parts=ED)
        fres = carve(0, 2, 2, D, parts=T)
        fgn = carve(None, 2, D, parts=T)
        fx2 = carve(None, 2, 2, D, parts=T)
        fxn = carve(None, 2, D, parts=T)
        fxt = carve(None, 2, 2, BN)
        fh1 = carve(None, 3, 2, BN)
        fh2 = carve(None, 3, 2, BN)
        fw = carve(None, 2, 2, NX, parts=T)
        fwt = carve(None, 2, BN, parts=NX)
        fyb = carve(None, 2, 2, D, parts=T)

        psum = ctx.enter_context(nc.psum_tensor("psum", [128, 8, 512], F32))

        c_a, c_b, c_ff, c_walk = sem("const_a"), sem("const_b"), sem("const_ff"), sem("const_walk")
        dve_o, act_o, pool_o = sem("dve_order"), sem("act_order"), sem("pool_order")
        bn_ready = sem("bn_ready")
        x_in = [sem(f"x_in{i}") for i in range(5)]
        a_stored = [sem(f"a_stored{u}") for u in range(2)]
        xn_ready, xn_turned, xnt_ready = sem("xn_ready"), sem("xn_turned"), sem("xnt_ready")
        gnn_done, mkv_done, gnn_out = sem("gnn_done"), sem("mkv_done"), sem("gnn_out")
        kmin_ready, kexp_ready, kphi_ready, state_done = sem("kmin_ready"), sem("kexp_ready"), sem("kphi_ready"), sem("state_done")
        zero_ready, state_ready = sem("zero_ready"), sem("state_ready")
        m_in = [sem(f"m_in{u}") for u in range(2)]
        m_q, m_min, m_exp, m_phi = sem("m_q"), sem("m_min"), sem("m_exp"), sem("m_phi")
        m_nd, m_at, m_o, m_x1 = sem("m_nd"), sem("m_at"), sem("m_o"), sem("m_x1")
        m_t, m_tc, m_h, m_hr, m_y, m_outr = sem("m_t"), sem("m_tc"), sem("m_h"), sem("m_hr"), sem("m_y"), sem("m_outr")
        m_stored = sem("m_stored")
        gather_go = sem("gather_go")
        gathered = [sem(f"gathered{r}") for r in range(RB)]
        attr_in = [sem(f"attr_in{r}") for r in range(RB)]
        e_done, ke_done, score_done = sem("e_done"), sem("ke_done"), sem("score_done")
        turned, turned_out = sem("turned"), sem("turned_out")
        dst_in, mask_ready = sem("dst_in"), sem("mask_ready")
        fence_out, fence_in = sem("fence_out"), sem("fence_in")
        ends_ready, carry_ready, shifted, exped, back, back_out = (
            sem("ends_ready"), sem("carry_ready"), sem("shifted"), sem("exped"), sem("back"), sem("back_out"))
        last_in, walk_steps, walk_ready, walk_out, walk_in = (
            sem("last_in"), sem("walk_steps"), sem("walk_ready"), sem("walk_out"), sem("walk_in"))
        rec_ready, walk_clear = sem("rec_ready"), sem("walk_clear")
        acc_zero = sem("acc_zero")
        meta_ready = sem("meta_ready")
        v_in = [sem(f"v_in{r}") for r in range(RD)]
        att_in = [sem(f"att_in{r}") for r in range(RD)]
        ev_done, ve_done, pv_ready, sum_done, acc_done = sem("ev_done"), sem("ve_done"), sem("pv_ready"), sem("sum_done"), sem("acc_done")
        f_in = [sem(f"f_in{u}") for u in range(2)]
        f_xn, f_t, f_tc, f_lg, f_sm, f_ex, f_w = sem("f_xn"), sem("f_t"), sem("f_tc"), sem("f_lg"), sem("f_sm"), sem("f_ex"), sem("f_w")
        f_wt, f_wtc, f_h1, f_r1, f_h2, f_r2, f_y, f_ya = (
            sem("f_wt"), sem("f_wtc"), sem("f_h1"), sem("f_r1"), sem("f_h2"), sem("f_r2"), sem("f_y"), sem("f_ya"))
        f_bo, f_bo_done, f_outr = sem("f_bo"), sem("f_bo_done"), sem("f_outr")
        f_stored = [sem(f"f_stored{u}") for u in range(2)]

        CONST_A, CONST_B = 16 * 6, 16 * 8

        block = ctx.enter_context(nc.Block())

        def node_rows(t_expr, k=1):
            return bass.ds(t_expr * T, k * T)

        def twice(eng, n, body, order=()):
            body(0, 0)
            body(1, 1)
            for o in order:
                o.reset()
            with eng.Fori(1, n // 2) as it:
                body(it * 2, 0)
                body(it * 2 + 1, 1)
                for o in order:
                    o.reset()
            if n % 2:
                body(n - 1, 0)
                for o in order:
                    o.reset()

        @block.sync
        def _(sp):
            sp.dma_start(ident[:, :], a["ident"]).then_inc(c_a, 16)
            sp.dma_start(wcat, a["w_gnn"].rearrange("(c p) n -> p c n", p=128)).then_inc(c_a, 16)
            sp.dma_start(wmkv, a["w_mkv"].rearrange("(c p) n -> p c n", p=128)).then_inc(c_a, 16)
            sp.dma_start(rows[:, :], a["rows"]).then_inc(c_a, 16)
            sp.dma_start(cols[:, :], a["cols"]).then_inc(c_a, 16)
            sp.dma_start(blockm[:, :], a["blockm"]).then_inc(c_a, 16)

            for i in range(5):
                sp.dma_start(x_all[:, i * 10:(i + 1) * 10, :],
                             a["x"][i * 10 * T:(i + 1) * 10 * T, :].rearrange("(t p) d -> p t d", p=T)).then_inc(x_in[i], 16)

            def store_a(t, u):
                sp.wait_ge(xnt_ready, t + 1)
                sp.dma_start(xn_d[node_rows(t), :], xn[:, u, :]).then_inc(a_stored[u], 16)
                sp.dma_start(xnt_d[:, :, node_rows(t)].rearrange("c p n -> p c n"), xnt[:, u]).then_inc(a_stored[u], 16)
                sp.wait_ge(gnn_out, t + 1)
                for i, tab in enumerate((q_tab, k_tab, v_tab)):
                    sp.dma_start(tab[node_rows(t), :], qkv[:, u, i * D:(i + 1) * D]).then_inc(a_stored[u], 16)
                sp.dma_start(skip_d[node_rows(t), :], skp[:, u, :]).then_inc(a_stored[u], 16)

            twice(sp, NT, store_a)

            sp.dma_start(wmq, a["w_mq"].rearrange("(c p) n -> p c n", p=128)).then_inc(c_b, 16)
            sp.dma_start(wmo, a["w_mo"].rearrange("(c p) n -> p c n", p=128)).then_inc(c_b, 16)
            sp.dma_start(wm1, a["w_m1"].rearrange("(c p) n -> p c n", p=128)).then_inc(c_b, 16)
            sp.dma_start(wm2, a["w_m2"].rearrange("(c p) n -> p c n", p=128)).then_inc(c_b, 16)
            sp.dma_start(we[:, :], a["w_e"]).then_inc(c_b, 16)
            sp.dma_start(iota[:, :], a["iota"]).then_inc(c_b, 16)
            sp.dma_start(wr[:, :, :], a["w_r"].rearrange("(c p) n -> p c n", p=128)).then_inc(c_b, 16)
            sp.dma_start(bo_e[:, :], a["bo_e"]).then_inc(c_b, 16)

            sp.wait_ge(walk_ready, 1)
            sp.dma_start(walk_d.rearrange("w (i s) -> i w s", s=SU), walk_i[:, :, :]).then_inc(walk_out, 16)
            sp.dma_start(jb_d, walk_s[:, 3, :]).then_inc(walk_out, 16)

            for u in range(2):
                sp.wait_ge(a_stored[u], 16 * 6 * (NT // 2))
            sp.wait_ge(state_ready, 1)

            def load_mix(b, u):
                if not (isinstance(b, int) and b < 2):
                    sp.wait_ge(m_outr, b - 1)
                sp.dma_start(mxt[:, u], xnt_d[:, :, bass.ds(b * BN, BN)].rearrange("c p n -> p c n")).then_inc(m_in[u], 16)
                sp.dma_start(mxn[:, u], xn_d[bass.ds(b * BN, BN), :].rearrange("(t p) d -> p t d", p=T)).then_inc(m_in[u], 16)
                sp.dma_start(mres[:, u], skip_d[bass.ds(b * BN, BN), :].rearrange("(t p) d -> p t d", p=T)).then_inc(m_in[u], 16)

            attr_c = a["attr_t"].rearrange("f (c n) -> f c n", c=CH)

            def load_attr(gg, bt, r):
                if not (isinstance(gg, int) and gg < RB):
                    sp.wait_ge(e_done, gg - RB + 1)
                sp.dma_start(atg[:, r, :].rearrange("p (g t) -> p g t", g=G),
                             attr_c[:, G * r:G * (r + 1), bass.ds(bt * T, T)]).then_inc(attr_in[r], 16)

            def b_body(b, u):
                load_mix(b, u)
                for g in range(GPI):
                    load_attr(b * GPI + g, b * 2 + g // RB, g % RB)
                    if g == 2 and not (isinstance(b, int) and b == 0):
                        store_mix(b - 1)

            def store_mix(b):
                sp.wait_ge(m_outr, b + 1)
                sp.dma_start(res_d[bass.ds(b * BN, BN), :].rearrange("(t p) d -> p t d", p=T), mout[:, :, :]).then_inc(m_stored, 16)

            twice(sp, NB, b_body)
            store_mix(NB - 1)

            for i, name in enumerate(("w_x1", "w_x2", "w_xo")):
                sp.dma_start(wx[i].rearrange("p e c n -> p (e c) n"),
                             a[name].rearrange("(k p) n -> p k n", p=128)).then_inc(c_ff, 16)
            sp.wait_ge(m_stored, 16 * NB)
            dst_flat = a["dst"].rearrange("(c n) -> c n", c=CH)
            with nc.allow_non_contiguous_dma(reason="replicates dst over the heads"):
                for c in range(CH):
                    sp.dma_start(sc_di[c * H:(c + 1) * H, :],
                                 dst_flat[c:c + 1, :].broadcast_to((H, CE))).then_inc(dst_in, 16)
                sp.wait_ge(walk_clear, 1)
                sp.wait_ge(walk_out, 32)
                sp.dma_start(walk[0:1, 0, 0:SP_], walk_d[0:1, :]).then_inc(walk_in, 16)
                sp.dma_start(walk[0:1, 1, LAG:LAG + SP_], walk_d[1:2, :]).then_inc(walk_in, 16)
                sp.dma_start(walk[0:1, 2, 0:SP_], walk_d[2:3, :]).then_inc(walk_in, 16)
                sp.dma_start(jb_all, jb_d.rearrange("i s -> (i s)").partition_broadcast(T)).then_inc(walk_in, 16)
                sp.wait_ge(ends_ready, 1)
                sp.dma_start(fence_d.rearrange("k p -> p k"), ends[:, 0:4]).then_inc(fence_out, 16)
                sp.wait_ge(fence_out, 16)
                sp.dma_start(fence[:, 0:4, :], fence_d.rearrange("k (c h) -> h k c", h=H)).then_inc(fence_in, 16)
                sp.wait_ge(carry_ready, 1)
                sp.dma_start(fence_d[0:2, :].rearrange("k (c h) -> h k c", h=H), fence[:, 8:10, :]).then_inc(fence_out, 16)
                sp.wait_ge(fence_out, 32)
                sp.dma_start(ends[:, 4:6], fence_d[0:2, :].rearrange("k p -> p k")).then_inc(fence_in, 16)

            sp.wait_ge(walk_in, 64)
            sp.wait_ge(back_out, NT)
            regs = [sp.alloc_register(f"sp_tile{s}") for s in range(SU)]

            def d_body(it):
                sp.load(regs, walk[0:1, 0, bass.ds(it * SU, SU)])
                for s in range(SU):
                    i = sp.snap(regs[s], min_val=0, max_val=ET - 1)
                    r = s % RD
                    if not (isinstance(it, int) and s < RD):
                        sp.wait_ge(ev_done, it * SU + s - RD + 1)
                    sp.dma_start(att[:, r, :], a["attr_t"][:, bass.ds(i * T, T)]).then_inc(att_in[r], 16)

            d_body(0)
            with sp.Fori(1, SI) as it:
                d_body(it)

            sp.wait_ge(acc_done, SP_)

            def load_res(b, u):
                if not (isinstance(b, int) and b < 2):
                    sp.wait_ge(f_xn, b - 1)
                sp.dma_start(fres[:, u], res_d[bass.ds(b * BN, BN), :].rearrange("(t p) d -> p t d", p=T)).then_inc(f_in[u], 16)

            def store_out(b, u):
                sp.wait_ge(f_outr, b + 1)
                sp.dma_start(out[bass.ds(b * BN, BN), :].rearrange("(t p) d -> p t d", p=T), fyb[:, u]).then_inc(f_stored[u], 16)

            load_res(0, 0)
            load_res(1, 1)

            def e_body(b, u):
                store_out(b, u)
                load_res(b + 2, u)

            e_body(0, 0)
            e_body(1, 1)
            with sp.Fori(1, (NB - 2) // 2) as it:
                e_body(it * 2, 0)
                e_body(it * 2 + 1, 1)
            e_body(NB - 3, 0)
            store_out(NB - 2, 1)
            store_out(NB - 1, 0)
            sp.wait_ge(f_stored[0], 16 * ((NB + 1) // 2))
            sp.wait_ge(f_stored[1], 16 * (NB // 2))

        @block.gpsimd
        def _(pool):
            pool.dma_start(wz[:, :], a["dst_last"].broadcast_to((SI, ET))).then_inc(last_in, 16)
            nc.gpsimd.iota(wi[:, :], [[T, ET]], base=0, channel_multiplier=0).then_inc(walk_steps, 1)
            nc.gpsimd.iota(walk_k[:, 0:SU], [[T, SU]], base=0, channel_multiplier=T * SU).then_inc(walk_steps, 1)
            nc.gpsimd.iota(walk_k[:, SU:2 * SU], [[1, SU]], base=0, channel_multiplier=SU).then_inc(walk_steps, 1)
            pool.dma_start(src_t[:, :], a["src_t"]).then_inc(c_walk, 16)
            pool.dma_start(dst_t[:, :], a["dst_t"]).then_inc(c_walk, 16)
            pool.wait_ge(c_walk, 32)
            for u in range(2):
                pool.wait_ge(a_stored[u], 16 * 6 * (NT // 2))
            order = Order(pool, pool_o)

            def b_body(b):
                for half in range(2):
                    for r in range(RB):
                        wait(pool, gathered[r], 16 * 2 * G * (b * 2 + half - 1))
                    lo = b * (G * GPI) + half * 16
                    order(nc.gpsimd.tensor_copy(idx[:, half, 0, :], src_t[:, bass.ds(lo, 16)]))
                    order(nc.gpsimd.tensor_copy(idx[:, half, 1, :], dst_t[:, bass.ds(lo, 16)]))
                    for g4 in range(RB):
                        gg = b * GPI + half * RB + g4
                        if not (isinstance(b, int) and b == 0 and half == 0):
                            pool.wait_ge(score_done, gg - RB + 1)
                        pool.sem_inc(gather_go, 1)
                        for tile in range(G):
                            w = g4 * G + tile
                            nc.gpsimd.indirect_dma_start(
                                kg[:, g4, tile, :], None, k_tab, bass.IndirectOffsetOnAxis(idx[:, half, 0, w:w + 1], 0)
                            ).then_inc(gathered[g4], 16)
                            nc.gpsimd.indirect_dma_start(
                                qg[:, g4, tile, :], None, q_tab, bass.IndirectOffsetOnAxis(idx[:, half, 1, w:w + 1], 0)
                            ).then_inc(gathered[g4], 16)
                order.reset()

            b_body(0)
            with pool.Fori(1, NB) as b:
                b_body(b)

            pool.wait_ge(back_out, NT)

            def d_body(it):
                for s in range(SU):
                    r = s % RD
                    k = it * SU + s
                    pool.wait_ge(meta_ready, k + 1)
                    if not (isinstance(it, int) and s < RD):
                        pool.wait_ge(pv_ready, k - RD + 1)
                    pool.sem_inc(gather_go, 1)
                    nc.gpsimd.indirect_dma_start(
                        vg[:, r, :], None, v_tab, bass.IndirectOffsetOnAxis(pv[:, r, D + H + 1:D + RW].bitcast(I32), 0)
                    ).then_inc(v_in[r], 16)

            d_body(0)
            with pool.Fori(1, SI) as it:
                d_body(it)

        @block.tensor
        def _(pe):
            mm, tr = nc.tensor.matmul, nc.tensor.transpose
            pe.wait_ge(c_a, CONST_A)
            pe.wait_ge(zero_ready, 1)
            for c in range(2):
                mm(psum[:, 6 + c, 0:129], zero[:, 0:128], zero[:, :], start=True, stop=False)

            def turn(t, u):
                pe.wait_ge(xn_ready, t + 1)
                wait(pe, xnt_ready, t - 1)
                for c in range(2):
                    last = tr(psum[:, u, c * T:(c + 1) * T], xn[:, u, c * 128:(c + 1) * 128], ident[0:T, 0:T])
                last.then_inc(xn_turned, 1)

            def state(t, u):
                pe.wait_ge(kphi_ready, t + 1)
                for c in range(2):
                    last = mm(psum[:, 6 + c, 0:129], kphi[:, u, c * 128:(c + 1) * 128], vone[:, u, c, :],
                              start=False, stop=False)
                last.then_inc(state_done, 1)

            def a_body(t, u, first=False, last_tile=False):
                pe.wait_ge(xnt_ready, t + 1)
                wait(pe, gnn_out, t)
                for half in range(2):
                    for c in range(2):
                        last = mm(psum[0:T, 2 + half, :], xnt[:, u, c, :], wcat[:, c, half * 512:(half + 1) * 512],
                                  start=(c == 0), stop=(c == 1))
                last.then_inc(gnn_done, 1)
                wait(pe, kphi_ready, t - 1)
                for c in range(2):
                    last = mm(psum[0:T, 4 + u, :], xnt[:, u, c, :], wmkv[:, c, :], start=(c == 0), stop=(c == 1))
                last.then_inc(mkv_done, 1)
                if not last_tile:
                    turn(t + 1, 1 - u)
                if not first:
                    state(t - 1, 1 - u)

            turn(0, 0)
            a_body(0, 0, first=True)
            a_body(1, 1)
            with pe.Fori(1, NT // 2 - 1) as it:
                a_body(it * 2, 0)
                a_body(it * 2 + 1, 1)
            a_body(NT - 2, 0)
            a_body(NT - 1, 1, last_tile=True)
            state(NT - 1, 1)
            for c in range(2):
                last = mm(psum[:, 6 + c, 0:129], zero[:, 0:128], zero[:, :], start=False, stop=True)
            last.then_inc(state_done, 1)

            pe.wait_ge(c_b, CONST_B)
            pe.wait_ge(state_ready, 1)

            def eproj(gg, g):
                pe.wait_ge(attr_in[g % RB], (gg // RB + 1) * 16 if isinstance(gg, int) else (gg - g % RB) * (16 // RB) + 16)
                wait(pe, ke_done, gg - 1)
                for tile in range(G):
                    bk = 2 * (g % 2) + tile // 2
                    last = mm(psum[0:T, bk, (tile % 2) * D:(tile % 2 + 1) * D],
                              atg[:, g % RB, tile * T:(tile + 1) * T], we[:, :], start=True, stop=True)
                last.then_inc(e_done, 1)

            def mix(b, u, g):
                if g == 0:
                    pe.wait_ge(m_in[u], (b // 2 + 1) * 48 if isinstance(b, int) else (b - u) * 24 + 48)
                    wait(pe, m_outr, b)
                    for o in range(2):
                        for c in range(2):
                            last = mm(psum[:, 4, o * BN:(o + 1) * BN], wmq[:, c, o * 128:(o + 1) * 128], mxt[:, u, c, :],
                                      start=(c == 0), stop=(c == 1))
                    last.then_inc(m_q, 1)
                elif g == 1:
                    pe.wait_ge(m_phi, b + 1)
                    for w, m in ((0, kvbd), (1, ksbd)):
                        for c in range(2):
                            last = mm(psum[:, 5 + w, c * BN:(c + 1) * BN], m[:, c, :], mqp[:, c, :], start=True, stop=True)
                    last.then_inc(m_nd, 1)
                elif g == 2:
                    pe.wait_ge(m_at, b + 1)
                    for t in range(2):
                        for c in range(2):
                            last = mm(psum[0:T, 7, t * D:(t + 1) * D], mat[:, c, t * T:(t + 1) * T], wmo[:, c, :],
                                      start=(c == 0), stop=(c == 1))
                    last.then_inc(m_o, 1)
                elif g == 3:
                    pe.wait_ge(m_x1, b + 1)
                    for t in range(2):
                        for c in range(2):
                            last = tr(psum[:, 4, c * BN + t * T:c * BN + (t + 1) * T], mx1[:, t, c * 128:(c + 1) * 128], ident[0:T, 0:T])
                    last.then_inc(m_t, 1)
                elif g == 4 or g == 5:
                    pe.wait_ge(m_tc, b + 1)
                    for pair in range(2 * (g - 4), 2 * (g - 4) + 2):
                        bk = 5 + pair % 2
                        if pair >= 2:
                            pe.wait_ge(m_hr, b * 4 + pair - 1)
                        for o in range(2):
                            n = 2 * pair + o
                            for c in range(2):
                                last = mm(psum[:, bk, o * BN:(o + 1) * BN], wm1[:, c, n * 128:(n + 1) * 128], mx1t[:, c, :],
                                          start=(c == 0), stop=(c == 1))
                        last.then_inc(m_h, 1)
                elif g == 6:
                    pe.wait_ge(m_hr, b * 4 + 4)
                    for t in range(2):
                        for n in range(8):
                            last = mm(psum[0:T, 7, t * D:(t + 1) * D], mh[:, n, t * T:(t + 1) * T], wm2[:, n, :],
                                      start=(n == 0), stop=(n == 7))
                    last.then_inc(m_y, 1)

            def b_body(b, u):
                for g in range(GPI):
                    eproj(b * GPI + g, g)
                    mix(b, u, g)

            twice(pe, NB, b_body)

            pe.wait_ge(score_done, ET // G)
            for bt in range(CT):
                wait(pe, turned_out, bt - 3)
                tr(psum[:, bt % 4, 0:T], scores[:, bt * 128:(bt + 1) * 128], ident[0:T, 0:T]).then_inc(turned, 1)
            pe.wait_ge(exped, 1)
            for bt in range(CT):
                wait(pe, back_out, bt - 3)
                if bt < 4:
                    pe.wait_ge(turned_out, CT)
                tr(psum[0:T, bt % 4, 0:128], sc_a[:, bt * T:(bt + 1) * T], ident[:, :]).then_inc(back, 1)

            pe.wait_ge(back_out, NT)

            def ev(it, s):
                k, r = it * SU + s, s % RD
                pe.wait_ge(att_in[r], (it * 2 + s // RD + 1) * 16)
                wait(pe, ve_done, k - RD + 1)
                mm(psum[0:T, r, 0:D], att[:, r, :], we[:, :], start=True, stop=True).then_inc(ev_done, 1)

            def sums(it, s):
                k, r = it * SU + s, s % RD
                pe.wait_ge(pv_ready, k + 1)
                wait(pe, acc_done, k - RD + 1)
                mm(psum[0:T, 4 + r, 0:PV], hot[:, r, :], pv[:, r, 0:PV], start=True, stop=True).then_inc(sum_done, 1)

            def d_body(it):
                for s in range(SU):
                    ev(it, s)
                    if s >= 2:
                        sums(it, s - 2)
                    elif not (isinstance(it, int) and it == 0):
                        sums(it - 1, s + SU - 2)

            d_body(0)
            with pe.Fori(1, SI) as it:
                d_body(it)
            sums(SI - 1, SU - 2)
            sums(SI - 1, SU - 1)

            pe.wait_ge(c_ff, 48)
            pe.wait_ge(acc_done, SP_)

            def prelude(b, u):
                pe.wait_ge(f_xn, b + 1)
                wait(pe, f_tc, b)
                for t in range(2):
                    for c in range(2):
                        last = tr(psum[:, 6, c * BN + t * T:c * BN + (t + 1) * T], fxn[:, t, c * 128:(c + 1) * 128], ident[0:T, 0:T])
                last.then_inc(f_t, 1)

            def layer1(b, u, e):
                n = b * NX + e
                wait(pe, f_r1, n - 1)
                for o in range(2):
                    for c in range(2):
                        last = mm(psum[:, e % 2, o * BN:(o + 1) * BN], wx[0][:, e, c, o * 128:(o + 1) * 128], fxt[:, u, c, :],
                                  start=(c == 0), stop=(c == 1))
                last.then_inc(f_h1, 1)

            def layer2(b, u, e):
                n = b * NX + e
                pe.wait_ge(f_r1, n + 1)
                wait(pe, f_r2, n - 1)
                for o in range(2):
                    for c in range(2):
                        last = mm(psum[:, 2 + e % 2, o * BN:(o + 1) * BN], wx[1][:, e, c, o * 128:(o + 1) * 128], fh1[:, e % 3, c, :],
                                  start=(c == 0), stop=(c == 1))
                last.then_inc(f_h2, 1)

            def layer3(b, u, e):
                n = b * NX + e
                pe.wait_ge(f_r2, n + 1)
                wait(pe, f_ya, n - 1)
                for t in range(2):
                    for c in range(2):
                        last = mm(psum[0:T, 4 + e % 2, t * D:(t + 1) * D], fh2[:, e % 3, c, t * T:(t + 1) * T], wx[2][:, e, c, :],
                                  start=(c == 0), stop=(c == 1))
                last.then_inc(f_y, 1)

            def router(b, u):
                pe.wait_ge(f_tc, b + 1)
                wait(pe, f_bo, b)
                for t in range(2):
                    for c in range(2):
                        last = mm(psum[0:T, 7, t * NX:(t + 1) * NX], fxt[:, u, c, t * T:(t + 1) * T], wr[:, c, :],
                                  start=(c == 0), stop=(c == 1))
                last.then_inc(f_lg, 1)

            def weights_t(b, u):
                pe.wait_ge(f_w, b + 1)
                for t in range(2):
                    last = tr(psum[0:NX, 7, 256 + t * T:256 + (t + 1) * T], fw[:, u, t, :], ident[0:T, 0:T])
                last.then_inc(f_wt, 1)

            def bias_out(b, u):
                pe.wait_ge(f_wtc, b + 1)
                for t in range(2):
                    last = mm(psum[0:T, 7, t * D:(t + 1) * D], fwt[:, u, t * T:(t + 1) * T], bo_e[:, :], start=True, stop=True)
                last.then_inc(f_bo_done, 1)

            def e_body(b, u, last_block=False):
                router(b, u)
                for e in range(NX + 2):
                    if e < NX:
                        layer1(b, u, e)
                    if 1 <= e <= NX:
                        layer2(b, u, e - 1)
                    if e >= 2:
                        layer3(b, u, e - 2)
                    if e == 1:
                        weights_t(b, u)
                    if e == 3:
                        bias_out(b, u)
                    if e == 6 and not last_block:
                        prelude(b + 1, 1 - u)

            prelude(0, 0)
            e_body(0, 0)
            e_body(1, 1)
            with pe.Fori(1, NB // 2) as it:
                e_body(it * 2, 0)
                e_body(it * 2 + 1, 1)
            e_body(NB - 1, 0, last_block=True)

        @block.scalar
        def _(act):
            copy, fn = nc.scalar.copy, nc.scalar.activation
            order = Order(act, act_o)

            def a_body(t, u):
                act.wait_ge(xn_turned, t + 1)
                wait(act, mkv_done, t - 1)
                if not (isinstance(t, int) and t < 2):
                    act.wait_ge(a_stored[u], (t - u) * 48)
                copy(xnt[:, u].rearrange("p c n -> p (c n)"), psum[:, u, 0:2 * T]).then_inc(xnt_ready, 1)
                act.wait_ge(kmin_ready, t + 1)
                wait(act, kphi_ready, t - 1)
                fn(kexp[:, u, :], kmin[:, u, :], ACT.Exp).then_inc(kexp_ready, 1)

            twice(act, NT, a_body)

            act.wait_ge(state_ready, 1)
            act.wait_ge(c_a, CONST_A)

            def b_body(b, u):
                act.wait_ge(m_min, b + 1)
                fn(mqe[:, :, :], mqn[:, :, :], ACT.Exp).then_inc(m_exp, 1)
                act.wait_ge(m_t, b + 1)
                copy(mx1t[:, :, :].rearrange("p c n -> p (c n)"), psum[:, 4, 0:2 * BN]).then_inc(m_tc, 1)
                for pair in range(4):
                    act.wait_ge(m_h, b * 4 + pair + 1)
                    for o in range(2):
                        n = 2 * pair + o
                        last = fn(mh[:, n, :], psum[:, 5 + pair % 2, o * BN:(o + 1) * BN], ACT.Relu,
                                  bias=cols[:, C_B1 + n:C_B1 + n + 1])
                    last.then_inc(m_hr, 1)

            twice(act, NB, b_body)

            act.wait_ge(score_done, ET // G)
            for bt in range(CT):
                act.wait_ge(turned, bt + 1)
                copy(sc_a[:, bt * T:(bt + 1) * T], psum[:, bt % 4, 0:T]).then_inc(turned_out, 1)
            act.wait_ge(shifted, 1)
            fn(sc_a, sc_a, ACT.Exp, scale=SCALE).then_inc(exped, 1)
            sview = rec[:, :, :].rearrange("p (b c) m -> p b c m", c=CH)
            for bt in range(CT):
                act.wait_ge(back, bt + 1)
                copy(sview[:, bt, :, 0:H], psum[0:T, bt % 4, 0:128].rearrange("p (c h) -> p c h", c=CH)).then_inc(back_out, 1)

            act.wait_ge(walk_in, 64)
            act.wait_ge(back_out, CT)
            act.wait_ge(rec_ready, 2)
            regs = [act.alloc_register(f"act_tile{s}") for s in range(SU)]

            def d_body(it):
                act.load(regs, walk[0:1, 2, bass.ds(it * SU, SU)])
                for s in range(SU):
                    k, r = it * SU + s, s % RD
                    i = act.snap(regs[s], min_val=0, max_val=ET - 1)
                    if not (isinstance(it, int) and s < RD):
                        act.wait_ge(sum_done, k - RD + 1)
                    copy(pv[:, r, D:D + RW], rec[:, bass.ds(i, 1), :].rearrange("p o m -> p (o m)")).then_inc(meta_ready, 1)

            d_body(0)
            with act.Fori(1, SI) as it:
                d_body(it)

            act.wait_ge(acc_done, SP_)

            def turned_x(b, u):
                act.wait_ge(f_t, b + 1)
                if not (isinstance(b, int) and b < 2):
                    act.wait_ge(f_h1, (b - 1) * NX)
                copy(fxt[:, u].rearrange("p c n -> p (c n)"), psum[:, 6, 0:2 * BN]).then_inc(f_tc, 1)

            def relu(done, used, ready, bk, to, layer, b, e):
                n = b * NX + e
                act.wait_ge(done, n + 1)
                wait(act, used, n - 1)
                for o in range(2):
                    col = e * 2 + o
                    last = fn(to[:, e % 3, o, :], psum[:, bk + e % 2, o * BN:(o + 1) * BN], ACT.Relu,
                              bias=bns[:, layer, 1, col:col + 1], scale=bns[:, layer, 0, col:col + 1])
                last.then_inc(ready, 1)

            def e_body(b, u, last_block=False):
                for e in range(NX + 1):
                    if e < NX:
                        relu(f_h1, f_h2, f_r1, 0, fh1, 0, b, e)
                    if e == 0:
                        act.wait_ge(f_sm, b + 1)
                        fn(fsm[:, u, 0:16], fsm[:, u, 0:16], ACT.Exp).then_inc(f_ex, 1)
                    if e >= 1:
                        relu(f_h2, f_y, f_r2, 2, fh2, 1, b, e - 1)
                    if e == 1:
                        act.wait_ge(f_wt, b + 1)
                        copy(fwt[:, u, :], psum[0:NX, 7, 256:256 + BN]).then_inc(f_wtc, 1)
                    if e == 6 and not last_block:
                        turned_x(b + 1, 1 - u)

            act.wait_ge(bn_ready, 2)
            turned_x(0, 0)
            e_body(0, 0)
            e_body(1, 1)
            with act.Fori(1, NB // 2) as it:
                e_body(it * 2, 0)
                e_body(it * 2 + 1, 1)
            e_body(NB - 1, 0, last_block=True)

        @block.vector
        def _(dve):
            tt, ts, stt = nc.vector.tensor_tensor, nc.vector.tensor_scalar, nc.vector.scalar_tensor_tensor
            order = Order(dve, dve_o)

            def signal(ins, sem, value):
                ins.then_inc(sem, 1)
                dve.wait_ge(sem, value)

            def rsqrt(x, eps, y, t):
                order(ts(x, x, eps, None, ALU.add))
                order(ts(y.bitcast(I32), x.bitcast(I32), 1, None, ALU.logical_shift_right))
                order(ts(y.bitcast(I32), y.bitcast(I32), -1.0, float(0x5F3759DF), ALU.mult, ALU.add))
                for _ in range(3):
                    order(stt(t, y, 0.5, y, ALU.mult, ALU.mult))
                    order(tt(t, t, x, ALU.mult))
                    order(stt(y, t, 1.5, y, ALU.subtract, ALU.mult, reverse0=True))

            def norm2(x, to):
                for t in range(2):
                    i = nc.vector.bn_stats(stats[:, t, 0:6], x[:, t, :])
                order(i)
                for t in range(2):
                    i = nc.vector.bn_aggr(stats[:, t, 6:8], stats[:, t, 0:6])
                order(i)
                rsqrt(stats[:, :, 7:8], LN_EPS, stats[:, :, 8:9], stats[:, :, 9:10])
                for t in range(2):
                    i = ts(to[:, t, :], x[:, t, :], stats[:, t, 6:7], stats[:, t, 8:9], ALU.subtract, ALU.mult)
                return i

            def row2(at):
                return rows[:, at:at + D].unsqueeze(1).broadcast_to((T, 2, D))

            nc.vector.memset(zero, 0.0)
            nc.vector.memset(vone.rearrange("p u c n -> p (u c n)"), 1.0).then_inc(zero_ready, 1)
            dve.wait_ge(c_a, CONST_A)
            for layer in range(2):
                col = [cols[:, C_FF + (layer * 5 + i) * 16:C_FF + (layer * 5 + i + 1) * 16] for i in range(5)]
                b_, g_, be_, m_, v_ = col
                scale, bias = bns[:, layer, 0, :], bns[:, layer, 1, :]
                rsqrt(v_, BN_EPS, scale, bias)
                order(tt(scale, scale, g_, ALU.mult))
                order(tt(bias, b_, m_, ALU.subtract))
                order(tt(bias, bias, scale, ALU.mult))
                tt(bias, bias, be_, ALU.add).then_inc(bn_ready, 1)

            dve.wait_ge(last_in, 16)
            dve.wait_ge(walk_steps, 3)
            order(tt(wf, wz, wi, ALU.add))
            order(nc.vector.tensor_copy(walk_s[:, 0, :], walk_k[:, 0:SU]))
            for s in range(SU):
                order(ts(wl, wf, walk_s[:, 0, s:s + 1], 0.0, ALU.is_lt, ALU.add, accum_out=walk_s[:, 1, s:s + 1]))
            order(ts(walk_s[:, 2, :], walk_s[:, 1, :], float(ET - 1), float(T), ALU.min, ALU.mult))
            order(tt(walk_s[:, 3, :], walk_s[:, 0, :], walk_s[:, 2, :], ALU.subtract))
            order(ts(walk_s[:, 1, :], walk_s[:, 1, :], float(ET - 1), None, ALU.min))
            order(nc.vector.tensor_copy(walk_i[:, 0, :], walk_s[:, 1, :]))
            order(tt(walk_s[:, 4, :], walk_k[:, SU:2 * SU], walk_s[:, 1, :], ALU.subtract))
            order(ts(walk_s[:, 4, :], walk_s[:, 4, :], float(NT - 1), None, ALU.min))
            order(nc.vector.tensor_copy(walk_i[:, 1, :], walk_s[:, 4, :]))
            order(nc.vector.memset(walk_s[:, 5, :], 0.0))
            for c in range(1, CH):
                order(stt(walk_s[:, 5, :], walk_s[:, 1, :], float(CT * c), walk_s[:, 5, :], ALU.is_ge, ALU.add))
            order(ts(walk_s[:, 4, :], walk_s[:, 1, :], float(CH), None, ALU.mult))
            order(stt(walk_s[:, 4, :], walk_s[:, 5, :], float(1 - CT * CH), walk_s[:, 4, :], ALU.mult, ALU.add))
            nc.vector.tensor_copy(walk_i[:, 2, :], walk_s[:, 4, :]).then_inc(walk_ready, 1)
            order.reset()

            def ln(t, u):
                wait(dve, xn_turned, t - 1)
                if not (isinstance(t, int) and t < 2):
                    dve.wait_ge(a_stored[u], (t - u) * 48)
                one, st = bass.ds(t, 1), xstat[:, bass.ds(t, 1), :].rearrange("p o k -> p (o k)")
                ts(xn[:, u, :], x_all[:, one, :].rearrange("p o d -> p (o d)"), st[:, 0:1], st[:, 2:3],
                   ALU.subtract, ALU.mult).then_inc(xn_ready, 1)

            def phi_k(t, u):
                dve.wait_ge(kexp_ready, t + 1)
                wait(dve, state_done, t - 1)
                stt(kphi[:, u, :], kt[:, u, :], 0.0, kexp[:, u, :], ALU.max, ALU.add).then_inc(kphi_ready, 1)

            def tables(t, u):
                dve.wait_ge(gnn_done, t + 1)
                both = psum[0:T, 2:4, :].rearrange("p b n -> p (b n)")
                tt(qkv[:, u, :], both[:, 0:3 * D], rows[:, R_GNN:R_GNN + 3 * D], ALU.add)
                order(tt(skp[:, u, :], both[:, 3 * D:4 * D], rows[:, R_GNN + 3 * D:R_GNN + 4 * D], ALU.add))
                tt(skp[:, u, :], skp[:, u, :], x_all[:, bass.ds(t, 1), :].rearrange("p o d -> p (o d)"), ALU.add).then_inc(gnn_out, 1)
                dve.wait_ge(mkv_done, t + 1)
                wait(dve, state_done, t - 1)
                order(tt(kt[:, u, :], psum[0:T, 4 + u, 0:D], rows[:, R_MKV:R_MKV + D], ALU.add))
                ts(kmin[:, u, :], kt[:, u, :], 0.0, None, ALU.min).then_inc(kmin_ready, 1)
                order(tt(vone[:, u, :, 0:128], psum[0:T, 4 + u, D:2 * D].rearrange("p (c n) -> p c n", c=2),
                         rows[:, R_MKV + D:R_MKV + 2 * D].rearrange("p (c n) -> p c n", c=2), ALU.add))

            def a_body(t, u, last_tile=False):
                if not last_tile:
                    ln(t + 1, 1 - u)
                if not (isinstance(t, int) and t == 0):
                    phi_k(t - 1, 1 - u)
                tables(t, u)

            for i in range(5):
                dve.wait_ge(x_in[i], 16)
                for t in range(10):
                    last = nc.vector.bn_stats(xsix[:, t, :], x_all[:, i * 10 + t, :])
                order(last)
                for t in range(10):
                    last = nc.vector.bn_aggr(xstat[:, i * 10 + t, 0:2], xsix[:, t, :])
                order(last)
            rsqrt(xstat[:, :, 1:2], LN_EPS, xstat[:, :, 2:3], xstat[:, :, 3:4])
            ln(0, 0)
            a_body(0, 0)
            a_body(1, 1)
            order.reset()
            with dve.Fori(1, NT // 2 - 1) as it:
                a_body(it * 2, 0)
                a_body(it * 2 + 1, 1)
                order.reset()
            a_body(NT - 2, 0)
            a_body(NT - 1, 1, last_tile=True)
            phi_k(NT - 1, 1)
            dve.wait_ge(state_done, NT + 1)
            for c in range(2):
                order(nc.vector.tensor_copy(ksum[:, c:c + 1], psum[:, 6 + c, 128:129]))
                tt(kvbd[:, c, :], psum[:, 6 + c, 0:128], blockm[:, :], ALU.mult)
                last = ts(ksbd[:, c, :], blockm[:, :], ksum[:, c:c + 1], None, ALU.mult)
            last.then_inc(state_ready, 1)
            order.reset()

            def edges(b, g):
                gg, r = b * GPI + g, g % RB
                dve.wait_ge(gathered[r], (gg // RB + 1) * 128 if isinstance(gg, int) else (gg - r) * 32 + 128)
                dve.wait_ge(e_done, gg + 1)
                flat = kg[:, r].rearrange("p g d -> p (g d)")
                e = psum[0:T, 2 * (g % 2):2 * (g % 2) + 2, :].rearrange("p b n -> p (b n)")
                signal(tt(flat, flat, e, ALU.add), ke_done, gg + 1)
                order(tt(flat, flat, qg[:, r].rearrange("p g d -> p (g d)"), ALU.mult))
                nc.vector.tensor_reduce(scores[:, bass.ds(gg * (G * H), G * H)].rearrange("p (g h) -> p g h", g=G), kg[:, r].rearrange("p g (h c) -> p g h c", h=H),
                                        AX, ALU.add).then_inc(score_done, 1)

            def mix(b, u, g):
                if g == 0:
                    dve.wait_ge(m_q, b + 1)
                    for op, to in ((ALU.min, mqn), (ALU.max, mq)):
                        for c in range(2):
                            i = ts(to[:, c, :], psum[:, 4, c * BN:(c + 1) * BN], cols[:, C_BQ + c:C_BQ + c + 1], 0.0, ALU.add, op)
                        if op == ALU.min:
                            i.then_inc(m_min, 1)
                    order(i)
                    dve.wait_ge(m_exp, b + 1)
                    tt(mqp, mq, mqe, ALU.add).then_inc(m_phi, 1)
                elif g == 1:
                    dve.wait_ge(m_nd, b + 1)
                    z = mz.rearrange("p c n -> p (c n)")
                    order(ts(z, psum[:, 6, 0:2 * BN], Z_EPS, None, ALU.add))
                    order(nc.vector.reciprocal(z, z))
                    tt(mat.rearrange("p c n -> p (c n)"), psum[:, 5, 0:2 * BN], z, ALU.mult).then_inc(m_at, 1)
                elif g == 2:
                    dve.wait_ge(m_o, b + 1)
                    dve.wait_ge(m_in[u], (b // 2 + 1) * 48 if isinstance(b, int) else (b - u) * 24 + 48)
                    order(tt(my, psum[0:T, 7, :].rearrange("p (t d) -> p t d", t=2), row2(R_BO), ALU.add))
                    order(tt(my, my, mxn[:, u], ALU.add))
                    order(norm2(my, mx1))
                    order(tt(mx1, mx1, row2(R_G1), ALU.mult))
                    signal(tt(mx1, mx1, row2(R_E1), ALU.add), m_x1, b + 1)
                elif g == 6:
                    dve.wait_ge(m_y, b + 1)
                    order(tt(my2, psum[0:T, 7, :].rearrange("p (t d) -> p t d", t=2), row2(R_B2), ALU.add))
                    order(tt(my2, my2, mx1, ALU.add))
                    order(norm2(my2, my))
                    order(tt(my, my, row2(R_G2), ALU.mult))
                    order(tt(my, my, row2(R_E2), ALU.add))
                    wait(dve, m_stored, b * 16)
                    tt(mout, my, mres[:, u], ALU.add).then_inc(m_outr, 1)

            def b_body(b, u):
                for g in range(GPI):
                    edges(b, g)
                    mix(b, u, g)

            twice(dve, NB, b_body, (order,))

            dve.wait_ge(dst_in, 16 * CH)
            dve.wait_ge(turned_out, CT)
            dve.wait_ge(c_walk, 32)
            dve.wait_ge(turned, CT)
            nc.vector.tensor_copy(rec[:, :, H:H + 1].rearrange("p e o -> p (e o)"), dst_t[:, :]).then_inc(rec_ready, 1)
            nc.vector.tensor_copy(rec[:, :, H + 1:RW].bitcast(I32).rearrange("p e o -> p (e o)"), src_t[:, :]).then_inc(rec_ready, 1)
            nc.vector.memset(walk.rearrange("p w n -> p (w n)"), 0).then_inc(walk_clear, 1)
            nc.vector.memset(sc_m[:, 0:1], 0.0)
            nc.vector.memset(sc_m[:, CE:CE + 1], 0.0)
            nc.vector.tensor_copy(ends[:, 2:3], sc_di[:, 0:1])
            nc.vector.tensor_copy(ends[:, 3:4], sc_di[:, CE - 1:CE])
            order(tt(sc_m[:, 1:CE], sc_di[:, 1:CE], sc_di[:, 0:CE - 1], ALU.is_equal))
            order(ts(sc_m[:, 1:CE], sc_m[:, 1:CE], BIG, -BIG, ALU.mult, ALU.add))
            scan = nc.vector.tensor_tensor_scan
            m_fwd, m_bwd = sc_m[:, 0:CE], sc_m[:, 1:CE + 1][:, ::-1]
            order(scan(sc_f, m_fwd, sc_a, -BIG, ALU.add, ALU.max))
            order(nc.vector.tensor_copy(ends[:, 0:1], sc_f[:, CE - 1:CE]))
            order(scan(sc_f[:, ::-1], m_bwd, sc_a[:, ::-1], -BIG, ALU.add, ALU.max))
            nc.vector.tensor_copy(ends[:, 1:2], sc_f[:, 0:1]).then_inc(ends_ready, 1)
            dve.wait_ge(fence_in, 16)
            nc.vector.memset(fence[:, 4, 0:1], 0.0)
            tt(fence[:, 4, 1:CH], fence[:, 2, 1:CH], fence[:, 3, 0:CH - 1], ALU.is_equal)
            order(tt(fence[:, 5, :], fence[:, 2, :], fence[:, 3, :], ALU.is_equal))
            order(ts(fence[:, 4:6, :], fence[:, 4:6, :], BIG, -BIG, ALU.mult, ALU.add))
            nc.vector.memset(fence[:, 8:10, :], -BIG)
            order(tt(fence[:, 6, :], fence[:, 4, :], fence[:, 5, :], ALU.add))
            order(scan(fence[:, 7, :], fence[:, 6, :], fence[:, 0, :], -BIG, ALU.add, ALU.max))
            order(tt(fence[:, 8, 1:CH], fence[:, 7, 0:CH - 1], fence[:, 4, 1:CH], ALU.add))
            order(nc.vector.memset(fence[:, 6, CH - 1:CH], -BIG))
            order(tt(fence[:, 6, 0:CH - 1], fence[:, 4, 1:CH], fence[:, 5, 0:CH - 1], ALU.add))
            order(scan(fence[:, 7, ::-1], fence[:, 6, ::-1], fence[:, 1, ::-1], -BIG, ALU.add, ALU.max))
            tt(fence[:, 9, 0:CH - 1], fence[:, 7, 1:CH], fence[:, 4, 1:CH], ALU.add).then_inc(carry_ready, 1)
            dve.wait_ge(fence_in, 32)
            order(scan(sc_f, m_fwd, sc_a, ends[:, 4:5], ALU.add, ALU.max))
            order(scan(sc_f[:, ::-1], m_bwd, sc_f[:, ::-1], ends[:, 5:6], ALU.add, ALU.max))
            tt(sc_a, sc_a, sc_f, ALU.subtract).then_inc(shifted, 1)

            dve.wait_ge(back, CT)
            order(nc.vector.memset(region_x[0:T, :], 0.0))
            dve.wait_ge(walk_in, 64)
            order.reset()
            regs = [dve.alloc_register(f"dve_tile{s}") for s in range(SU)]

            def add(it, s, reg):
                k, r = it * SU + s, s % RD
                j = dve.snap(reg, min_val=0, max_val=NT - 1)
                dve.wait_ge(sum_done, k + 1)
                wait(dve, acc_done, k)
                to = acc[:, bass.ds(j, 1), :].rearrange("p o f -> p (o f)")
                tt(to, to, psum[0:T, 4 + r, 0:PV], ALU.add).then_inc(acc_done, 1)

            def d_body(it):
                dve.load(regs, walk[0:1, 1, bass.ds(it * SU, SU)])
                for s in range(SU):
                    k, r = it * SU + s, s % RD
                    dve.wait_ge(v_in[r], (it * 2 + s // RD + 1) * 16)
                    dve.wait_ge(ev_done, k + 1)
                    tt(vg[:, r, :], vg[:, r, :], psum[0:T, r, 0:D], ALU.add).then_inc(ve_done, 1)
                    dve.wait_ge(meta_ready, k + 1)
                    if not (isinstance(it, int) and s < RD):
                        dve.wait_ge(sum_done, k - RD + 1)
                    ts(hot[:, r, :], iota[:, :], jb_all[:, bass.ds(k, 1)], pv[:, r, D + H:D + H + 1], ALU.add, ALU.is_equal)
                    dve.wait_ge(ve_done, k + 1)
                    tt(pv[:, r, 0:D].rearrange("p (h c) -> p h c", h=H), vg[:, r, :].rearrange("p (h c) -> p h c", h=H),
                       pv[:, r, D:PV].unsqueeze(2).broadcast_to((T, H, C)), ALU.mult).then_inc(pv_ready, 1)
                    if s >= LAG:
                        add(it, s - LAG, regs[s])
                    elif not (isinstance(it, int) and it == 0):
                        add(it - 1, s + SU - LAG, regs[s])

            d_body(0)
            with dve.Fori(1, SI) as it:
                d_body(it)
            dve.load(regs, walk[0:1, 1, SI * SU:SI * SU + SU])
            for s in range(LAG):
                add(SI - 1, SU - LAG + s, regs[s])

            dve.wait_ge(acc_done, SP_)

            def prelude(b, u):
                dve.wait_ge(f_in[u], (b // 2 + 1) * 16 if isinstance(b, int) else (b - u) * 8 + 16)
                wait(dve, f_t, b)
                part = acc[:, bass.ds(b * 2, 2), :]
                rs = fsm[:, u, 16:32].rearrange("p (t h) -> p t h", t=2)
                order(ts(rs, part[:, :, D:PV], S_EPS, None, ALU.add))
                order(nc.vector.reciprocal(rs, rs))
                for t in range(2):
                    one = acc[:, bass.ds(b * 2 + t, 1), :].rearrange("p o f -> p (o f)")
                    i = tt(fgn[:, t, :].rearrange("p (h c) -> p h c", h=H), one[:, 0:D].rearrange("p (h c) -> p h c", h=H),
                           rs[:, t, :].unsqueeze(2).broadcast_to((T, H, C)), ALU.mult)
                order(i)
                order(tt(fx2[:, u], fgn, fres[:, u], ALU.add))
                norm2(fx2[:, u], fxn).then_inc(f_xn, 1)

            def router(b, u):
                dve.wait_ge(f_lg, b + 1)
                lg = fsm[:, u, 0:16].rearrange("p (t e) -> p t e", t=2)
                mx = stats[:, :, 12:13]
                order(tt(lg, psum[0:T, 7, 0:16].rearrange("p (t e) -> p t e", t=2),
                         rows[:, R_BR:R_BR + NX].unsqueeze(1).broadcast_to((T, 2, NX)), ALU.add))
                order(nc.vector.tensor_reduce(mx, lg, AX, ALU.max))
                tt(lg, lg, mx.broadcast_to((T, 2, NX)), ALU.subtract).then_inc(f_sm, 1)
                dve.wait_ge(f_ex, b + 1)
                order(nc.vector.tensor_reduce(mx, lg, AX, ALU.add))
                order(nc.vector.reciprocal(mx, mx))
                signal(tt(fw[:, u], lg, mx.broadcast_to((T, 2, NX)), ALU.mult), f_w, b + 1)

            def bias_out(b, u):
                dve.wait_ge(f_bo_done, b + 1)
                if not (isinstance(b, int) and b < 2):
                    dve.wait_ge(f_stored[u], (b - u) * 8)
                signal(tt(fyb[:, u], psum[0:T, 7, :].rearrange("p (t d) -> p t d", t=2), fx2[:, u], ALU.add), f_bo, b + 1)

            def gate(b, u, e):
                n = b * NX + e
                dve.wait_ge(f_y, n + 1)
                for t in range(2):
                    i = stt(fyb[:, u, t, :], psum[0:T, 4 + e % 2, t * D:(t + 1) * D], fw[:, u, t, e:e + 1], fyb[:, u, t, :],
                            ALU.mult, ALU.add)
                signal(i, f_ya, n + 1)

            def e_body(b, u, last_block=False):
                router(b, u)
                bias_out(b, u)
                for e in range(NX):
                    gate(b, u, e)
                    if e == 3 and not last_block:
                        prelude(b + 1, 1 - u)
                order(nc.vector.memset(ksum[:, 0:1], 0.0))
                dve.sem_inc(f_outr, 1)

            prelude(0, 0)
            e_body(0, 0)
            e_body(1, 1)
            order.reset()
            with dve.Fori(1, NB // 2) as it:
                e_body(it * 2, 0)
                e_body(it * 2 + 1, 1)
                order.reset()
            e_body(NB - 1, 0, last_block=True)


_OUT = (N, D)


def kernel(**inputs):
    import concourse.bacc as bacc
    from concourse.bass_utils import run_bass_kernel_spmd

    g = {k: np.asarray(v) for k, v in inputs.items()}

    def gnn(n):
        return g["L0_gnn_" + n]

    def mix(n):
        return g["L0_mix_" + n]

    def ffn(n):
        return g["L0_ffn_" + n]

    def columns(v):
        return np.ascontiguousarray(v.reshape(-1, 128).T)

    row = np.concatenate([gnn("bq"), gnn("bk"), gnn("bv"), gnn("bskip"), mix("bk"), mix("bv"), mix("bo"), mix("b2"),
                          mix("ln1_g"), mix("ln1_b"), mix("ln2_g"), mix("ln2_b"), ffn("br")])
    dst = g["dst"].astype(np.int32, copy=False)
    src = g["src"].astype(np.int32, copy=False)

    def places(v):
        return v.reshape(CH, CT, T).transpose(2, 1, 0).reshape(T, ET)

    arrays = {
        "x": g["x"],
        "dst": dst,
        "src_t": places(src),
        "dst_t": places(dst),
        "dst_last": np.ascontiguousarray(dst.reshape(ET, T)[:, T - 1].reshape(1, ET)),
        "attr_t": np.ascontiguousarray(g["edge_attr_64"].T),
        "w_gnn": np.concatenate([gnn("Wq").T, gnn("Wk").T, gnn("Wv").T, gnn("Wskip").T], 1),
        "w_e": np.ascontiguousarray(gnn("We").T),
        "w_mkv": np.concatenate([mix("Wk"), mix("Wv")], 1),
        "w_mq": mix("Wq"), "w_mo": mix("Wo"), "w_m1": mix("W1"), "w_m2": mix("W2"),
        "w_x1": ffn("W1").reshape(NX * D, D), "w_x2": ffn("W2").reshape(NX * D, D), "w_xo": ffn("Wo").reshape(NX * D, D),
        "w_r": ffn("Wr"), "bo_e": ffn("bo"),
        "rows": np.ascontiguousarray(np.broadcast_to(row, (T, ROWS))),
        "cols": np.concatenate([columns(mix("bq")), columns(mix("b1"))]
                               + [columns(ffn(n + i)) for i in "12" for n in ("b", "g", "be", "m", "v")], 1),
        "ident": np.eye(128, dtype=np.float32),
        "blockm": np.kron(np.eye(128 // C, dtype=np.float32), np.ones((C, C), np.float32)),
        "iota": np.ascontiguousarray(np.broadcast_to(np.arange(T, dtype=np.float32), (T, T))),
    }
    arrays = {k: np.ascontiguousarray(v) for k, v in arrays.items()}
    from concourse import mybir as _mybir

    nc = bacc.Bacc("TRN2", target_bir_lowering=False, num_devices=1)
    aps = {n: nc.dram_tensor("in_" + n, v.shape, _mybir.dt.from_np(v.dtype), kind="ExternalInput").ap()
           for n, v in arrays.items()}
    out = nc.dram_tensor("out_0", _OUT, F32, kind="ExternalOutput").ap()
    build(nc, aps, out)
    r = run_bass_kernel_spmd(nc, [{"in_" + n: v for n, v in arrays.items()}], core_ids=[0])
    return r.results[0]["out_0"]
```

```python
from contextlib import ExitStack

import numpy as np

import concourse.bass as bass
from concourse import mybir

F32 = mybir.dt.float32
I32 = mybir.dt.int32
F32R = mybir.dt.float32r
ALU = mybir.AluOpType
ACT = mybir.ActivationFunctionType
AX = mybir.AxisListType.X

N, E_, D, ED = 6250, 100000, 256, 64
H, C = 8, 32
T = 125
NT, ET = N // T, E_ // T
BN = 2 * T
NB = N // BN
FF = 1024
NX = 8
LN_EPS, BN_EPS, Z_EPS, S_EPS = 1e-5, 1e-3, 1e-6, 1e-16
EP, E2 = ET // 2, 2 * T
SB = 18
STEPS = NB * SB
SU = 6
SI = STEPS // SU
assert STEPS >= EP + NT - 1 and SB % SU == 0
RK, R, RA = 9, 6, 3
CH = 16
CE = E_ // CH
CT = ET // CH
RW = H + 2
PV = D + H
LAGD = 3
LAGQ = 4
LAGP = 2
LAG = 2
KV = 128 + H // 2
LAGS = 4
WALK = STEPS + LAGQ + SU
BIG = 1.0e30
SCALE = float(C) ** -0.5
R_GNN, R_MKV, R_BO, R_B2, R_G1, R_E1, R_G2, R_E2, R_BR = 0, 1024, 1536, 1792, 2048, 2304, 2560, 2816, 3072
ROWS = 3080
C_BQ, C_B1, C_G1, C_E1, C_FF = 0, 2, 10, 12, 14
COLS = C_FF + 10 * 16


def wait(eng, sem, value):
    if isinstance(value, int) and value <= 0:
        return
    eng.wait_ge(sem, value)


class Order:

    def __init__(self, eng, sem):
        self.eng, self.sem, self.n = eng, sem, 0

    def __call__(self, ins):
        self.n += 1
        ins.then_inc(self.sem, 1)
        self.eng.wait_ge(self.sem, self.n)

    def reset(self):
        self.eng.sem_clear(self.sem)
        self.n = 0


def build(nc, a, out):
    ctx = ExitStack()
    with ctx:
        def sb(name, shape, dt=F32):
            return ctx.enter_context(nc.sbuf_tensor(name, shape, dt))

        def sem(name):
            return ctx.enter_context(nc.semaphore(name))

        def dram(name, shape, dt=F32):
            return nc.dram_tensor(name, shape, dt).ap()

        k_tab, v_tab = dram("k_tab", (N, D)), dram("v_tab", (N, D))
        xn_d, xnt_d = dram("xn_d", (N, D)), dram("xnt_d", (2, 128, N))
        skip_d, res_d = dram("skip_d", (N, D)), dram("res_d", (N, D))
        walk_d, jb_d = dram("walk_d", (3, STEPS), I32), dram("jb_d", (SI, SU))
        fence_d = dram("fence_d", (4, 128))

        region_x = sb("region_x", [128, NT * PV])
        early = ExitStack()
        with early:
            weights = early.enter_context(nc.sbuf_tensor("weights", [128, 12288], F32))
            region_r = early.enter_context(nc.sbuf_tensor("region_r", [128, ET * (RW + 2) + ROWS], F32))
            region_s = early.enter_context(nc.sbuf_tensor("region_s", [128, 11400], F32))
        wx_low = sb("wx_low", [128, 12288], F32R)
        wx_up = sb("wx_up", [128, 12288], F32R)
        sb("rows_tail", [128, ET * (RW + 2) + ROWS - 12288])
        parts_x = sb("parts_x", [128, 2, 2, 2, BN], F32R)
        parts_h = sb("parts_h", [128, 4, 2, 2, BN], F32R)
        sb("region_s_tail", [128, 11400 - 12 * 2 * BN])
        rec = region_r[0:T, 0:ET * RW].rearrange("p (e m) -> p e m", m=RW)
        src_t = region_r[0:T, ET * RW:ET * (RW + 1)].bitcast(I32)
        dst_t = region_r[0:T, ET * (RW + 1):ET * (RW + 2)].bitcast(I32)
        rows = region_r[0:T, ET * (RW + 2):ET * (RW + 2) + ROWS]
        cols = sb("cols", [128, COLS])
        bns = sb("bns", [128, 2, 2, 16])
        ident = sb("ident", [128, 128])
        blockm = sb("blockm", [128, 128])
        iota = sb("iota", [T, T])
        we = sb("we", [2 * ED, 2, D])
        idx = sb("idx", [T, RK, 2], I32)
        part = sb("part", [T, 3, 2 * H])
        node = sb("node", [T, 1])
        node_i = sb("node_i", [T, 1], I32)
        walk_i = sb("walk_i", [SI, 3, SU], I32)
        walk_s = sb("walk_s", [SI, 6, SU])
        kvbd = sb("kvbd", [128, 2, KV])
        wr = sb("wr", [128, 2, NX])
        wr_h, wr_l = sb("wr_h", [128, 2, NX], F32R), sb("wr_l", [128, 2, NX], F32R)
        bo_e = sb("bo_e", [NX, D])
        ends = sb("ends", [128, 8])
        fence = sb("fence", [H, 10, CH])
        stats = sb("stats", [T, 2, 16])
        ksum = sb("ksum", [128, 2])
        fsm = sb("fsm", [T, 2, 32])

        wcat = weights[:, 0:2048].rearrange("p (c n) -> p c n", c=2)
        wmkv = weights[:, 2048:3072].rearrange("p (c n) -> p c n", c=2)
        wmq = weights[:, 3072:3584].rearrange("p (c n) -> p c n", c=2)
        wmo = weights[:, 3584:4096].rearrange("p (c n) -> p c n", c=2)
        wm1 = weights[:, 4096:6144].rearrange("p (c n) -> p c n", c=2)
        wm2 = weights[:, 6144:8192].rearrange("p (c n) -> p c n", c=8)
        wx = [weights[:, 4096 * i:4096 * (i + 1)].rearrange("p (e c n) -> p e c n", e=NX, c=2) for i in range(3)]

        assert 3 * 4096 <= ET * (RW + 2) + R_BR
        wxh, wxl = ([w[:, 4096 * i:4096 * (i + 1)].rearrange("p (e c n) -> p e c n", e=NX, c=2) for i in range(3)]
                    for w in (wx_up, wx_low))

        used = [0]

        def carve(start, *shape, parts=128):
            size = int(np.prod(shape))
            if start is not None:
                used[0] = start
            at = used[0]
            used[0] += size
            assert used[0] <= 11400, used
            flat = region_s[0:parts, at:at + size]
            if len(shape) == 1:
                return flat
            names = "abcd"[:len(shape)]
            return flat.rearrange(f"p ({' '.join(names)}) -> p {' '.join(names)}",
                                  **{n: s for n, s in zip(names[:-1], shape[:-1])})

        skip_row = rows[:, R_GNN:R_GNN + D]
        x_all = region_x[0:T, 0:NT * D].rearrange("p (t d) -> p t d", t=NT)
        xstat = sb("xstat", [T, NT, 4])
        xsix = sb("xsix", [T, 10, 6])
        xn = carve(0, 2, D, parts=T)
        xnt = carve(None, 2, 2, T)
        kv = carve(None, 2, 2 * D, parts=T)
        xnb = carve(None, 2, D, parts=T)
        skp = carve(None, 2, D, parts=T)
        kt = carve(None, 2, D, parts=T)
        krelu = carve(None, 2, D, parts=T)
        kexp = carve(None, 2, D, parts=T)
        kphi = carve(None, 2, D, parts=T)
        vone = carve(None, 2, 2, 129, parts=T)
        zero = carve(None, 129)
        assert used[0] <= 8200
        mxt = carve(0, 2, 2, BN)
        mres = carve(None, 2, D, parts=T)
        mq, mqe, mqp = (carve(None, 2, BN) for _ in range(3))
        mat = carve(None, 2, BN)
        mx1 = carve(None, 2, D, parts=T)
        mx1t = carve(None, 2, BN)
        mh = carve(None, 8, BN)
        my = carve(None, 2, 2, D, parts=T)
        mout = sb("mout", [T, 2, D])
        mx2 = sb("mx2", [T, 2, D])
        rec_tail = rec[:, :, :].rearrange("p e m -> p (e m)")[:, ET * H:ET * RW]
        mxn = rec_tail[:, 0:4 * D].rearrange("p (u t d) -> p u t d", u=2, t=2)
        matn = rec_tail[:, 4 * D:6 * D].rearrange("p (t d) -> p t d", t=2)
        mden = rec_tail[:, 6 * D:6 * D + 4 * H].rearrange("p (o t h) -> p o t h", o=2, t=2)
        assert used[0] <= 8200
        wf, wl = region_s[0:SI, 8200:8200 + EP], region_s[0:SI, 8600:8600 + EP]
        wz, wi = region_s[0:SI, 9000:9000 + EP].bitcast(I32), region_s[0:SI, 9400:9400 + EP].bitcast(I32)
        walk_k = sb("walk_k", [SI, 2 * SU], I32)
        dstb = carve(8200, RA, E2, parts=T).bitcast(I32)
        jb_all = carve(None, STEPS, parts=T)
        jneg = carve(None, STEPS, parts=T)
        walk = carve(None, 3, WALK, parts=1).bitcast(I32)
        q_all = x_all
        tail = weights[:, 8192:12288]
        kg_a = tail[0:T, 0:6 * 2 * D].rearrange("p (r w d) -> p r w d", r=6, w=2)
        kg_b = rows[:, 0:3 * 2 * D].rearrange("p (r w d) -> p r w d", r=3, w=2)
        kg = [kg_a[:, r] for r in range(6)] + [kg_b[:, r] for r in range(3)]
        att_b = tail[:, 3072:3072 + RA * T].rearrange("p (r t) -> p r t", r=RA)
        hott = tail[0:T, 3500:3500 + 2 * E2].rearrange("p (r n) -> p r n", r=2)
        scores = rec[:, :, :].rearrange("p e m -> p (e m)")[:, 0:ET * H]
        sc_a = region_x[:, 0:CE]
        sc_m = region_x[:, CE:2 * CE + 1]
        sc_f = region_s[:, 0:CE]
        sc_di = sc_f.bitcast(I32)
        acc = region_x[0:T, :].rearrange("p (t f) -> p t f", t=NT)
        vg = carve(0, R, 2, D, parts=T)
        pv = carve(None, R, 2, D + RW, parts=T)
        hot = carve(None, RA, 2, T, parts=T)
        att_d = carve(None, RA, T)
        assert used[0] <= 8200
        fres = carve(12 * 2 * BN, 2, 2, D, parts=T)
        fgn = fxn = carve(None, 2, D, parts=T)
        fx2 = carve(None, 2, 2, D, parts=T)
        fxh, fxl = (parts_x[:, i] for i in range(2))
        fh = carve(None, 2, 2, BN)
        fh1h, fh1l, fh2h, fh2l = (parts_h[:, i] for i in range(4))
        fw = carve(None, 2, 2, NX, parts=T)
        fwt = carve(None, 2, BN, parts=NX)
        fyb = carve(None, 2, 2, D, parts=T)

        psum = ctx.enter_context(nc.psum_tensor("psum", [128, 8, 512], F32))

        c_a, c_b, c_ff, c_walk = sem("const_a"), sem("const_b"), sem("const_ff"), sem("const_walk")
        dve_o, act_o, pool_o = sem("dve_order"), sem("act_order"), sem("pool_order")
        bn_ready = sem("bn_ready")
        x_in = [sem(f"x_in{i}") for i in range(5)]
        a_stored = [sem(f"a_stored{u}") for u in range(2)]
        xn_ready, xn_turned, xnt_ready, xnb_ready = sem("xn_ready"), sem("xn_turned"), sem("xnt_ready"), sem("xnb_ready")
        sq_done, kv_done, mkv_done, sq_read, gnn_out = sem("sq_done"), sem("kv_done"), sem("mkv_done"), sem("sq_read"), sem("gnn_out")
        kt_ready, kexp_ready, kphi_ready, state_done = sem("kt_ready"), sem("kexp_ready"), sem("kphi_ready"), sem("state_done")
        zero_ready, state_ready, skip_row_ready = sem("zero_ready"), sem("state_ready"), sem("skip_row_ready")
        m_in = [sem(f"m_in{u}") for u in range(2)]
        m_q, m_exp, m_phi = sem("m_q"), sem("m_exp"), sem("m_phi")
        m_nd, m_an, m_att, m_at, m_o, m_x1 = sem("m_nd"), sem("m_an"), sem("m_att"), sem("m_at"), sem("m_o"), sem("m_x1")
        m_t, m_tc, m_h, m_hr, m_y, m_outr = sem("m_t"), sem("m_tc"), sem("m_h"), sem("m_hr"), sem("m_y"), sem("m_outr")
        m_stored, m_y_read, m_res_in = sem("m_stored"), sem("m_y_read"), sem("m_res_in")
        gather_go = sem("gather_go")
        gathered = [sem(f"gathered{r}") for r in range(RK)]
        att_in = [sem(f"att_in{r}") for r in range(RA)]
        dstb_in = [sem(f"dstb_in{r}") for r in range(RA)]
        jneg_ready, we_zero = sem("jneg_ready"), sem("we_zero")
        e_done, e_copied, hott_ready, q_done, mult_done, red_done, score_done = (
            sem("e_done"), sem("e_copied"), sem("hott_ready"), sem("q_done"), sem("mult_done"), sem("red_done"), sem("score_done"))
        turned, turned_out = sem("turned"), sem("turned_out")
        dst_in, mask_ready = sem("dst_in"), sem("mask_ready")
        fence_out, fence_in = sem("fence_out"), sem("fence_in")
        ends_ready, carry_ready, shifted, exped, back, back_out = (
            sem("ends_ready"), sem("carry_ready"), sem("shifted"), sem("exped"), sem("back"), sem("back_out"))
        last_in, walk_steps, walk_ready, walk_out, walk_in = (
            sem("last_in"), sem("walk_steps"), sem("walk_ready"), sem("walk_out"), sem("walk_in"))
        rec_ready, walk_clear = sem("rec_ready"), sem("walk_clear")
        acc_zero = sem("acc_zero")
        meta_ready = sem("meta_ready")
        v_in = [sem(f"v_in{r}") for r in range(R)]
        attv_in = [sem(f"attv_in{r}") for r in range(RA)]
        ev_done, pv_ready, sum_done, acc_done = sem("ev_done"), sem("pv_ready"), sem("sum_done"), sem("acc_done")
        f_in = [sem(f"f_in{u}") for u in range(2)]
        f_xn, f_t, f_tc, f_lg, f_sm, f_ex, f_w = sem("f_xn"), sem("f_t"), sem("f_tc"), sem("f_lg"), sem("f_sm"), sem("f_ex"), sem("f_w")
        f_wt, f_wtc, f_h1, f_r1, f_h2, f_r2, f_y, f_ya = (
            sem("f_wt"), sem("f_wtc"), sem("f_h1"), sem("f_r1"), sem("f_h2"), sem("f_r2"), sem("f_y"), sem("f_ya"))
        f_bo, f_bo_done, f_outr = sem("f_bo"), sem("f_bo_done"), sem("f_outr")
        f_wh, f_wl, f_xh, f_r1h, f_r2h = sem("f_wh"), sem("f_wl"), sem("f_xh"), sem("f_r1h"), sem("f_r2h")
        f_stored = [sem(f"f_stored{u}") for u in range(2)]

        CONST_A, CONST_B = 16 * 6, 16 * 9

        block = ctx.enter_context(nc.Block())

        def node_rows(t_expr, k=1):
            return bass.ds(t_expr * T, k * T)

        def tile_pair(ref, place):
            return ref[:, bass.ds(place, 2, CH), :]

        def twice(eng, n, body, order=()):
            body(0, 0)
            body(1, 1)
            for o in order:
                o.reset()
            with eng.Fori(1, n // 2) as it:
                body(it * 2, 0)
                body(it * 2 + 1, 1)
                for o in order:
                    o.reset()
            if n % 2:
                body(n - 1, 0)
                for o in order:
                    o.reset()

        @block.sync
        def _(sp):
            for i in range(5):
                sp.dma_start(x_all[:, i * 10:(i + 1) * 10, :],
                             a["x"][i * 10 * T:(i + 1) * 10 * T, :].rearrange("(t p) d -> p t d", p=T)).then_inc(x_in[i], 16)
            sp.dma_start(ident[:, :], a["ident"]).then_inc(c_a, 16)
            sp.dma_start(wcat, a["w_gnn"].rearrange("(c p) n -> p c n", p=128)).then_inc(c_a, 16)
            sp.dma_start(wmkv, a["w_mkv"].rearrange("(c p) n -> p c n", p=128)).then_inc(c_a, 16)
            sp.dma_start(rows[:, :], a["rows"]).then_inc(c_a, 16)
            sp.dma_start(cols[:, :], a["cols"]).then_inc(c_a, 16)
            sp.dma_start(blockm[:, :], a["blockm"]).then_inc(c_a, 16)

            sp.wait_ge(walk_ready, 1)
            sp.dma_start(walk_d.rearrange("w (i s) -> i w s", s=SU), walk_i[:, :, :]).then_inc(walk_out, 16)
            sp.dma_start(jb_d, walk_s[:, 3, :]).then_inc(walk_out, 16)
            sp.wait_ge(walk_clear, 1)
            sp.wait_ge(walk_out, 32)
            sp.dma_start(walk[0:1, 0, LAGD:LAGD + STEPS], walk_d[0:1, :]).then_inc(walk_in, 16)
            sp.dma_start(walk[0:1, 1, LAGQ:LAGQ + STEPS], walk_d[1:2, :]).then_inc(walk_in, 16)
            sp.dma_start(walk[0:1, 2, LAGP:LAGP + STEPS], walk_d[2:3, :]).then_inc(walk_in, 16)
            with nc.allow_non_contiguous_dma(reason="one row to every partition"):
                sp.dma_start(jb_all, jb_d.rearrange("i s -> (i s)").partition_broadcast(T)).then_inc(walk_in, 16)

            def store_a(t, u):
                sp.wait_ge(xnt_ready, t + 1)
                sp.wait_ge(xnb_ready, t + 1)
                sp.dma_start(xn_d[node_rows(t), :], xnb[:, u, :]).then_inc(a_stored[u], 16)
                sp.dma_start(xnt_d[:, :, node_rows(t)].rearrange("c p n -> p c n"), xnt[:, u]).then_inc(a_stored[u], 16)
                sp.wait_ge(gnn_out, t + 1)
                for i, tab in enumerate((k_tab, v_tab)):
                    sp.dma_start(tab[node_rows(t), :], kv[:, u, i * D:(i + 1) * D]).then_inc(a_stored[u], 16)
                sp.dma_start(skip_d[node_rows(t), :], skp[:, u, :]).then_inc(a_stored[u], 16)

            twice(sp, NT, store_a)

            sp.dma_start(wmq, a["w_mq"].rearrange("(c p) n -> p c n", p=128)).then_inc(c_b, 16)
            sp.dma_start(wmo, a["w_mo"].rearrange("(c p) n -> p c n", p=128)).then_inc(c_b, 16)
            sp.dma_start(wm1, a["w_m1"].rearrange("(c p) n -> p c n", p=128)).then_inc(c_b, 16)
            sp.dma_start(wm2, a["w_m2"].rearrange("(c p) n -> p c n", p=128)).then_inc(c_b, 16)
            for half in range(2):
                sp.wait_ge(we_zero, 1)
                sp.dma_start(we[half * ED:(half + 1) * ED, half, :], a["w_e"]).then_inc(c_b, 16)
            sp.dma_start(iota[:, :], a["iota"]).then_inc(c_b, 16)
            sp.dma_start(wr[:, :, :], a["w_r"].rearrange("(c p) n -> p c n", p=128)).then_inc(c_b, 16)
            sp.dma_start(bo_e[:, :], a["bo_e"]).then_inc(c_b, 16)

            for u in range(2):
                sp.wait_ge(a_stored[u], 16 * 5 * (NT // 2))
            sp.wait_ge(state_ready, 1)

            def load_mix(b, u):
                wait(sp, m_x1, b - 1)
                sp.dma_start(mxt[:, u], xnt_d[:, :, bass.ds(b * BN, BN)].rearrange("c p n -> p c n")).then_inc(m_in[u], 16)
                sp.dma_start(mxn[:, u], xn_d[bass.ds(b * BN, BN), :].rearrange("(t p) d -> p t d", p=T)).then_inc(m_in[u], 16)

            def load_skip(b):
                wait(sp, m_outr, b)
                sp.dma_start(mres[:, :, :], skip_d[bass.ds(b * BN, BN), :].rearrange("(t p) d -> p t d", p=T)).then_inc(m_res_in, 16)

            dst_all = a["dst"]
            sp.wait_ge(walk_in, 64)
            regs = [sp.alloc_register(f"sp_pair{s}") for s in range(SU)]

            late = [sp.alloc_register(f"sp_late{s}") for s in range(SU)]

            def load_dst(k, ra, reg):
                i = sp.snap(reg, min_val=0, max_val=EP - 1)
                wait(sp, hott_ready, k - RA + 1)
                sp.dma_start(dstb[:, ra, :], dst_all[bass.ds(i * E2, E2)].partition_broadcast(T)).then_inc(dstb_in[ra], 16)

            def b_body(b, u):
                load_mix(b, u)
                for s in range(SB):
                    k, ra = b * SB + s, s % RA
                    if s % SU == 0:
                        sp.load(regs, walk[0:1, 0, bass.ds(k + LAGD, SU)])
                        sp.load(late, walk[0:1, 0, bass.ds(k, SU)])
                    i = sp.snap(regs[s % SU], min_val=0, max_val=EP - 1)
                    wait(sp, e_done, k - RA + 1)
                    sp.dma_start(att_b[:, ra, :], a["attr_p"][:, bass.ds(i * T, T)]).then_inc(att_in[ra], 16)
                    if s >= LAGD or not (isinstance(b, int) and b == 0):
                        load_dst(k - LAGD, ra, late[s % SU])
                    if s == 0 and not (isinstance(b, int) and b < 2):
                        load_skip(b - 2)
                    if s == 11 and not (isinstance(b, int) and b < 2):
                        store_mix(b - 2)

            def store_mix(b):
                sp.wait_ge(m_outr, b + 1)
                sp.dma_start(res_d[bass.ds(b * BN, BN), :].rearrange("(t p) d -> p t d", p=T), mout[:, :, :]).then_inc(m_stored, 16)

            with nc.allow_non_contiguous_dma(reason="one row to every partition"):
                twice(sp, NB, b_body)
                sp.load(late, walk[0:1, 0, STEPS:STEPS + SU])
                for s in range(LAGD):
                    load_dst(STEPS - LAGD + s, s % RA, late[s])
            for b in (NB - 2, NB - 1):
                load_skip(b)
                store_mix(b)
            sp.wait_ge(score_done, STEPS)

            for i, name in enumerate(("w_x1", "w_x2", "w_xo")):
                sp.dma_start(wx[i].rearrange("p e c n -> p (e c) n"),
                             a[name].rearrange("(k p) n -> p k n", p=128)).then_inc(c_ff, 16)
            sp.wait_ge(m_stored, 16 * NB)
            dst_flat = a["dst"].rearrange("(c n) -> c n", c=CH)
            with nc.allow_non_contiguous_dma(reason="replicates dst over the heads"):
                for c in range(CH):
                    sp.dma_start(sc_di[c * H:(c + 1) * H, :],
                                 dst_flat[c:c + 1, :].broadcast_to((H, CE))).then_inc(dst_in, 16)
                sp.wait_ge(ends_ready, 1)
                sp.dma_start(fence_d.rearrange("k p -> p k"), ends[:, 0:4]).then_inc(fence_out, 16)
                sp.wait_ge(fence_out, 16)
                sp.dma_start(fence[:, 0:4, :], fence_d.rearrange("k (c h) -> h k c", h=H)).then_inc(fence_in, 16)
                sp.wait_ge(carry_ready, 1)
                sp.dma_start(fence_d[0:2, :].rearrange("k (c h) -> h k c", h=H), fence[:, 8:10, :]).then_inc(fence_out, 16)
                sp.wait_ge(fence_out, 32)
                sp.dma_start(ends[:, 4:6], fence_d[0:2, :].rearrange("k p -> p k")).then_inc(fence_in, 16)

            sp.wait_ge(back_out, CT)

            def d_body(it):
                sp.load(regs, walk[0:1, 0, bass.ds(it * SU + LAGD, SU)])
                for s in range(SU):
                    k, ra = it * SU + s, s % RA
                    i = sp.snap(regs[s], min_val=0, max_val=EP - 1)
                    wait(sp, ev_done, k - RA + 1)
                    sp.dma_start(att_d[:, ra, :], a["attr_p"][:, bass.ds(i * T, T)]).then_inc(attv_in[ra], 16)

            d_body(0)
            with sp.Fori(1, SI) as it:
                d_body(it)

            sp.wait_ge(acc_done, STEPS)

            def load_res(b, u):
                if not (isinstance(b, int) and b < 2):
                    sp.wait_ge(f_xn, b - 1)
                sp.dma_start(fres[:, u], res_d[bass.ds(b * BN, BN), :].rearrange("(t p) d -> p t d", p=T)).then_inc(f_in[u], 16)

            def store_out(b, u):
                sp.wait_ge(f_outr, b + 1)
                sp.dma_start(out[bass.ds(b * BN, BN), :].rearrange("(t p) d -> p t d", p=T), fyb[:, u]).then_inc(f_stored[u], 16)

            load_res(0, 0)
            load_res(1, 1)

            def e_body(b, u):
                store_out(b, u)
                load_res(b + 2, u)

            e_body(0, 0)
            e_body(1, 1)
            with sp.Fori(1, (NB - 2) // 2) as it:
                e_body(it * 2, 0)
                e_body(it * 2 + 1, 1)
            e_body(NB - 3, 0)
            store_out(NB - 2, 1)
            store_out(NB - 1, 0)
            sp.wait_ge(f_stored[0], 16 * ((NB + 1) // 2))
            sp.wait_ge(f_stored[1], 16 * (NB // 2))

        @block.gpsimd
        def _(pool):
            pool.dma_start(wz[:, :], a["dst_last"].broadcast_to((SI, EP))).then_inc(last_in, 16)
            nc.gpsimd.iota(wi[:, :], [[T, EP]], base=0, channel_multiplier=0).then_inc(walk_steps, 1)
            nc.gpsimd.iota(walk_k[:, 0:SU], [[T, SU]], base=0, channel_multiplier=T * SU).then_inc(walk_steps, 1)
            nc.gpsimd.iota(walk_k[:, SU:2 * SU], [[1, SU]], base=0, channel_multiplier=SU).then_inc(walk_steps, 1)
            nc.gpsimd.iota(node_i[:, :], [[0, 1]], base=0, channel_multiplier=1).then_inc(walk_steps, 1)
            pool.dma_start(src_t[:, :], a["src_t"]).then_inc(c_walk, 16)
            pool.dma_start(dst_t[:, :], a["dst_t"]).then_inc(c_walk, 16)

            pool.wait_ge(skip_row_ready, 1)

            def a_body(t, u):
                pool.wait_ge(xn_ready, t + 1)
                if not (isinstance(t, int) and t < 2):
                    pool.wait_ge(a_stored[u], (t - u) * 40)
                nc.gpsimd.tensor_tensor(xnb[:, u, :], xn[:, u, :], rows[:, R_BO:R_BO + D], ALU.add)
                x_t = x_all[:, bass.ds(t, 1), :].rearrange("p o d -> p (o d)")
                nc.gpsimd.tensor_tensor(x_t, x_t, skip_row, ALU.add).then_inc(xnb_ready, 1)

            twice(pool, NT, a_body)
            for u in range(2):
                pool.wait_ge(a_stored[u], 16 * 5 * (NT // 2))

            def b_body(b):
                for s in range(SB):
                    k, r = b * SB + s, s % RK
                    pool.wait_ge(e_copied, k + 1)
                    pool.sem_inc(gather_go, 1)
                    for w in range(2):
                        nc.gpsimd.indirect_dma_start(
                            kg[r][:, w, :], None, k_tab, bass.IndirectOffsetOnAxis(idx[:, r, w:w + 1], 0), compute_op=ALU.add
                        ).then_inc(gathered[r], 16)

            b_body(0)
            with pool.Fori(1, NB) as b:
                b_body(b)

            def d_body(it):
                for s in range(SU):
                    pool.wait_ge(meta_ready, it * SU + s + 1)
                    pool.sem_inc(gather_go, 1)
                    for w in range(2):
                        nc.gpsimd.indirect_dma_start(
                            vg[:, s, w, :], None, v_tab,
                            bass.IndirectOffsetOnAxis(pv[:, s, w, D + H + 1:D + RW].bitcast(I32), 0), compute_op=ALU.add
                        ).then_inc(v_in[s], 16)

            d_body(0)
            with pool.Fori(1, SI) as it:
                d_body(it)

        @block.tensor
        def _(pe):
            mm, tr = nc.tensor.matmul, nc.tensor.transpose
            pe.wait_ge(c_a, CONST_A)
            pe.wait_ge(zero_ready, 1)
            for c in range(2):
                mm(psum[:, 6 + c, 0:129], zero[:, 0:128], zero[:, :], start=True, stop=False)

            def turn(t, u):
                pe.wait_ge(xn_ready, t + 1)
                wait(pe, xnt_ready, t - 1)
                for c in range(2):
                    last = tr(psum[:, u, c * T:(c + 1) * T], xn[:, u, c * 128:(c + 1) * 128], ident[0:T, 0:T])
                last.then_inc(xn_turned, 1)

            def state(t, u):
                pe.wait_ge(kphi_ready, t + 1)
                for c in range(2):
                    last = mm(psum[:, 6 + c, 0:129], kphi[:, u, c * 128:(c + 1) * 128], vone[:, u, c, :],
                              start=False, stop=False)
                last.then_inc(state_done, 1)

            def a_body(t, u, first=False, last_tile=False):
                pe.wait_ge(xnt_ready, t + 1)
                for half, (read, done) in enumerate(((sq_read, sq_done), (gnn_out, kv_done))):
                    wait(pe, read, t)
                    for c in range(2):
                        last = mm(psum[0:T, 2 + half, :], xnt[:, u, c, :], wcat[:, c, half * 512:(half + 1) * 512],
                                  start=(c == 0), stop=(c == 1))
                    last.then_inc(done, 1)
                if not last_tile:
                    turn(t + 1, 1 - u)
                wait(pe, kphi_ready, t - 1)
                for c in range(2):
                    last = mm(psum[0:T, 4 + u, :], xnt[:, u, c, :], wmkv[:, c, :], start=(c == 0), stop=(c == 1))
                last.then_inc(mkv_done, 1)
                if not first:
                    state(t - 1, 1 - u)

            turn(0, 0)
            a_body(0, 0, first=True)
            a_body(1, 1)
            with pe.Fori(1, NT // 2 - 1) as it:
                a_body(it * 2, 0)
                a_body(it * 2 + 1, 1)
            a_body(NT - 2, 0)
            a_body(NT - 1, 1, last_tile=True)
            state(NT - 1, 1)
            for c in range(2):
                last = mm(psum[:, 6 + c, 0:129], zero[:, 0:128], zero[:, :], start=False, stop=True)
            last.then_inc(state_done, 1)

            pe.wait_ge(c_b, CONST_B)
            pe.wait_ge(state_ready, 1)

            def eproj(k, s, turn_of, sets, att, there, done, copied):
                pe.wait_ge(there[s % RA], turn_of * 16)
                wait(pe, copied, k - sets + 1)
                for w in range(2):
                    last = mm(psum[0:T, s % sets * 2 + w, 0:D], att[:, s % RA, :],
                              we[:, w, :], start=True, stop=True)
                last.then_inc(done, 1)

            def qprod(k, s, reg):
                j = pe.snap(reg, min_val=0, max_val=NT - 1)
                pe.wait_ge(hott_ready, k + 1)
                wait(pe, mult_done, k - 1)
                for w in range(2):
                    last = mm(psum[0:T, 2 + s % 2, w * D:(w + 1) * D], hott[:, s % 2, w * T:(w + 1) * T],
                              q_all[:, bass.ds(j, 1), :].rearrange("p o d -> p (o d)"), start=True, stop=True)
                last.then_inc(q_done, 1)

            def mix(b, u, g):
                kind = g[0]
                if kind == "q":
                    o = g[1]
                    if o == 0:
                        pe.wait_ge(m_in[u], (b // 2 + 1) * 32 if isinstance(b, int) else (b - u) * 16 + 32)
                        wait(pe, m_x1, b)
                    for c in range(2):
                        last = mm(psum[:, 7, o * BN:(o + 1) * BN], wmq[:, c, o * 128:(o + 1) * 128], mxt[:, u, c, :],
                                  start=(c == 0), stop=(c == 1))
                    if o == 1:
                        last.then_inc(m_q, 1)
                elif kind == "attend":
                    pe.wait_ge(m_phi, b + 1)
                    for t in range(2):
                        for c in range(2):
                            last = mm(psum[0:T, 4 + 3 * t, c * KV:(c + 1) * KV], mqp[:, c, t * T:(t + 1) * T], kvbd[:, c, :],
                                      start=True, stop=True)
                    last.then_inc(m_nd, 1)
                elif kind == "turn":
                    pe.wait_ge(m_an, b + 1)
                    for t in range(2):
                        for c in range(2):
                            last = tr(psum[:, 4, c * BN + t * T:c * BN + (t + 1) * T], matn[:, t, c * 128:(c + 1) * 128], ident[0:T, 0:T])
                    last.then_inc(m_att, 1)
                elif kind == "out":
                    pe.wait_ge(m_at, b + 1)
                    for t in range(2):
                        for c in range(2):
                            last = mm(psum[0:T, 7, t * D:(t + 1) * D], mat[:, c, t * T:(t + 1) * T], wmo[:, c, :],
                                      start=(c == 0), stop=(c == 1))
                    last.then_inc(m_o, 1)
                elif kind == "turn1":
                    pe.wait_ge(m_x1, b + 1)
                    for t in range(2):
                        for c in range(2):
                            last = tr(psum[:, 4, c * BN + t * T:c * BN + (t + 1) * T], mx1[:, t, c * 128:(c + 1) * 128], ident[0:T, 0:T])
                    last.then_inc(m_t, 1)
                elif kind == "up":
                    n = g[1]
                    pair, o = n // 2, n % 2
                    if n == 0:
                        pe.wait_ge(m_tc, b + 1)
                    if n == 2:
                        wait(pe, m_y_read, b)
                    if o == 0 and pair >= 2:
                        pe.wait_ge(m_hr, b * 4 + pair - 1)
                    for c in range(2):
                        last = mm(psum[:, 5 + pair % 2, o * BN:(o + 1) * BN], wm1[:, c, n * 128:(n + 1) * 128], mx1t[:, c, :],
                                  start=(c == 0), stop=(c == 1))
                    if o == 1:
                        last.then_inc(m_h, 1)
                elif kind == "down":
                    if g[1] == 0:
                        pe.wait_ge(m_hr, b * 4 + 4)
                    for i in range(g[1], g[2]):
                        t, n = i // 8, i % 8
                        last = mm(psum[0:T, 6, t * D:(t + 1) * D], mh[:, n, t * T:(t + 1) * T], wm2[:, n, :],
                                  start=(n == 0), stop=(n == 7))
                    if g[2] == 16:
                        last.then_inc(m_y, 1)

            pe.wait_ge(walk_in, 64)
            regs = [pe.alloc_register(f"pe_tile{s}") for s in range(SU)]
            mix_at = {1: ("q", 0), 2: ("q", 1), 8: ("attend",), 11: ("turn",), 12: ("out",)}
            late_at = {0: ("turn1",), 3: ("up", 0), 4: ("up", 1), 5: ("up", 2), 6: ("up", 3), 7: ("up", 4), 9: ("up", 5),
                       10: ("up", 6), 11: ("up", 7), 13: ("down", 0, 3), 14: ("down", 3, 6), 15: ("down", 6, 9),
                       16: ("down", 9, 12), 17: ("down", 12, 16)}

            def b_body(b, u):
                for s in range(SB):
                    k = b * SB + s
                    if s % SU == 0:
                        pe.load(regs, walk[0:1, 1, bass.ds(k, SU)])
                    eproj(k, s, b * (SB // RA) + s // RA + 1, 1, att_b, att_in, e_done, e_copied)
                    if s >= LAGQ or not (isinstance(b, int) and b == 0):
                        qprod(k - LAGQ, s, regs[s % SU])
                    if s in late_at and not (isinstance(b, int) and b == 0):
                        mix(b - 1, 1 - u, late_at[s])
                    if s in mix_at:
                        mix(b, u, mix_at[s])

            twice(pe, NB, b_body)
            pe.load(regs, walk[0:1, 1, STEPS:STEPS + SU])
            for s in range(LAGQ):
                qprod(STEPS - LAGQ + s, s, regs[s])
            for g in late_at.values():
                mix(NB - 1, 0, g)

            pe.wait_ge(score_done, STEPS)
            for bt in range(CT):
                wait(pe, turned_out, bt - 3)
                tr(psum[:, bt % 4, 0:T], scores[:, bt * 128:(bt + 1) * 128], ident[0:T, 0:T]).then_inc(turned, 1)
            pe.wait_ge(exped, 1)
            for bt in range(CT):
                wait(pe, back_out, bt - 3)
                if bt < 4:
                    pe.wait_ge(turned_out, CT)
                tr(psum[0:T, bt % 4, 0:128], sc_a[:, bt * T:(bt + 1) * T], ident[:, :]).then_inc(back, 1)

            pe.wait_ge(back_out, CT)

            def sums(k, s):
                pe.wait_ge(pv_ready, k + 1)
                bank = psum[0:T, 4 + s % 2, 0:PV]
                wait(pe, acc_done, k - 1)
                for w in range(2):
                    last = mm(bank, hot[:, s % RA, w, :], pv[:, s, w, 0:PV], start=(w == 0), stop=(w == 1))
                last.then_inc(sum_done, 1)

            def d_body(it):
                for s in range(SU):
                    k = it * SU + s
                    eproj(k, s, it * (SU // RA) + s // RA + 1, 2, att_d, attv_in, ev_done, meta_ready)
                    if s >= LAGS or not (isinstance(it, int) and it == 0):
                        sums(k - LAGS, (s - LAGS) % SU)

            d_body(0)
            with pe.Fori(1, SI) as it:
                d_body(it)
            for s in range(SU - LAGS, SU):
                sums(STEPS - SU + s, s)

            pe.wait_ge(c_ff, 48)
            pe.wait_ge(acc_done, STEPS)

            def prelude(b, u):
                pe.wait_ge(f_xn, b + 1)
                wait(pe, f_tc, b)
                for t in range(2):
                    for c in range(2):
                        last = tr(psum[:, 6, c * BN + t * T:c * BN + (t + 1) * T], fxn[:, t, c * 128:(c + 1) * 128], ident[0:T, 0:T])
                last.then_inc(f_t, 1)

            def mm3(to, lhs, rhs, start, stop):
                mm(to, lhs[0], rhs[0], start=start, stop=False)
                mm(to, lhs[0], rhs[1], start=False, stop=False)
                return mm(to, lhs[1], rhs[0], start=False, stop=stop)

            def split_weights(b, e, i):
                if isinstance(b, int) and b == 0:
                    pe.wait_ge(f_wl, 1 + e * 3 + i + 1)

            def layer1(b, u, e):
                n = b * NX + e
                wait(pe, f_r1h, n - 1)
                split_weights(b, e, 0)
                for o in range(2):
                    for c in range(2):
                        last = mm3(psum[:, e % 2, o * BN:(o + 1) * BN], [w[0][:, e, c, o * 128:(o + 1) * 128] for w in (wxh, wxl)],
                                   [x[:, u, c, :] for x in (fxh, fxl)], c == 0, c == 1)
                last.then_inc(f_h1, 1)

            def layer2(b, u, e):
                n = b * NX + e
                pe.wait_ge(f_r1, n + 1)
                wait(pe, f_r2h, n - 1)
                split_weights(b, e, 1)
                for o in range(2):
                    for c in range(2):
                        last = mm3(psum[:, 2 + e % 2, o * BN:(o + 1) * BN], [w[1][:, e, c, o * 128:(o + 1) * 128] for w in (wxh, wxl)],
                                   [x[:, e % 2, c, :] for x in (fh1h, fh1l)], c == 0, c == 1)
                last.then_inc(f_h2, 1)

            def layer3(b, u, e):
                n = b * NX + e
                pe.wait_ge(f_r2, n + 1)
                wait(pe, f_ya, n - 1)
                split_weights(b, e, 2)
                for t in range(2):
                    for c in range(2):
                        last = mm3(psum[0:T, 4 + e % 2, t * D:(t + 1) * D], [x[:, e % 2, c, t * T:(t + 1) * T] for x in (fh2h, fh2l)],
                                   [w[2][:, e, c, :] for w in (wxh, wxl)], c == 0, c == 1)
                last.then_inc(f_y, 1)

            def router(b, u):
                pe.wait_ge(f_tc, b + 1)
                wait(pe, f_bo, b)
                if isinstance(b, int) and b == 0:
                    pe.wait_ge(f_wl, 1)
                for t in range(2):
                    for c in range(2):
                        last = mm3(psum[0:T, 7, t * NX:(t + 1) * NX], [x[:, u, c, t * T:(t + 1) * T] for x in (fxh, fxl)],
                                   [wr_h[:, c, :], wr_l[:, c, :]], c == 0, c == 1)
                last.then_inc(f_lg, 1)

            def weights_t(b, u):
                pe.wait_ge(f_w, b + 1)
                for t in range(2):
                    last = tr(psum[0:NX, 7, 256 + t * T:256 + (t + 1) * T], fw[:, u, t, :], ident[0:T, 0:T])
                last.then_inc(f_wt, 1)

            def bias_out(b, u):
                pe.wait_ge(f_wtc, b + 1)
                for t in range(2):
                    last = mm(psum[0:T, 7, t * D:(t + 1) * D], fwt[:, u, t * T:(t + 1) * T], bo_e[:, :], start=True, stop=True)
                last.then_inc(f_bo_done, 1)

            def e_body(b, u, last_block=False):
                router(b, u)
                for e in range(NX + 2):
                    if e < NX:
                        layer1(b, u, e)
                    if 1 <= e <= NX:
                        layer2(b, u, e - 1)
                    if e == 2:
                        bias_out(b, u)
                    if e >= 2:
                        layer3(b, u, e - 2)
                    if e == 1:
                        weights_t(b, u)
                    if e == 7 and not last_block:
                        prelude(b + 1, 1 - u)

            prelude(0, 0)
            e_body(0, 0)
            e_body(1, 1)
            with pe.Fori(1, NB // 2) as it:
                e_body(it * 2, 0)
                e_body(it * 2 + 1, 1)
            e_body(NB - 1, 0, last_block=True)

        @block.scalar
        def _(act):
            copy, fn = nc.scalar.copy, nc.scalar.activation
            order = Order(act, act_o)

            def a_body(t, u):
                act.wait_ge(xn_turned, t + 1)
                wait(act, mkv_done, t - 1)
                if not (isinstance(t, int) and t < 2):
                    act.wait_ge(a_stored[u], (t - u) * 40)
                copy(xnt[:, u].rearrange("p c n -> p (c n)"), psum[:, u, 0:2 * T]).then_inc(xnt_ready, 1)
                if not (isinstance(t, int) and t == 0):
                    phi_k(t - 1, 1 - u)

            def phi_k(t, u):
                act.wait_ge(kt_ready, t + 1)
                wait(act, kphi_ready, t - 1)
                fn(krelu[:, u, :], kt[:, u, :], ACT.Relu)
                fn(kexp[:, u, :], kt[:, u, :], ACT.Exp).then_inc(kexp_ready, 1)

            twice(act, NT, a_body)
            phi_k(NT - 1, 1)

            act.wait_ge(state_ready, 1)
            act.wait_ge(c_a, CONST_A)
            act.wait_ge(c_walk, 32)
            act.wait_ge(walk_in, 64)
            act.wait_ge(jneg_ready, 1)
            regs = [act.alloc_register(f"act_pair{s}") for s in range(SU)]

            def start_edges(k, s, reg):
                i = act.snap(reg, min_val=0, max_val=EP - 1)
                wait(act, red_done, k - RK + 1)
                copy(idx[:, s % RK, :], src_t[:, bass.ds(i * 2, 2)])
                act.wait_ge(e_done, k + 1)
                copy(kg[s % RK], psum[0:T, 0:2, 0:D]).then_inc(e_copied, 1)

            def one_hot(k, s, turn_of):
                act.wait_ge(dstb_in[s % RA], turn_of * 16)
                wait(act, q_done, k - 1)
                order(fn(hott[:, s % 2, :], dstb[:, s % RA, :], ACT.Abs, bias=jneg[:, bass.ds(k, 1)]))
                fn(hott[:, s % 2, :], hott[:, s % 2, :], ACT.Relu, bias=1.0, scale=-1.0).then_inc(hott_ready, 1)

            def mix(b, g):
                if g == "phi":
                    act.wait_ge(m_q, b + 1)
                    for c in range(2):
                        fn(mq[:, c, :], psum[:, 7, c * BN:(c + 1) * BN], ACT.Relu, bias=cols[:, C_BQ + c:C_BQ + c + 1])
                        last = fn(mqe[:, c, :], psum[:, 7, c * BN:(c + 1) * BN], ACT.Exp, bias=cols[:, C_BQ + c:C_BQ + c + 1])
                    last.then_inc(m_exp, 1)
                elif g == "turn":
                    act.wait_ge(m_att, b + 1)
                    copy(mat[:, :, :].rearrange("p c n -> p (c n)"), psum[:, 4, 0:2 * BN]).then_inc(m_at, 1)
                elif g == "turn1":
                    act.wait_ge(m_t, b + 1)
                    for c in range(2):
                        last = fn(mx1t[:, c, :], psum[:, 4, c * BN:(c + 1) * BN], ACT.Identity,
                                  scale=cols[:, C_G1 + c:C_G1 + c + 1], bias=cols[:, C_E1 + c:C_E1 + c + 1])
                    last.then_inc(m_tc, 1)
                else:
                    pair = g
                    act.wait_ge(m_h, b * 4 + pair + 1)
                    for o in range(2):
                        n = 2 * pair + o
                        last = fn(mh[:, n, :], psum[:, 5 + pair % 2, o * BN:(o + 1) * BN], ACT.Relu,
                                  bias=cols[:, C_B1 + n:C_B1 + n + 1])
                    last.then_inc(m_hr, 1)

            mix_at, late_at = {4: "phi", 11: "turn"}, {0: "turn1", 5: 0, 7: 1, 9: 2, 11: 3}

            def b_body(b, u):
                for s in range(SB):
                    k = b * SB + s
                    if s % SU == 0:
                        act.load(regs, walk[0:1, 0, bass.ds(k + LAGD, SU)])
                    start_edges(k, s, regs[s % SU])
                    if s >= LAGD or not (isinstance(b, int) and b == 0):
                        one_hot(k - LAGD, (s - LAGD) % SB, b * (SB // RA) + s // RA)
                    if s in mix_at:
                        mix(b, mix_at[s])
                    if s in late_at and not (isinstance(b, int) and b == 0):
                        mix(b - 1, late_at[s])

            twice(act, NB, b_body, (order,))
            for s in range(LAGD):
                one_hot(STEPS - LAGD + s, SB - LAGD + s, STEPS // RA)
            for g in late_at.values():
                mix(NB - 1, g)
            order.reset()

            act.wait_ge(score_done, STEPS)
            for bt in range(CT):
                act.wait_ge(turned, bt + 1)
                copy(sc_a[:, bt * T:(bt + 1) * T], psum[:, bt % 4, 0:T]).then_inc(turned_out, 1)
            act.wait_ge(shifted, 1)
            fn(sc_a, sc_a, ACT.Exp, scale=SCALE).then_inc(exped, 1)
            sview = rec[:, :, :].rearrange("p (b c) m -> p b c m", c=CH)
            for bt in range(CT):
                act.wait_ge(back, bt + 1)
                copy(sview[:, bt, :, 0:H], psum[0:T, bt % 4, 0:128].rearrange("p (c h) -> p c h", c=CH)).then_inc(back_out, 1)

            act.wait_ge(back_out, CT)
            act.wait_ge(rec_ready, 2)

            def d_body(it):
                act.load(regs, walk[0:1, 2, bass.ds(it * SU + LAGP, SU)])
                for s in range(SU):
                    k = it * SU + s
                    place = act.snap(regs[s], min_val=0, max_val=ET - CH - 1)
                    wait(act, sum_done, k - R + 1)
                    copy(pv[:, s, :, D:D + RW], tile_pair(rec, place))
                    act.wait_ge(ev_done, k + 1)
                    copy(vg[:, s, :, :], psum[0:T, s % 2 * 2:s % 2 * 2 + 2, 0:D]).then_inc(meta_ready, 1)

            d_body(0)
            with act.Fori(1, SI) as it:
                d_body(it)

            act.wait_ge(acc_done, STEPS)

            def turned_x(b, u):
                act.wait_ge(f_t, b + 1)
                if not (isinstance(b, int) and b < 2):
                    act.wait_ge(f_h1, (b - 1) * NX)
                copy(fxh[:, u].rearrange("p c n -> p (c n)"), psum[:, 6, 0:2 * BN]).then_inc(f_xh, 1)

            def upper_weights(e):
                for i in range(3):
                    copy(wxh[i][:, e].rearrange("p c n -> p (c n)"), wx[i][:, e].rearrange("p c n -> p (c n)")).then_inc(f_wh, 1)

            def relu(done, used, low, ready, bk, to, layer, b, e):
                n = b * NX + e
                act.wait_ge(done, n + 1)
                wait(act, low, n)
                for o in range(2):
                    col = e * 2 + o
                    last = fn(fh[:, layer, o, :], psum[:, bk + e % 2, o * BN:(o + 1) * BN], ACT.Relu,
                              bias=bns[:, layer, 1, col:col + 1], scale=bns[:, layer, 0, col:col + 1])
                order(last)
                wait(act, used, n - 1)
                copy(to[:, e % 2].rearrange("p c n -> p (c n)"), fh[:, layer].rearrange("p c n -> p (c n)")).then_inc(ready, 1)

            def e_body(b, u, last_block=False):
                for e in range(NX + 1):
                    if isinstance(b, int) and b == 0 and e < NX - 2:
                        upper_weights(e + 2)
                    if e < NX:
                        relu(f_h1, f_h2, f_r1, f_r1h, 0, fh1h, 0, b, e)
                    if e == 0:
                        act.wait_ge(f_sm, b + 1)
                        fn(fsm[:, u, 0:16], fsm[:, u, 0:16], ACT.Exp).then_inc(f_ex, 1)
                    if e >= 1:
                        relu(f_h2, f_y, f_r2, f_r2h, 2, fh2h, 1, b, e - 1)
                    if e == 1:
                        act.wait_ge(f_wt, b + 1)
                        copy(fwt[:, u, :], psum[0:NX, 7, 256:256 + BN]).then_inc(f_wtc, 1)
                    if e == 7 and not last_block:
                        turned_x(b + 1, 1 - u)

            act.wait_ge(c_ff, 48)
            copy(wr_h[:, :, :], wr[:, :, :]).then_inc(f_wh, 1)
            upper_weights(0)
            upper_weights(1)
            act.wait_ge(bn_ready, 2)
            turned_x(0, 0)
            e_body(0, 0)
            e_body(1, 1)
            order.reset()
            with act.Fori(1, NB // 2) as it:
                e_body(it * 2, 0)
                e_body(it * 2 + 1, 1)
                order.reset()
            e_body(NB - 1, 0, last_block=True)

        @block.vector
        def _(dve):
            tt, ts, stt = nc.vector.tensor_tensor, nc.vector.tensor_scalar, nc.vector.scalar_tensor_tensor
            order = Order(dve, dve_o)

            def signal(ins, sem, value):
                ins.then_inc(sem, 1)
                dve.wait_ge(sem, value)

            def root_start(x, eps, y):
                order(ts(x, x, eps, None, ALU.add))
                order(ts(y.bitcast(I32), x.bitcast(I32), 1, None, ALU.logical_shift_right))
                order(ts(y.bitcast(I32), y.bitcast(I32), -1.0, float(0x5F3759DF), ALU.mult, ALU.add))

            def root_step(x, y, t):
                order(stt(t, y, 0.5, y, ALU.mult, ALU.mult))
                order(tt(t, t, x, ALU.mult))
                order(stt(y, t, 1.5, y, ALU.subtract, ALU.mult, reverse0=True))

            def rsqrt(x, eps, y, t):
                root_start(x, eps, y)
                for _ in range(3):
                    root_step(x, y, t)

            var, root, scratch = stats[:, :, 7:8], stats[:, :, 8:9], stats[:, :, 9:10]

            def norm_stats(x):
                for t in range(2):
                    i = nc.vector.bn_stats(stats[:, t, 0:6], x[:, t, :])
                order(i)
                for t in range(2):
                    i = nc.vector.bn_aggr(stats[:, t, 6:8], stats[:, t, 0:6])
                order(i)

            def norm_apply(x, to):
                for t in range(2):
                    i = ts(to[:, t, :], x[:, t, :], stats[:, t, 6:7], stats[:, t, 8:9], ALU.subtract, ALU.mult)
                return i

            def norm2(x, to):
                norm_stats(x)
                rsqrt(var, LN_EPS, root, scratch)
                return norm_apply(x, to)

            def row2(at):
                return rows[:, at:at + D].unsqueeze(1).broadcast_to((T, 2, D))

            nc.vector.memset(we[:, :, :].rearrange("p w d -> p (w d)"), 0.0).then_inc(we_zero, 1)
            nc.vector.memset(zero, 0.0)
            nc.vector.memset(vone.rearrange("p u c n -> p (u c n)"), 1.0).then_inc(zero_ready, 1)
            dve.wait_ge(last_in, 16)
            dve.wait_ge(walk_steps, 4)
            nc.vector.tensor_copy(node[:, :], node_i[:, :])
            order(tt(wf, wz, wi, ALU.add))
            order(nc.vector.tensor_copy(walk_s[:, 0, :], walk_k[:, 0:SU]))
            for s in range(SU):
                order(ts(wl, wf, walk_s[:, 0, s:s + 1], 0.0, ALU.is_lt, ALU.add, accum_out=walk_s[:, 1, s:s + 1]))
            order(ts(walk_s[:, 2, :], walk_s[:, 1, :], float(EP - 1), float(T), ALU.min, ALU.mult))
            order(tt(walk_s[:, 3, :], walk_s[:, 0, :], walk_s[:, 2, :], ALU.subtract))
            order(ts(walk_s[:, 1, :], walk_s[:, 1, :], float(EP - 1), None, ALU.min))
            order(nc.vector.tensor_copy(walk_i[:, 0, :], walk_s[:, 1, :]))
            order(tt(walk_s[:, 4, :], walk_k[:, SU:2 * SU], walk_s[:, 1, :], ALU.subtract))
            order(ts(walk_s[:, 4, :], walk_s[:, 4, :], float(NT - 1), None, ALU.min))
            order(nc.vector.tensor_copy(walk_i[:, 1, :], walk_s[:, 4, :]))
            order(nc.vector.memset(walk_s[:, 5, :], 0.0))
            for c in range(1, CH):
                order(stt(walk_s[:, 5, :], walk_s[:, 1, :], float(CT // 2 * c), walk_s[:, 5, :], ALU.is_ge, ALU.add))
            order(ts(walk_s[:, 4, :], walk_s[:, 1, :], float(2 * CH), None, ALU.mult))
            order(stt(walk_s[:, 4, :], walk_s[:, 5, :], float(1 - CT * CH), walk_s[:, 4, :], ALU.mult, ALU.add))
            nc.vector.tensor_copy(walk_i[:, 2, :], walk_s[:, 4, :]).then_inc(walk_ready, 1)
            nc.vector.memset(walk.rearrange("p w n -> p (w n)"), 0).then_inc(walk_clear, 1)
            order.reset()

            def ln(t, u):
                wait(dve, xn_turned, t - 1)
                wait(dve, xnb_ready, t - 1)
                one, st = bass.ds(t, 1), xstat[:, bass.ds(t, 1), :].rearrange("p o k -> p (o k)")
                ts(xn[:, u, :], x_all[:, one, :].rearrange("p o d -> p (o d)"), st[:, 0:1], st[:, 2:3],
                   ALU.subtract, ALU.mult).then_inc(xn_ready, 1)

            def phi_k(t, u):
                dve.wait_ge(kexp_ready, t + 1)
                wait(dve, state_done, t - 1)
                stt(kphi[:, u, :], kexp[:, u, :], 1.0, krelu[:, u, :], ALU.min, ALU.add).then_inc(kphi_ready, 1)

            def tables(t, u):
                dve.wait_ge(sq_done, t + 1)
                dve.wait_ge(xnb_ready, t + 1)
                if not (isinstance(t, int) and t < 2):
                    dve.wait_ge(a_stored[u], (t - u) * 40)
                x_t = x_all[:, bass.ds(t, 1), :].rearrange("p o d -> p (o d)")
                order(tt(skp[:, u, :], psum[0:T, 2, 0:D], x_t, ALU.add))
                tt(x_t, psum[0:T, 2, D:2 * D], rows[:, R_GNN + D:R_GNN + 2 * D], ALU.add).then_inc(sq_read, 1)
                dve.wait_ge(kv_done, t + 1)
                tt(kv[:, u, :], psum[0:T, 3, :], rows[:, R_GNN + 2 * D:R_GNN + 4 * D], ALU.add).then_inc(gnn_out, 1)
                dve.wait_ge(mkv_done, t + 1)
                wait(dve, state_done, t - 1)
                tt(kt[:, u, :], psum[0:T, 4 + u, 0:D], rows[:, R_MKV:R_MKV + D], ALU.add).then_inc(kt_ready, 1)
                order(tt(vone[:, u, :, 0:128], psum[0:T, 4 + u, D:2 * D].rearrange("p (c n) -> p c n", c=2),
                         rows[:, R_MKV + D:R_MKV + 2 * D].rearrange("p (c n) -> p c n", c=2), ALU.add))

            def a_body(t, u, last_tile=False):
                if not last_tile:
                    ln(t + 1, 1 - u)
                if not (isinstance(t, int) and t == 0):
                    phi_k(t - 1, 1 - u)
                tables(t, u)

            for i in range(5):
                dve.wait_ge(x_in[i], 16)
                for t in range(10):
                    last = nc.vector.bn_stats(xsix[:, t, :], x_all[:, i * 10 + t, :])
                order(last)
                for t in range(10):
                    last = nc.vector.bn_aggr(xstat[:, i * 10 + t, 0:2], xsix[:, t, :])
                order(last)
            rsqrt(xstat[:, :, 1:2], LN_EPS, xstat[:, :, 2:3], xstat[:, :, 3:4])
            dve.wait_ge(c_a, CONST_A)
            tt(skip_row, skip_row, rows[:, R_E2:R_E2 + D], ALU.add).then_inc(skip_row_ready, 1)
            order(tt(rows[:, R_B2:R_B2 + D], rows[:, R_B2:R_B2 + D], rows[:, R_E1:R_E1 + D], ALU.add))
            ln(0, 0)
            a_body(0, 0)
            a_body(1, 1)
            order.reset()
            with dve.Fori(1, NT // 2 - 1) as it:
                a_body(it * 2, 0)
                a_body(it * 2 + 1, 1)
                order.reset()
            a_body(NT - 2, 0)
            a_body(NT - 1, 1, last_tile=True)
            phi_k(NT - 1, 1)
            dve.wait_ge(state_done, NT + 1)
            for c in range(2):
                order(nc.vector.tensor_copy(ksum[:, c:c + 1], psum[:, 6 + c, 128:129]))
                tt(kvbd[:, c, 0:128], psum[:, 6 + c, 0:128], blockm[:, :], ALU.mult)
                last = ts(kvbd[:, c, 128:KV], blockm[:, ::C], ksum[:, c:c + 1], None, ALU.mult)
            last.then_inc(state_ready, 1)
            order.reset()

            dve.wait_ge(walk_in, 64)
            ts(jneg, jb_all, -1.0, node[:, 0:1], ALU.mult, ALU.subtract).then_inc(jneg_ready, 1)
            order(nc.vector.memset(scores, 0.0))
            order.reset()
            regs = [dve.alloc_register(f"dve_walk{s}") for s in range(SU)]
            score_rows = scores.rearrange("p (e h) -> p e h", h=H)

            def multiply(k, s, turn_of):
                dve.wait_ge(gathered[s % RK], turn_of * 32)
                dve.wait_ge(q_done, k + 1)
                flat = kg[s % RK].rearrange("p w d -> p (w d)")
                tt(flat, flat, psum[0:T, 2 + s % 2, :], ALU.mult).then_inc(mult_done, 1)

            def total(k, s):
                dve.wait_ge(mult_done, k + 1)
                wait(dve, score_done, k - 2)
                nc.vector.tensor_reduce(part[:, s % 3, :], kg[s % RK].rearrange("p w (h c) -> p (w h) c", c=C),
                                        AX, ALU.add).then_inc(red_done, 1)

            def keep(k, s, reg):
                to = tile_pair(score_rows, dve.snap(reg, min_val=0, max_val=ET - CH - 1))
                dve.wait_ge(red_done, k + 1)
                wait(dve, score_done, k)
                tt(to, to, part[:, s % 3, :].rearrange("p (w h) -> p w h", w=2), ALU.add).then_inc(score_done, 1)

            def mix(b, u, g):
                if g == "phi":
                    dve.wait_ge(m_exp, b + 1)
                    stt(mqp, mqe, 1.0, mq, ALU.min, ALU.add).then_inc(m_phi, 1)
                elif g == "attend":
                    dve.wait_ge(m_nd, b + 1)
                    den = mden.rearrange("p o t h -> p (o t h)")
                    both = [psum[0:T, 4 + 3 * t, 0:2 * KV].rearrange("p (c n) -> p c n", c=2) for t in range(2)]
                    for t in range(2):
                        i = ts(mden[:, 0, t].rearrange("p (c h) -> p c h", c=2), both[t][:, :, 128:KV], Z_EPS, None, ALU.add)
                    order(i)
                    order(nc.vector.reciprocal(den[:, 2 * H:4 * H], den[:, 0:2 * H]))
                    for t in range(2):
                        i = tt(matn[:, t, :].rearrange("p (c h d) -> p c h d", c=2, d=C),
                               both[t][:, :, 0:128].rearrange("p c (h d) -> p c h d", d=C),
                               mden[:, 1, t, :].rearrange("p (c h) -> p c h", c=2).unsqueeze(3).broadcast_to((T, 2, H // 2, C)), ALU.mult)
                    i.then_inc(m_an, 1)
                elif g == "sum1":
                    dve.wait_ge(m_o, b + 1)
                    dve.wait_ge(m_in[u], (b // 2 + 1) * 32 if isinstance(b, int) else (b - u) * 16 + 32)
                    order(tt(my[:, u], psum[0:T, 7, :].rearrange("p (t d) -> p t d", t=2), mxn[:, u], ALU.add))
                    norm_stats(my[:, u])
                elif g == "norm1":
                    signal(norm_apply(my[:, u], mx1), m_x1, b + 1)
                    order(tt(my[:, u], mx1, row2(R_G1), ALU.mult))
                elif g == "root":
                    root_start(var, LN_EPS, root)
                    root_step(var, root, scratch)
                elif g == "root2":
                    root_step(var, root, scratch)
                    root_step(var, root, scratch)
                elif g == "sum2":
                    dve.wait_ge(m_y, b + 1)
                    wait(dve, m_stored, b * 16)
                    signal(tt(mout[:, :, :], psum[0:T, 6, :].rearrange("p (t d) -> p t d", t=2), my[:, u], ALU.add), m_y_read, b + 1)
                    order(tt(mout[:, :, :], mout[:, :, :], row2(R_B2), ALU.add))
                    norm_stats(mout)
                elif g == "norm2":
                    order(norm_apply(mout, mx2))
                    order(tt(mx2[:, :, :], mx2[:, :, :], row2(R_G2), ALU.mult))
                    dve.wait_ge(m_res_in, (b + 1) * 16)
                    tt(mout[:, :, :], mx2[:, :, :], mres[:, :, :], ALU.add).then_inc(m_outr, 1)

            mix_at = {3: "phi", 5: "attend", 10: "sum1", 11: "root", 12: "root2", 13: "norm1"}
            late_at = {0: "sum2", 2: "root", 4: "root2", 6: "norm2"}

            def b_body(b, u):
                for s in range(SB):
                    k = b * SB + s
                    if s % SU == 0:
                        dve.load(regs, walk[0:1, 2, bass.ds(k, SU)])
                    if s in late_at and not (isinstance(b, int) and b < 2):
                        mix(b - 2, u, late_at[s])
                    if s in mix_at:
                        mix(b, u, mix_at[s])
                    multiply(k, s, b * (SB // RK) + s // RK + 1)
                    if s >= 1 or not (isinstance(b, int) and b == 0):
                        total(k - 1, (s - 1) % SB)
                    if s >= LAGP or not (isinstance(b, int) and b == 0):
                        keep(k - LAGP, (s - LAGP) % SB, regs[s % SU])

            twice(dve, NB, b_body, (order,))
            total(STEPS - 1, SB - 1)
            dve.load(regs, walk[0:1, 2, STEPS:STEPS + SU])
            for s in range(LAGP):
                keep(STEPS - LAGP + s, SB - LAGP + s, regs[s])
            for b in (NB - 2, NB - 1):
                for g in late_at.values():
                    mix(b, b % 2, g)
            order.reset()

            for layer in range(2):
                col = [cols[:, C_FF + (layer * 5 + i) * 16:C_FF + (layer * 5 + i + 1) * 16] for i in range(5)]
                b_, g_, be_, m_, v_ = col
                scale, bias = bns[:, layer, 0, :], bns[:, layer, 1, :]
                rsqrt(v_, BN_EPS, scale, bias)
                order(tt(scale, scale, g_, ALU.mult))
                order(tt(bias, b_, m_, ALU.subtract))
                order(tt(bias, bias, scale, ALU.mult))
                tt(bias, bias, be_, ALU.add).then_inc(bn_ready, 1)
            order.reset()

            dve.wait_ge(dst_in, 16 * CH)
            dve.wait_ge(turned_out, CT)
            dve.wait_ge(c_walk, 32)
            dve.wait_ge(turned, CT)
            by_place = rec[:, :, :].rearrange("p (b c) m -> p c b m", c=CH)
            nc.vector.tensor_copy(by_place[:, :, :, H], dst_t[:, :].rearrange("p (c b) -> p c b", c=CH)).then_inc(rec_ready, 1)
            nc.vector.tensor_copy(by_place[:, :, :, H + 1].bitcast(I32), src_t[:, :].rearrange("p (c b) -> p c b", c=CH)).then_inc(rec_ready, 1)
            nc.vector.memset(sc_m[:, 0:1], 0.0)
            nc.vector.memset(sc_m[:, CE:CE + 1], 0.0)
            nc.vector.tensor_copy(ends[:, 2:3], sc_di[:, 0:1])
            nc.vector.tensor_copy(ends[:, 3:4], sc_di[:, CE - 1:CE])
            order(tt(sc_m[:, 1:CE], sc_di[:, 1:CE], sc_di[:, 0:CE - 1], ALU.is_equal))
            order(ts(sc_m[:, 1:CE], sc_m[:, 1:CE], BIG, -BIG, ALU.mult, ALU.add))
            scan = nc.vector.tensor_tensor_scan
            m_fwd, m_bwd = sc_m[:, 0:CE], sc_m[:, 1:CE + 1][:, ::-1]
            order(scan(sc_f, m_fwd, sc_a, -BIG, ALU.add, ALU.max))
            order(nc.vector.tensor_copy(ends[:, 0:1], sc_f[:, CE - 1:CE]))
            order(scan(sc_f[:, ::-1], m_bwd, sc_a[:, ::-1], -BIG, ALU.add, ALU.max))
            nc.vector.tensor_copy(ends[:, 1:2], sc_f[:, 0:1]).then_inc(ends_ready, 1)
            dve.wait_ge(fence_in, 16)
            nc.vector.memset(fence[:, 4, 0:1], 0.0)
            tt(fence[:, 4, 1:CH], fence[:, 2, 1:CH], fence[:, 3, 0:CH - 1], ALU.is_equal)
            order(tt(fence[:, 5, :], fence[:, 2, :], fence[:, 3, :], ALU.is_equal))
            order(ts(fence[:, 4:6, :], fence[:, 4:6, :], BIG, -BIG, ALU.mult, ALU.add))
            nc.vector.memset(fence[:, 8:10, :], -BIG)
            order(tt(fence[:, 6, :], fence[:, 4, :], fence[:, 5, :], ALU.add))
            order(scan(fence[:, 7, :], fence[:, 6, :], fence[:, 0, :], -BIG, ALU.add, ALU.max))
            order(tt(fence[:, 8, 1:CH], fence[:, 7, 0:CH - 1], fence[:, 4, 1:CH], ALU.add))
            order(nc.vector.memset(fence[:, 6, CH - 1:CH], -BIG))
            order(tt(fence[:, 6, 0:CH - 1], fence[:, 4, 1:CH], fence[:, 5, 0:CH - 1], ALU.add))
            order(scan(fence[:, 7, ::-1], fence[:, 6, ::-1], fence[:, 1, ::-1], -BIG, ALU.add, ALU.max))
            tt(fence[:, 9, 0:CH - 1], fence[:, 7, 1:CH], fence[:, 4, 1:CH], ALU.add).then_inc(carry_ready, 1)
            dve.wait_ge(fence_in, 32)
            order(scan(sc_f, m_fwd, sc_a, ends[:, 4:5], ALU.add, ALU.max))
            order(scan(sc_f[:, ::-1], m_bwd, sc_f[:, ::-1], ends[:, 5:6], ALU.add, ALU.max))
            tt(sc_a, sc_a, sc_f, ALU.subtract).then_inc(shifted, 1)

            dve.wait_ge(back, CT)
            order(nc.vector.memset(region_x[0:T, :], 0.0))
            order.reset()

            def add(k, s, reg):
                j = dve.snap(reg, min_val=0, max_val=NT - 1)
                dve.wait_ge(sum_done, k + 1)
                wait(dve, acc_done, k)
                to = acc[:, bass.ds(j, 1), :].rearrange("p o f -> p (o f)")
                tt(to, to, psum[0:T, 4 + s % 2, 0:PV], ALU.add).then_inc(acc_done, 1)

            def d_body(it):
                dve.load(regs, walk[0:1, 1, bass.ds(it * SU + LAGQ - LAG, SU)])
                for s in range(SU):
                    k = it * SU + s
                    dve.wait_ge(meta_ready, k + 1)
                    wait(dve, sum_done, k - RA + 1)
                    for w in range(2):
                        ts(hot[:, s % RA, w, :], iota[:, :], jb_all[:, bass.ds(k, 1)], pv[:, s, w, D + H:D + H + 1], ALU.add, ALU.is_equal)
                    dve.wait_ge(v_in[s], it * 32 + 32)
                    tt(pv[:, s, :, 0:D].rearrange("p w (h c) -> p w h c", h=H), vg[:, s].rearrange("p w (h c) -> p w h c", h=H),
                       pv[:, s, :, D:PV].unsqueeze(3).broadcast_to((T, 2, H, C)), ALU.mult).then_inc(pv_ready, 1)
                    if s >= LAG or not (isinstance(it, int) and it == 0):
                        add(k - LAG, s, regs[s])

            d_body(0)
            with dve.Fori(1, SI) as it:
                d_body(it)
            dve.load(regs, walk[0:1, 1, STEPS + LAGQ - LAG:STEPS + LAGQ - LAG + SU])
            for s in range(LAG):
                add(STEPS - LAG + s, s, regs[s])

            dve.wait_ge(acc_done, STEPS)

            def residual(b, u):
                dve.wait_ge(f_in[u], (b // 2 + 1) * 16 if isinstance(b, int) else (b - u) * 8 + 16)
                wait(dve, f_t, b)
                both = acc[:, bass.ds(b * 2, 2), :]
                rs = fsm[:, u, 16:32].rearrange("p (t h) -> p t h", t=2)
                order(ts(rs, both[:, :, D:PV], S_EPS, None, ALU.add))
                order(nc.vector.reciprocal(rs, rs))
                for t in range(2):
                    one = acc[:, bass.ds(b * 2 + t, 1), :].rearrange("p o f -> p (o f)")
                    i = tt(fgn[:, t, :].rearrange("p (h c) -> p h c", h=H), one[:, 0:D].rearrange("p (h c) -> p h c", h=H),
                           rs[:, t, :].unsqueeze(2).broadcast_to((T, H, C)), ALU.mult)
                order(i)
                order(tt(fx2[:, u], fgn, fres[:, u], ALU.add))
                norm_stats(fx2[:, u])

            def residual_norm(b, u):
                norm_apply(fx2[:, u], fxn).then_inc(f_xn, 1)

            def lower_x(b, u):
                dve.wait_ge(f_xh, b + 1)
                tt(fxl[:, u].rearrange("p c n -> p (c n)"), psum[:, 6, 0:2 * BN],
                   fxh[:, u].rearrange("p c n -> p (c n)").bitcast(F32), ALU.subtract).then_inc(f_tc, 1)

            def lower_weights(e):
                for i in range(3):
                    dve.wait_ge(f_wh, 1 + e * 3 + i + 1)
                    tt(wxl[i][:, e].rearrange("p c n -> p (c n)"), wx[i][:, e].rearrange("p c n -> p (c n)"),
                       wxh[i][:, e].rearrange("p c n -> p (c n)").bitcast(F32), ALU.subtract).then_inc(f_wl, 1)

            def lower(upper_ready, ready, used, up, low, layer, b, e):
                n = b * NX + e
                dve.wait_ge(upper_ready, n + 1)
                wait(dve, used, n - 1)
                tt(low[:, e % 2].rearrange("p c n -> p (c n)"), fh[:, layer].rearrange("p c n -> p (c n)"),
                   up[:, e % 2].rearrange("p c n -> p (c n)").bitcast(F32), ALU.subtract).then_inc(ready, 1)

            logits = [fsm[:, u, 0:16].rearrange("p (t e) -> p t e", t=2) for u in range(2)]
            mx = stats[:, :, 12:13]

            def router(b, u):
                dve.wait_ge(f_lg, b + 1)
                lg = logits[u]
                order(tt(lg, psum[0:T, 7, 0:16].rearrange("p (t e) -> p t e", t=2),
                         rows[:, R_BR:R_BR + NX].unsqueeze(1).broadcast_to((T, 2, NX)), ALU.add))
                order(nc.vector.tensor_reduce(mx, lg, AX, ALU.max))
                tt(lg, lg, mx.broadcast_to((T, 2, NX)), ALU.subtract).then_inc(f_sm, 1)

            def gates(b, u):
                dve.wait_ge(f_ex, b + 1)
                order(nc.vector.tensor_reduce(mx, logits[u], AX, ALU.add))
                order(nc.vector.reciprocal(mx, mx))
                signal(tt(fw[:, u], logits[u], mx.broadcast_to((T, 2, NX)), ALU.mult), f_w, b + 1)

            def bias_out(b, u):
                dve.wait_ge(f_bo_done, b + 1)
                if not (isinstance(b, int) and b < 2):
                    dve.wait_ge(f_stored[u], (b - u) * 8)
                signal(tt(fyb[:, u], psum[0:T, 7, :].rearrange("p (t d) -> p t d", t=2), fx2[:, u], ALU.add), f_bo, b + 1)

            def gate(b, u, e):
                n = b * NX + e
                dve.wait_ge(f_y, n + 1)
                for t in range(2):
                    i = stt(fyb[:, u, t, :], psum[0:T, 4 + e % 2, t * D:(t + 1) * D], fw[:, u, t, e:e + 1], fyb[:, u, t, :],
                            ALU.mult, ALU.add)
                signal(i, f_ya, n + 1)

            def e_body(b, u, last_block=False):
                router(b, u)
                for e in range(NX + 2):
                    if isinstance(b, int) and b == 0 and 1 <= e < NX:
                        lower_weights(e)
                    if e < NX:
                        lower(f_r1h, f_r1, f_h2, fh1h, fh1l, 0, b, e)
                    if e == 0:
                        gates(b, u)
                    if 1 <= e <= NX:
                        lower(f_r2h, f_r2, f_y, fh2h, fh2l, 1, b, e - 1)
                    if e == 2:
                        bias_out(b, u)
                    if e >= 2:
                        gate(b, u, e - 2)
                    if not last_block:
                        if e == 2:
                            residual(b + 1, 1 - u)
                        elif e == 3:
                            root_start(var, LN_EPS, root)
                            root_step(var, root, scratch)
                        elif e == 4:
                            root_step(var, root, scratch)
                            root_step(var, root, scratch)
                        elif e == 5:
                            residual_norm(b + 1, 1 - u)
                        elif e == 8:
                            lower_x(b + 1, 1 - u)
                order(nc.vector.memset(ksum[:, 0:1], 0.0))
                dve.sem_inc(f_outr, 1)

            residual(0, 0)
            rsqrt(var, LN_EPS, root, scratch)
            residual_norm(0, 0)
            dve.wait_ge(f_wh, 1)
            tt(wr_l[:, :, :], wr[:, :, :], wr_h[:, :, :].bitcast(F32), ALU.subtract).then_inc(f_wl, 1)
            lower_weights(0)
            lower_x(0, 0)
            e_body(0, 0)
            e_body(1, 1)
            order.reset()
            with dve.Fori(1, NB // 2) as it:
                e_body(it * 2, 0)
                e_body(it * 2 + 1, 1)
                order.reset()
            e_body(NB - 1, 0, last_block=True)


_OUT = (N, D)


def kernel(**inputs):
    import concourse.bacc as bacc
    from concourse.bass_utils import run_bass_kernel_spmd

    g = {k: np.asarray(v) for k, v in inputs.items()}

    def gnn(n):
        return g["L0_gnn_" + n]

    def mix(n):
        return g["L0_mix_" + n]

    def ffn(n):
        return g["L0_ffn_" + n]

    def columns(v):
        return np.ascontiguousarray(v.reshape(-1, 128).T)

    row = np.concatenate([gnn("bskip"), gnn("bq"), gnn("bk"), gnn("bv"), mix("bk"), mix("bv"), mix("bo"), mix("b2"),
                          mix("ln1_g"), mix("ln1_b"), mix("ln2_g"), mix("ln2_b"), ffn("br")])
    dst = g["dst"].astype(np.int32, copy=False)
    src = g["src"].astype(np.int32, copy=False)

    def by_tile(v):
        return v.reshape(ET, T).T

    arrays = {
        "x": g["x"],
        "dst": dst,
        "src_t": by_tile(src),
        "dst_t": by_tile(dst),
        "dst_last": dst.reshape(EP, E2)[:, E2 - 1].reshape(1, EP),
        "attr_p": g["edge_attr_64"].reshape(EP, 2, T, ED).transpose(1, 3, 0, 2).reshape(2 * ED, EP * T),
        "w_gnn": np.concatenate([gnn("Wskip").T, gnn("Wq").T, gnn("Wk").T, gnn("Wv").T], 1),
        "w_e": np.ascontiguousarray(gnn("We").T),
        "w_mkv": np.concatenate([mix("Wk"), mix("Wv")], 1),
        "w_mq": mix("Wq"), "w_mo": mix("Wo"), "w_m1": mix("W1"), "w_m2": mix("W2"),
        "w_x1": ffn("W1").reshape(NX * D, D), "w_x2": ffn("W2").reshape(NX * D, D), "w_xo": ffn("Wo").reshape(NX * D, D),
        "w_r": ffn("Wr"), "bo_e": ffn("bo"),
        "rows": np.ascontiguousarray(np.broadcast_to(row, (T, ROWS))),
        "cols": np.concatenate([columns(mix("bq")), columns(mix("b1")), columns(mix("ln1_g")), columns(mix("ln1_b"))]
                               + [columns(ffn(n + i)) for i in "12" for n in ("b", "g", "be", "m", "v")], 1),
        "ident": np.eye(128, dtype=np.float32),
        "blockm": np.kron(np.eye(128 // C, dtype=np.float32), np.ones((C, C), np.float32)),
        "iota": np.ascontiguousarray(np.broadcast_to(np.arange(T, dtype=np.float32), (T, T))),
    }
    arrays = {k: np.ascontiguousarray(v) for k, v in arrays.items()}
    from concourse import mybir as _mybir

    nc = bacc.Bacc("TRN2", target_bir_lowering=False, num_devices=1)
    aps = {n: nc.dram_tensor("in_" + n, v.shape, _mybir.dt.from_np(v.dtype), kind="ExternalInput").ap()
           for n, v in arrays.items()}
    out = nc.dram_tensor("out_0", _OUT, F32, kind="ExternalOutput").ap()
    build(nc, aps, out)
    r = run_bass_kernel_spmd(nc, [{"in_" + n: v for n, v in arrays.items()}], core_ids=[0])
    return r.results[0]["out_0"]
```

```python
from contextlib import ExitStack

import numpy as np

import concourse.bass as bass
from concourse import mybir

F32 = mybir.dt.float32
I32 = mybir.dt.int32
F32R = mybir.dt.float32r
ALU = mybir.AluOpType
ACT = mybir.ActivationFunctionType
AX = mybir.AxisListType.X

N, E_, D, ED = 6250, 100000, 256, 64
H, C = 8, 32
T = 125
NT, ET = N // T, E_ // T
BN = 2 * T
NB = N // BN
FF = 1024
NX = 8
LN_EPS, BN_EPS, Z_EPS, S_EPS = 1e-5, 1e-3, 1e-6, 1e-16
EP, E2 = ET // 2, 2 * T
SB = 18
STEPS = NB * SB
SU = 6
SI = STEPS // SU
assert STEPS >= EP + NT - 1 and SB % SU == 0
RK, R, RA, RP = 9, 6, 3, 6
CH = 16
CE = E_ // CH
CT = ET // CH
RW = H + 2
PV = D + H
LAGD = 3
LAGW = LAGD + 3
LAGQ = 5
LAGP = 2
AHEAD_UP = 4
AHEAD_LOW = LAGQ + 3
LAG = 2
KV = 128 + H // 2
LAGS = 4
WALK = STEPS + LAGQ + SU
BIG = 1.0e30
SCALE = float(C) ** -0.5
R_GNN, R_MKV, R_BO, R_B2, R_G1, R_E1, R_G2, R_E2, R_BR = 0, 1024, 1536, 1792, 2048, 2304, 2560, 2816, 3072
ROWS = 3080
C_BQ, C_B1, C_G1, C_E1, C_FF = 0, 2, 10, 12, 14
COLS = C_FF + 10 * 16


def wait(eng, sem, value):
    if isinstance(value, int) and value <= 0:
        return
    eng.wait_ge(sem, value)


class Order:

    def __init__(self, eng, sem):
        self.eng, self.sem, self.n = eng, sem, 0

    def __call__(self, ins):
        self.n += 1
        ins.then_inc(self.sem, 1)
        self.eng.wait_ge(self.sem, self.n)

    def reset(self):
        self.eng.sem_clear(self.sem)
        self.n = 0


def build(nc, a, out):
    ctx = ExitStack()
    with ctx:
        def sb(name, shape, dt=F32):
            return ctx.enter_context(nc.sbuf_tensor(name, shape, dt))

        def sem(name):
            return ctx.enter_context(nc.semaphore(name))

        def dram(name, shape, dt=F32):
            return nc.dram_tensor(name, shape, dt).ap()

        k_tab, v_tab = dram("k_tab", (N, D)), dram("v_tab", (N, D))
        xn_d, xnt_d = dram("xn_d", (N, D)), dram("xnt_d", (2, 128, N))
        skip_d, res_d = dram("skip_d", (N, D)), dram("res_d", (N, D))
        walk_d, jb_d = dram("walk_d", (3, STEPS), I32), dram("jb_d", (SI, SU))
        fence_d = dram("fence_d", (4, 128))

        region_x = sb("region_x", [128, NT * PV])
        early = ExitStack()
        with early:
            weights = early.enter_context(nc.sbuf_tensor("weights", [128, 12288], F32))
            region_r = early.enter_context(nc.sbuf_tensor("region_r", [128, ET * (RW + 2) + ROWS], F32))
            region_s = early.enter_context(nc.sbuf_tensor("region_s", [128, 11400], F32))
        wx_low = sb("wx_low", [128, 12288], F32R)
        wx_up = sb("wx_up", [128, 12288], F32R)
        sb("rows_tail", [128, ET * (RW + 2) + ROWS - 12288])
        parts_x = sb("parts_x", [128, 2, 2, 2, BN], F32R)
        parts_h = sb("parts_h", [128, 4, 2, 2, BN], F32R)
        sb("region_s_tail", [128, 11400 - 12 * 2 * BN])
        rec = region_r[0:T, 0:ET * RW].rearrange("p (e m) -> p e m", m=RW)
        src_t = region_r[0:T, ET * RW:ET * (RW + 1)].bitcast(I32)
        dst_t = region_r[0:T, ET * (RW + 1):ET * (RW + 2)].bitcast(I32)
        rows = region_r[0:T, ET * (RW + 2):ET * (RW + 2) + ROWS]
        cols = sb("cols", [128, COLS])
        bns = sb("bns", [128, 2, 2, 16])
        ident = sb("ident", [128, 128])
        blockm = sb("blockm", [128, 128])
        iota = sb("iota", [T, T])
        we = sb("we", [2 * ED, D])
        idx = sb("idx", [T, RK, 2], I32)
        part = sb("part", [T, 3, 2 * H])
        node = sb("node", [T, 1])
        node_i = sb("node_i", [T, 1], I32)
        walk_i = sb("walk_i", [SI, 3, SU], I32)
        walk_s = sb("walk_s", [SI, 6, SU])
        kvbd = sb("kvbd", [128, 2, KV])
        wr = sb("wr", [128, 2, NX])
        wr_h, wr_l = sb("wr_h", [128, 2, NX], F32R), sb("wr_l", [128, 2, NX], F32R)
        bo_e = sb("bo_e", [NX, D])
        ends = sb("ends", [128, 8])
        fence = sb("fence", [H, 10, CH])
        stats = sb("stats", [T, 2, 16])
        ksum = sb("ksum", [128, 2])
        fsm = sb("fsm", [T, 2, 32])

        wcat = weights[:, 0:2048].rearrange("p (c n) -> p c n", c=2)
        wmkv = weights[:, 2048:3072].rearrange("p (c n) -> p c n", c=2)
        wcat_p, wmkv_p = ([wx_low[:, at + 3072 * i:at + 3072 * i + size].rearrange("p (c n) -> p c n", c=2) for i in (1, 2)]
                          for at, size in ((0, 2048), (2048, 1024)))
        xnt_h, xnt_l = (wx_low[:, 9216 + i * 4 * T:9216 + (i + 1) * 4 * T].rearrange("p (u c n) -> p u c n", u=2, c=2)
                        for i in range(2))
        wmq = weights[:, 3072:3584].rearrange("p (c n) -> p c n", c=2)
        wmo = weights[:, 3584:4096].rearrange("p (c n) -> p c n", c=2)
        wm1 = weights[:, 4096:6144].rearrange("p (c n) -> p c n", c=2)
        wm2 = weights[:, 6144:8192].rearrange("p (c n) -> p c n", c=8)
        wx = [weights[:, 4096 * i:4096 * (i + 1)].rearrange("p (e c n) -> p e c n", e=NX, c=2) for i in range(3)]

        assert 3 * 4096 <= ET * (RW + 2) + R_BR
        wxh, wxl = ([w[:, 4096 * i:4096 * (i + 1)].rearrange("p (e c n) -> p e c n", e=NX, c=2) for i in range(3)]
                    for w in (wx_up, wx_low))

        used = [0]

        def carve(start, *shape, parts=128):
            size = int(np.prod(shape))
            if start is not None:
                used[0] = start
            at = used[0]
            used[0] += size
            assert used[0] <= 11400, used
            flat = region_s[0:parts, at:at + size]
            if len(shape) == 1:
                return flat
            names = "abcd"[:len(shape)]
            return flat.rearrange(f"p ({' '.join(names)}) -> p {' '.join(names)}",
                                  **{n: s for n, s in zip(names[:-1], shape[:-1])})

        skip_row = rows[:, R_GNN:R_GNN + D]
        x_all = region_x[0:T, 0:NT * D].rearrange("p (t d) -> p t d", t=NT)
        xstat = sb("xstat", [T, NT, 4])
        xsix = sb("xsix", [T, 10, 6])
        xn = carve(0, 2, D, parts=T)
        xnt = carve(None, 2, 2, T)
        kv = carve(None, 2, 2 * D, parts=T)
        xnb = carve(None, 2, D, parts=T)
        skp = carve(None, 2, D, parts=T)
        kt = carve(None, 2, D, parts=T)
        krelu = carve(None, 2, D, parts=T)
        kexp = carve(None, 2, D, parts=T)
        kphi = carve(None, 2, D, parts=T)
        vone = carve(None, 2, 2, 129, parts=T)
        zero = carve(None, 129)
        assert used[0] <= 8200
        mxt = carve(0, 2, 2, BN)
        mres = carve(None, 2, D, parts=T)
        mq, mqe, mqp = (carve(None, 2, BN) for _ in range(3))
        mat = carve(None, 2, BN)
        mx1 = carve(None, 2, D, parts=T)
        mx1t = carve(None, 2, BN)
        mh = carve(None, 8, BN)
        my = carve(None, 2, 2, D, parts=T)
        mout = sb("mout", [T, 2, D])
        mx2 = sb("mx2", [T, 2, D])
        rec_tail = rec[:, :, :].rearrange("p e m -> p (e m)")[:, ET * H:ET * RW]
        mxn = rec_tail[:, 0:4 * D].rearrange("p (u t d) -> p u t d", u=2, t=2)
        matn = rec_tail[:, 4 * D:6 * D].rearrange("p (t d) -> p t d", t=2)
        mden = rec_tail[:, 6 * D:6 * D + 4 * H].rearrange("p (o t h) -> p o t h", o=2, t=2)
        assert used[0] <= 8200
        wf, wl = region_s[0:SI, 8200:8200 + EP], region_s[0:SI, 8600:8600 + EP]
        wz, wi = region_s[0:SI, 9000:9000 + EP].bitcast(I32), region_s[0:SI, 9400:9400 + EP].bitcast(I32)
        walk_k = sb("walk_k", [SI, 2 * SU], I32)
        dstb = carve(8200, RA, E2, parts=T).bitcast(I32)
        jb_all = carve(None, STEPS, parts=T)
        jneg = carve(None, STEPS, parts=T)
        walk = carve(None, 3, WALK, parts=1).bitcast(I32)
        q_all = x_all
        tail = weights[:, 8192:12288]
        kg_a = tail[0:T, 0:6 * 2 * D].rearrange("p (r w d) -> p r w d", r=6, w=2)
        kg_b = rows[:, 0:3 * 2 * D].rearrange("p (r w d) -> p r w d", r=3, w=2)
        kg = [kg_a[:, r] for r in range(6)] + [kg_b[:, r] for r in range(3)]
        att_b = weights[:, 0:RA * E2].rearrange("p (r t) -> p r t", r=RA)
        att_parts = wx_low[:, RA * E2:(RA + RP) * E2].rearrange("p (r t) -> p r t", r=RP)
        we_h, we_l = (wx_low[:, (RA + RP) * E2 + i * D:(RA + RP) * E2 + (i + 1) * D] for i in range(2))
        assert (RA + RP) * E2 + 2 * D <= 3072
        hott = tail[0:T, 3072:3072 + RA * E2].rearrange("p (r n) -> p r n", r=RA)
        scores = rec[:, :, :].rearrange("p e m -> p (e m)")[:, 0:ET * H]
        sc_a = region_x[:, 0:CE]
        sc_m = region_x[:, CE:2 * CE + 1]
        sc_f = region_s[:, 0:CE]
        CUT = 3072
        sc_d = [weights[:, 0:CUT].bitcast(I32), weights[:, 8192:8192 + CE - CUT + 1].bitcast(I32)]
        acc = region_x[0:T, :].rearrange("p (t f) -> p t f", t=NT)
        vg = carve(0, R, 2, D, parts=T)
        pv = carve(None, R, 2, D + RW, parts=T)
        hot = carve(None, RA, 2, T, parts=T)
        att_d = carve(None, RA, E2)
        assert used[0] <= 8200
        fres = carve(12 * 2 * BN, 2, 2, D, parts=T)
        fgn = fxn = carve(None, 2, D, parts=T)
        fx2 = carve(None, 2, 2, D, parts=T)
        fxh, fxl = (parts_x[:, i] for i in range(2))
        fh = carve(None, 2, 2, BN)
        fh1h, fh1l, fh2h, fh2l = (parts_h[:, i] for i in range(4))
        fw = carve(None, 2, 2, NX, parts=T)
        fwt = carve(None, 2, BN, parts=NX)
        fyb = carve(None, 2, 2, D, parts=T)

        psum = ctx.enter_context(nc.psum_tensor("psum", [128, 8, 512], F32))

        c_a, c_b, c_ff, c_walk = sem("const_a"), sem("const_b"), sem("const_ff"), sem("const_walk")
        dve_o, act_o, pool_o = sem("dve_order"), sem("act_order"), sem("pool_order")
        bn_ready = sem("bn_ready")
        x_in = [sem(f"x_in{i}") for i in range(5)]
        a_stored = [sem(f"a_stored{u}") for u in range(2)]
        xn_ready, xn_turned, xnt_ready, xnb_ready = sem("xn_ready"), sem("xn_turned"), sem("xnt_ready"), sem("xnb_ready")
        sq_done, kv_done, mkv_done, sq_read, gnn_out = sem("sq_done"), sem("kv_done"), sem("mkv_done"), sem("sq_read"), sem("gnn_out")
        kt_ready, kexp_ready, kphi_ready, state_done = sem("kt_ready"), sem("kexp_ready"), sem("kphi_ready"), sem("state_done")
        wa_up, wa_low, xnt_low = sem("wa_up"), sem("wa_low"), sem("xnt_low")
        zero_ready, state_ready, skip_row_ready = sem("zero_ready"), sem("state_ready"), sem("skip_row_ready")
        m_in = [sem(f"m_in{u}") for u in range(2)]
        m_xn_in = [sem(f"m_xn_in{u}") for u in range(2)]
        m_q, m_exp, m_phi = sem("m_q"), sem("m_exp"), sem("m_phi")
        m_nd, m_an, m_att, m_at, m_o, m_x1 = sem("m_nd"), sem("m_an"), sem("m_att"), sem("m_at"), sem("m_o"), sem("m_x1")
        m_t, m_tc, m_h, m_hr, m_y, m_outr = sem("m_t"), sem("m_tc"), sem("m_h"), sem("m_hr"), sem("m_y"), sem("m_outr")
        m_stored, m_y_read, m_res_in = sem("m_stored"), sem("m_y_read"), sem("m_res_in")
        gather_go = sem("gather_go")
        gathered = [sem(f"gathered{r}") for r in range(RK)]
        att_in = [sem(f"att_in{r}") for r in range(RA)]
        dstb_in = [sem(f"dstb_in{r}") for r in range(RA)]
        jneg_ready, we_parts = sem("jneg_ready"), sem("we_parts")
        att_up, att_low = sem("att_up"), sem("att_low")
        e_done, e_copied, hott_ready, q_done, mult_done, red_done, score_done = (
            sem("e_done"), sem("e_copied"), sem("hott_ready"), sem("q_done"), sem("mult_done"), sem("red_done"), sem("score_done"))
        turned, turned_out = sem("turned"), sem("turned_out")
        dst_in, mask_ready = sem("dst_in"), sem("mask_ready")
        fence_out, fence_in = sem("fence_out"), sem("fence_in")
        ends_ready, carry_ready, shifted, exped, back, back_out = (
            sem("ends_ready"), sem("carry_ready"), sem("shifted"), sem("exped"), sem("back"), sem("back_out"))
        last_in, walk_steps, walk_ready, walk_out, walk_in = (
            sem("last_in"), sem("walk_steps"), sem("walk_ready"), sem("walk_out"), sem("walk_in"))
        rec_ready, walk_clear = sem("rec_ready"), sem("walk_clear")
        att_zero, acc_zero = sem("att_zero"), sem("acc_zero")
        meta_ready = sem("meta_ready")
        v_in = [sem(f"v_in{r}") for r in range(R)]
        attv_in = [sem(f"attv_in{r}") for r in range(RA)]
        ev_done, pv_ready, sum_done, acc_done = sem("ev_done"), sem("pv_ready"), sem("sum_done"), sem("acc_done")
        f_in = [sem(f"f_in{u}") for u in range(2)]
        f_xn, f_t, f_tc, f_lg, f_sm, f_ex, f_w = sem("f_xn"), sem("f_t"), sem("f_tc"), sem("f_lg"), sem("f_sm"), sem("f_ex"), sem("f_w")
        f_wt, f_wtc, f_h1, f_r1, f_h2, f_r2, f_y, f_ya = (
            sem("f_wt"), sem("f_wtc"), sem("f_h1"), sem("f_r1"), sem("f_h2"), sem("f_r2"), sem("f_y"), sem("f_ya"))
        f_bo, f_bo_done, f_outr = sem("f_bo"), sem("f_bo_done"), sem("f_outr")
        f_wh, f_wl, f_xh, f_r1h, f_r2h = sem("f_wh"), sem("f_wl"), sem("f_xh"), sem("f_r1h"), sem("f_r2h")
        f_stored = [sem(f"f_stored{u}") for u in range(2)]

        CONST_A, CONST_B = 16 * 6, 16 * 9

        block = ctx.enter_context(nc.Block())

        def node_rows(t_expr, k=1):
            return bass.ds(t_expr * T, k * T)

        def tile_pair(ref, place):
            return ref[:, bass.ds(place, 2, CH), :]

        def before(b, e, d):
            if e >= d:
                return b, e - d
            return None if isinstance(b, int) and b == 0 else (b - 1, e - d + NX)

        def store_mix(eng, b):
            eng.wait_ge(m_outr, b + 1)
            eng.dma_start(res_d[bass.ds(b * BN, BN), :].rearrange("(t p) d -> p t d", p=T), mout[:, :, :]).then_inc(m_stored, 16)

        def twice(eng, n, body, order=()):
            body(0, 0)
            body(1, 1)
            for o in order:
                o.reset()
            with eng.Fori(1, n // 2) as it:
                body(it * 2, 0)
                body(it * 2 + 1, 1)
                for o in order:
                    o.reset()
            if n % 2:
                body(n - 1, 0)
                for o in order:
                    o.reset()

        @block.sync
        def _(sp):
            for i in range(5):
                sp.dma_start(x_all[:, i * 10:(i + 1) * 10, :],
                             a["x"][i * 10 * T:(i + 1) * 10 * T, :].rearrange("(t p) d -> p t d", p=T)).then_inc(x_in[i], 16)
            sp.dma_start(ident[:, :], a["ident"]).then_inc(c_a, 16)
            sp.dma_start(wcat, a["w_gnn"].rearrange("(c p) n -> p c n", p=128)).then_inc(c_a, 16)
            sp.dma_start(wmkv, a["w_mkv"].rearrange("(c p) n -> p c n", p=128)).then_inc(c_a, 16)
            sp.dma_start(rows[:, :], a["rows"]).then_inc(c_a, 16)
            sp.dma_start(cols[:, :], a["cols"]).then_inc(c_a, 16)
            sp.dma_start(blockm[:, :], a["blockm"]).then_inc(c_a, 16)

            sp.wait_ge(walk_ready, 1)
            sp.dma_start(walk_d.rearrange("w (i s) -> i w s", s=SU), walk_i[:, :, :]).then_inc(walk_out, 16)
            sp.dma_start(jb_d, walk_s[:, 3, :]).then_inc(walk_out, 16)
            sp.wait_ge(walk_clear, 1)
            sp.wait_ge(walk_out, 32)
            sp.dma_start(walk[0:1, 0, LAGW:LAGW + STEPS], walk_d[0:1, :]).then_inc(walk_in, 16)
            sp.dma_start(walk[0:1, 1, LAGQ:LAGQ + STEPS], walk_d[1:2, :]).then_inc(walk_in, 16)
            sp.dma_start(walk[0:1, 2, LAGP:LAGP + STEPS], walk_d[2:3, :]).then_inc(walk_in, 16)
            with nc.allow_non_contiguous_dma(reason="one row to every partition"):
                sp.dma_start(jb_all, jb_d.rearrange("i s -> (i s)").partition_broadcast(T)).then_inc(walk_in, 16)

            def store_a(t, u):
                sp.wait_ge(xnt_ready, t + 1)
                sp.wait_ge(xnb_ready, t + 1)
                sp.dma_start(xn_d[node_rows(t), :], xnb[:, u, :]).then_inc(a_stored[u], 16)
                sp.dma_start(xnt_d[:, :, node_rows(t)].rearrange("c p n -> p c n"), xnt[:, u]).then_inc(a_stored[u], 16)
                sp.wait_ge(gnn_out, t + 1)
                for i, tab in enumerate((k_tab, v_tab)):
                    sp.dma_start(tab[node_rows(t), :], kv[:, u, i * D:(i + 1) * D]).then_inc(a_stored[u], 16)
                sp.dma_start(skip_d[node_rows(t), :], skp[:, u, :]).then_inc(a_stored[u], 16)

            twice(sp, NT, store_a)

            sp.wait_ge(mkv_done, NT)
            sp.dma_start(wmq, a["w_mq"].rearrange("(c p) n -> p c n", p=128)).then_inc(c_b, 16)
            sp.dma_start(wmo, a["w_mo"].rearrange("(c p) n -> p c n", p=128)).then_inc(c_b, 16)
            sp.dma_start(wm1, a["w_m1"].rearrange("(c p) n -> p c n", p=128)).then_inc(c_b, 16)
            sp.dma_start(wm2, a["w_m2"].rearrange("(c p) n -> p c n", p=128)).then_inc(c_b, 16)
            for half in range(2):
                sp.dma_start(we[half * ED:(half + 1) * ED, :], a["w_e"]).then_inc(c_b, 16)
            sp.dma_start(iota[:, :], a["iota"]).then_inc(c_b, 16)
            sp.dma_start(wr[:, :, :], a["w_r"].rearrange("(c p) n -> p c n", p=128)).then_inc(c_b, 16)
            sp.dma_start(bo_e[:, :], a["bo_e"]).then_inc(c_b, 16)

            for u in range(2):
                sp.wait_ge(a_stored[u], 16 * 5 * (NT // 2))
            sp.wait_ge(state_ready, 1)

            def load_mix(b, u):
                wait(sp, m_x1, b - 1)
                sp.dma_start(mxt[:, u], xnt_d[:, :, bass.ds(b * BN, BN)].rearrange("c p n -> p c n")).then_inc(m_in[u], 16)

            def load_xn(b, u):
                wait(sp, m_x1, b - 1)
                sp.dma_start(mxn[:, u], xn_d[bass.ds(b * BN, BN), :].rearrange("(t p) d -> p t d", p=T)).then_inc(m_xn_in[u], 16)

            def load_skip(b):
                wait(sp, m_outr, b)
                sp.dma_start(mres[:, :, :], skip_d[bass.ds(b * BN, BN), :].rearrange("(t p) d -> p t d", p=T)).then_inc(m_res_in, 16)

            dst_all = a["dst"]
            sp.wait_ge(walk_in, 64)
            regs = [sp.alloc_register(f"sp_pair{s}") for s in range(SU)]

            late = [sp.alloc_register(f"sp_late{s}") for s in range(SU)]

            def load_dst(k, ra, reg):
                i = sp.snap(reg, min_val=0, max_val=EP - 1)
                wait(sp, hott_ready, k - RA + 1)
                sp.dma_start(dstb[:, ra, :], dst_all[bass.ds(i * E2, E2)].partition_broadcast(T)).then_inc(dstb_in[ra], 16)

            def b_body(b, u):
                load_mix(b, u)
                for s in range(SB):
                    k, ra = b * SB + s, s % RA
                    if s % SU == 0:
                        sp.load(regs, walk[0:1, 0, bass.ds(k + LAGW, SU)])
                        sp.load(late, walk[0:1, 0, bass.ds(k, SU)])
                    i = sp.snap(regs[s % SU], min_val=0, max_val=EP - 1)
                    wait(sp, att_low, k - RA + 1)
                    for half in range(2):
                        sp.dma_start(att_b[half * ED:(half + 1) * ED, ra, :], a["attr_t"][:, bass.ds(i * E2, E2)]).then_inc(att_in[ra], 16)
                    if s >= LAGW or not (isinstance(b, int) and b == 0):
                        load_dst(k - LAGW, (s - LAGW) % RA, late[s % SU])
                    if s == 5:
                        load_xn(b, u)
                    if s == 10 and not (isinstance(b, int) and b < 2):
                        load_skip(b - 2)

            with nc.allow_non_contiguous_dma(reason="one row to every partition"):
                twice(sp, NB, b_body)
                sp.load(late, walk[0:1, 0, STEPS:STEPS + SU])
                for s in range(LAGW):
                    load_dst(STEPS - LAGW + s, (STEPS - LAGW + s) % RA, late[s])
            load_skip(NB - 2)
            sp.wait_ge(score_done, STEPS)
            dst_flat = a["dst"].rearrange("(c n) -> c n", c=CH)
            with nc.allow_non_contiguous_dma(reason="replicates dst over the heads"):
                for c in range(CH):
                    for piece, cut in zip(sc_d, (slice(0, CUT), slice(CUT - 1, CE))):
                        sp.dma_start(piece[c * H:(c + 1) * H, :],
                                     dst_flat[c:c + 1, cut].broadcast_to((H, cut.stop - cut.start))).then_inc(dst_in, 16)
                store_mix(sp, NB - 2)
                load_skip(NB - 1)
                store_mix(sp, NB - 1)
                sp.wait_ge(mask_ready, 1)
                sp.wait_ge(m_stored, 16 * NB)
                sp.wait_ge(ends_ready, 1)
                sp.dma_start(fence_d.rearrange("k p -> p k"), ends[:, 0:4]).then_inc(fence_out, 16)
                sp.wait_ge(fence_out, 16)
                sp.dma_start(fence[:, 0:4, :], fence_d.rearrange("k (c h) -> h k c", h=H)).then_inc(fence_in, 16)
                sp.wait_ge(carry_ready, 1)
                sp.dma_start(fence_d[0:2, :].rearrange("k (c h) -> h k c", h=H), fence[:, 8:10, :]).then_inc(fence_out, 16)
                sp.wait_ge(fence_out, 32)
                sp.dma_start(ends[:, 4:6], fence_d[0:2, :].rearrange("k p -> p k")).then_inc(fence_in, 16)
                for i, name in enumerate(("w_x1", "w_x2", "w_xo")):
                    sp.dma_start(wx[i].rearrange("p e c n -> p (e c) n"),
                                 a[name].rearrange("(k p) n -> p k n", p=128)).then_inc(c_ff, 16)

            sp.wait_ge(back_out, CT)

            def d_body(it):
                sp.load(regs, walk[0:1, 0, bass.ds(it * SU + LAGW, SU)])
                for s in range(SU):
                    k, ra = it * SU + s, s % RA
                    i = sp.snap(regs[s], min_val=0, max_val=EP - 1)
                    wait(sp, ev_done, k - RA + 1)
                    sp.dma_start(att_d[0:ED, ra, :], a["attr_t"][:, bass.ds(i * E2, E2)]).then_inc(attv_in[ra], 16)

            d_body(0)
            with sp.Fori(1, SI) as it:
                d_body(it)

            sp.wait_ge(acc_done, STEPS)

            def load_res(b, u):
                if not (isinstance(b, int) and b < 2):
                    sp.wait_ge(f_xn, b - 1)
                sp.dma_start(fres[:, u], res_d[bass.ds(b * BN, BN), :].rearrange("(t p) d -> p t d", p=T)).then_inc(f_in[u], 16)

            def store_out(b, u):
                sp.wait_ge(f_outr, b + 1)
                sp.dma_start(out[bass.ds(b * BN, BN), :].rearrange("(t p) d -> p t d", p=T), fyb[:, u]).then_inc(f_stored[u], 16)

            load_res(0, 0)
            load_res(1, 1)

            def e_body(b, u):
                load_res(b + 2, u)
                store_out(b, u)

            e_body(0, 0)
            e_body(1, 1)
            with sp.Fori(1, (NB - 2) // 2) as it:
                e_body(it * 2, 0)
                e_body(it * 2 + 1, 1)
            e_body(NB - 3, 0)
            store_out(NB - 2, 1)
            store_out(NB - 1, 0)
            sp.wait_ge(f_stored[0], 16 * ((NB + 1) // 2))
            sp.wait_ge(f_stored[1], 16 * (NB // 2))

        @block.gpsimd
        def _(pool):
            pool.dma_start(wz[:, :], a["dst_last"].broadcast_to((SI, EP))).then_inc(last_in, 16)
            nc.gpsimd.iota(wi[:, :], [[T, EP]], base=0, channel_multiplier=0).then_inc(walk_steps, 1)
            nc.gpsimd.iota(walk_k[:, 0:SU], [[T, SU]], base=0, channel_multiplier=T * SU).then_inc(walk_steps, 1)
            nc.gpsimd.iota(walk_k[:, SU:2 * SU], [[1, SU]], base=0, channel_multiplier=SU).then_inc(walk_steps, 1)
            nc.gpsimd.iota(node_i[:, :], [[0, 1]], base=0, channel_multiplier=1).then_inc(walk_steps, 1)
            pool.dma_start(src_t[:, :], a["src_t"]).then_inc(c_walk, 16)
            pool.dma_start(dst_t[:, :], a["dst_t"]).then_inc(c_walk, 16)

            pool.wait_ge(skip_row_ready, 1)

            def a_body(t, u):
                pool.wait_ge(xn_ready, t + 1)
                if not (isinstance(t, int) and t < 2):
                    pool.wait_ge(a_stored[u], (t - u) * 40)
                nc.gpsimd.tensor_tensor(xnb[:, u, :], xn[:, u, :], rows[:, R_BO:R_BO + D], ALU.add)
                x_t = x_all[:, bass.ds(t, 1), :].rearrange("p o d -> p (o d)")
                nc.gpsimd.tensor_tensor(x_t, x_t, skip_row, ALU.add).then_inc(xnb_ready, 1)

            twice(pool, NT, a_body)
            for u in range(2):
                pool.wait_ge(a_stored[u], 16 * 5 * (NT // 2))

            def b_body(b):
                for s in range(SB):
                    k, r = b * SB + s, s % RK
                    pool.wait_ge(e_copied, k + 1)
                    pool.sem_inc(gather_go, 1)
                    for w in range(2):
                        nc.gpsimd.indirect_dma_start(
                            kg[r][:, w, :], None, k_tab, bass.IndirectOffsetOnAxis(idx[:, r, w:w + 1], 0), compute_op=ALU.add
                        ).then_inc(gathered[r], 16)

            b_body(0)
            with pool.Fori(1, NB) as b:
                b_body(b)

            pool.wait_ge(back, CT)
            nc.gpsimd.memset(acc[:, NT // 2:NT, :], 0.0).then_inc(acc_zero, 1)

            def d_body(it):
                for s in range(SU):
                    pool.wait_ge(meta_ready, it * SU + s + 1)
                    pool.sem_inc(gather_go, 1)
                    for w in range(2):
                        nc.gpsimd.indirect_dma_start(
                            vg[:, s, w, :], None, v_tab,
                            bass.IndirectOffsetOnAxis(pv[:, s, w, D + H + 1:D + RW].bitcast(I32), 0), compute_op=ALU.add
                        ).then_inc(v_in[s], 16)

            d_body(0)
            with pool.Fori(1, SI) as it:
                d_body(it)

        @block.tensor
        def _(pe):
            mm, tr = nc.tensor.matmul, nc.tensor.transpose
            pe.wait_ge(c_a, CONST_A)
            pe.wait_ge(zero_ready, 1)
            for c in range(2):
                mm(psum[:, 6 + c, 0:129], zero[:, 0:128], zero[:, :], start=True, stop=False)

            def mm3(to, lhs, rhs, start, stop):
                mm(to, lhs[0], rhs[0], start=start, stop=False)
                mm(to, lhs[0], rhs[1], start=False, stop=False)
                return mm(to, lhs[1], rhs[0], start=False, stop=stop)

            def turn(t, u):
                pe.wait_ge(xn_ready, t + 1)
                wait(pe, xnt_ready, t - 1)
                for c in range(2):
                    last = tr(psum[:, u, c * T:(c + 1) * T], xn[:, u, c * 128:(c + 1) * 128], ident[0:T, 0:T])
                last.then_inc(xn_turned, 1)

            def state(t, u):
                pe.wait_ge(kphi_ready, t + 1)
                for c in range(2):
                    last = mm(psum[:, 6 + c, 0:129], kphi[:, u, c * 128:(c + 1) * 128], vone[:, u, c, :],
                              start=False, stop=False)
                last.then_inc(state_done, 1)

            def a_body(t, u, first=False, last_tile=False):
                pe.wait_ge(xnt_low, t + 1)
                for half, (read, done) in enumerate(((sq_read, sq_done), (gnn_out, kv_done))):
                    wait(pe, read, t)
                    if first:
                        pe.wait_ge(wa_low, half + 1)
                    for c in range(2):
                        last = mm3(psum[0:T, 2 + half, :], [x[:, u, c, :] for x in (xnt_h, xnt_l)],
                                   [w[:, c, half * 512:(half + 1) * 512] for w in wcat_p], c == 0, c == 1)
                    last.then_inc(done, 1)
                    if half == 1 and not last_tile:
                        turn(t + 1, 1 - u)
                wait(pe, kphi_ready, t - 1)
                if first:
                    pe.wait_ge(wa_low, 3)
                for c in range(2):
                    last = mm3(psum[0:T, 4 + u, :], [x[:, u, c, :] for x in (xnt_h, xnt_l)],
                               [w[:, c, :] for w in wmkv_p], c == 0, c == 1)
                last.then_inc(mkv_done, 1)
                if not first:
                    state(t - 1, 1 - u)

            turn(0, 0)
            a_body(0, 0, first=True)
            a_body(1, 1)
            with pe.Fori(1, NT // 2 - 1) as it:
                a_body(it * 2, 0)
                a_body(it * 2 + 1, 1)
            a_body(NT - 2, 0)
            a_body(NT - 1, 1, last_tile=True)
            state(NT - 1, 1)
            for c in range(2):
                last = mm(psum[:, 6 + c, 0:129], zero[:, 0:128], zero[:, :], start=False, stop=True)
            last.then_inc(state_done, 1)

            pe.wait_ge(c_b, CONST_B)
            pe.wait_ge(state_ready, 1)

            def eproj_parts(k, s):
                pe.wait_ge(att_low, k + 1)
                wait(pe, e_copied, k - 1)
                for w in range(2):
                    to = psum[0:T, s % 2, w * D:(w + 1) * D]
                    att = att_parts[:, s % RP, w * T:(w + 1) * T]
                    mm(to, att, we_h[:, :], start=True, stop=False)
                    last = mm(to, att, we_l[:, :], start=False, stop=True)
                last.then_inc(e_done, 1)

            def eproj(k, s, turn_of):
                pe.wait_ge(attv_in[s % RA], turn_of * 16)
                wait(pe, meta_ready, k - 1)
                for w in range(2):
                    last = mm(psum[0:T, s % 2 * 2 + w, 0:D], att_d[:, s % RA, w * T:(w + 1) * T],
                              we[:, :], start=True, stop=True)
                last.then_inc(ev_done, 1)

            def qprod(k, s, reg):
                j = pe.snap(reg, min_val=0, max_val=NT - 1)
                pe.wait_ge(hott_ready, k + 1)
                wait(pe, mult_done, k - 1)
                for w in range(2):
                    last = mm(psum[0:T, 2 + s % 2, w * D:(w + 1) * D], hott[:, s % RA, w * T:(w + 1) * T],
                              q_all[:, bass.ds(j, 1), :].rearrange("p o d -> p (o d)"), start=True, stop=True)
                last.then_inc(q_done, 1)

            def mix(b, u, g):
                kind = g[0]
                if kind == "q":
                    o = g[1]
                    if o == 0:
                        pe.wait_ge(m_in[u], (b // 2 + 1) * 16 if isinstance(b, int) else (b - u) * 8 + 16)
                        wait(pe, m_x1, b)
                    for c in range(2):
                        last = mm(psum[:, 7, o * BN:(o + 1) * BN], wmq[:, c, o * 128:(o + 1) * 128], mxt[:, u, c, :],
                                  start=(c == 0), stop=(c == 1))
                    if o == 1:
                        last.then_inc(m_q, 1)
                elif kind == "attend":
                    pe.wait_ge(m_phi, b + 1)
                    for t in range(2):
                        for c in range(2):
                            last = mm(psum[0:T, 4 + 3 * t, c * KV:(c + 1) * KV], mqp[:, c, t * T:(t + 1) * T], kvbd[:, c, :],
                                      start=True, stop=True)
                    last.then_inc(m_nd, 1)
                elif kind == "turn":
                    pe.wait_ge(m_an, b + 1)
                    for t in range(2):
                        for c in range(2):
                            last = tr(psum[:, 4, c * BN + t * T:c * BN + (t + 1) * T], matn[:, t, c * 128:(c + 1) * 128], ident[0:T, 0:T])
                    last.then_inc(m_att, 1)
                elif kind == "out":
                    t = g[1]
                    if t == 0:
                        pe.wait_ge(m_at, b + 1)
                    for c in range(2):
                        last = mm(psum[0:T, 7, t * D:(t + 1) * D], mat[:, c, t * T:(t + 1) * T], wmo[:, c, :],
                                  start=(c == 0), stop=(c == 1))
                    if t == 1:
                        last.then_inc(m_o, 1)
                elif kind == "turn1":
                    pe.wait_ge(m_x1, b + 1)
                    for t in range(2):
                        for c in range(2):
                            last = tr(psum[:, 4, c * BN + t * T:c * BN + (t + 1) * T], mx1[:, t, c * 128:(c + 1) * 128], ident[0:T, 0:T])
                    last.then_inc(m_t, 1)
                elif kind == "up":
                    n = g[1]
                    pair, o = n // 2, n % 2
                    if n == 0:
                        pe.wait_ge(m_tc, b + 1)
                    if n == 2:
                        wait(pe, m_y_read, b)
                    if o == 0 and pair >= 2:
                        pe.wait_ge(m_hr, b * 4 + pair - 1)
                    for c in range(2):
                        last = mm(psum[:, 5 + pair % 2, o * BN:(o + 1) * BN], wm1[:, c, n * 128:(n + 1) * 128], mx1t[:, c, :],
                                  start=(c == 0), stop=(c == 1))
                    if o == 1:
                        last.then_inc(m_h, 1)
                elif kind == "down":
                    if g[1] == 0:
                        pe.wait_ge(m_hr, b * 4 + 4)
                    for i in range(g[1], g[2]):
                        t, n = i // 8, i % 8
                        last = mm(psum[0:T, 6, t * D:(t + 1) * D], mh[:, n, t * T:(t + 1) * T], wm2[:, n, :],
                                  start=(n == 0), stop=(n == 7))
                    if g[2] == 16:
                        last.then_inc(m_y, 1)

            pe.wait_ge(walk_in, 64)
            pe.wait_ge(we_parts, 2)
            regs = [pe.alloc_register(f"pe_tile{s}") for s in range(SU)]
            mix_at = {0: ("q", 0), 1: ("q", 1), 7: ("attend",), 10: ("turn",), 11: ("out", 0), 12: ("out", 1)}
            late_at = {1: ("turn1",), 2: ("up", 0), 3: ("up", 1), 4: ("up", 2), 5: ("up", 3), 6: ("up", 4), 8: ("up", 5),
                       9: ("up", 6), 10: ("up", 7), 12: ("down", 0, 1), 13: ("down", 1, 4), 14: ("down", 4, 7),
                       15: ("down", 7, 10), 16: ("down", 10, 13), 17: ("down", 13, 16)}

            def b_body(b, u):
                for s in range(SB):
                    k = b * SB + s
                    if s % SU == 0:
                        pe.load(regs, walk[0:1, 1, bass.ds(k, SU)])
                    eproj_parts(k, s)
                    if s >= LAGQ or not (isinstance(b, int) and b == 0):
                        qprod(k - LAGQ, (s - LAGQ) % SB, regs[s % SU])
                    if s in late_at and not (isinstance(b, int) and b == 0):
                        mix(b - 1, 1 - u, late_at[s])
                    if s in mix_at:
                        mix(b, u, mix_at[s])

            twice(pe, NB, b_body)
            pe.load(regs, walk[0:1, 1, STEPS:STEPS + SU])
            for s in range(LAGQ):
                qprod(STEPS - LAGQ + s, SB - LAGQ + s, regs[s])
            for g in late_at.values():
                mix(NB - 1, 0, g)

            pe.wait_ge(score_done, STEPS)
            for bt in range(CT):
                wait(pe, turned_out, bt - 3)
                tr(psum[:, bt % 4, 0:T], scores[:, bt * 128:(bt + 1) * 128], ident[0:T, 0:T]).then_inc(turned, 1)
            pe.wait_ge(exped, 1)
            for bt in range(CT):
                wait(pe, back_out, bt - 3)
                if bt < 4:
                    pe.wait_ge(turned_out, CT)
                tr(psum[0:T, bt % 4, 0:128], sc_a[:, bt * T:(bt + 1) * T], ident[:, :]).then_inc(back, 1)

            pe.wait_ge(back_out, CT)
            pe.wait_ge(att_zero, 1)

            def sums(k, s):
                pe.wait_ge(pv_ready, k + 1)
                bank = psum[0:T, 4 + s % 2, 0:PV]
                wait(pe, acc_done, k - 1)
                for w in range(2):
                    last = mm(bank, hot[:, s % RA, w, :], pv[:, s, w, 0:PV], start=(w == 0), stop=(w == 1))
                last.then_inc(sum_done, 1)

            def d_body(it):
                for s in range(SU):
                    k = it * SU + s
                    eproj(k, s, it * (SU // RA) + s // RA + 1)
                    if s >= LAGS or not (isinstance(it, int) and it == 0):
                        sums(k - LAGS, (s - LAGS) % SU)

            d_body(0)
            with pe.Fori(1, SI) as it:
                d_body(it)
            for s in range(SU - LAGS, SU):
                sums(STEPS - SU + s, s)

            pe.wait_ge(c_ff, 48)
            pe.wait_ge(acc_done, STEPS)

            def prelude(b, u):
                pe.wait_ge(f_xn, b + 1)
                wait(pe, f_tc, b)
                for t in range(2):
                    for c in range(2):
                        last = tr(psum[:, 6, c * BN + t * T:c * BN + (t + 1) * T], fxn[:, t, c * 128:(c + 1) * 128], ident[0:T, 0:T])
                last.then_inc(f_t, 1)

            def split_weights(b, e, i):
                if isinstance(b, int) and b == 0:
                    pe.wait_ge(f_wl, 1 + e * 3 + i + 1)

            def layer1(b, u, e):
                n = b * NX + e
                wait(pe, f_r1h, n - 1)
                split_weights(b, e, 0)
                for o in range(2):
                    for c in range(2):
                        last = mm3(psum[:, e % 2, o * BN:(o + 1) * BN], [w[0][:, e, c, o * 128:(o + 1) * 128] for w in (wxh, wxl)],
                                   [x[:, u, c, :] for x in (fxh, fxl)], c == 0, c == 1)
                last.then_inc(f_h1, 1)

            def layer2(b, e):
                n = b * NX + e
                pe.wait_ge(f_r1, n + 1)
                wait(pe, f_r2h, n - 1)
                split_weights(b, e, 1)
                for o in range(2):
                    for c in range(2):
                        last = mm3(psum[:, 2 + e % 2, o * BN:(o + 1) * BN], [w[1][:, e, c, o * 128:(o + 1) * 128] for w in (wxh, wxl)],
                                   [x[:, e % 2, c, :] for x in (fh1h, fh1l)], c == 0, c == 1)
                last.then_inc(f_h2, 1)

            def layer3(b, e):
                n = b * NX + e
                pe.wait_ge(f_r2, n + 1)
                wait(pe, f_ya, n - 1)
                split_weights(b, e, 2)
                for t in range(2):
                    for c in range(2):
                        last = mm3(psum[0:T, 4 + e % 2, t * D:(t + 1) * D], [x[:, e % 2, c, t * T:(t + 1) * T] for x in (fh2h, fh2l)],
                                   [w[2][:, e, c, :] for w in (wxh, wxl)], c == 0, c == 1)
                last.then_inc(f_y, 1)

            def router(b, u):
                pe.wait_ge(f_tc, b + 1)
                wait(pe, f_bo, b)
                if isinstance(b, int) and b == 0:
                    pe.wait_ge(f_wl, 1)
                for t in range(2):
                    for c in range(2):
                        last = mm3(psum[0:T, 7, t * NX:(t + 1) * NX], [x[:, u, c, t * T:(t + 1) * T] for x in (fxh, fxl)],
                                   [wr_h[:, c, :], wr_l[:, c, :]], c == 0, c == 1)
                last.then_inc(f_lg, 1)

            def weights_t(b, u):
                pe.wait_ge(f_w, b + 1)
                for t in range(2):
                    last = tr(psum[0:NX, 7, 256 + t * T:256 + (t + 1) * T], fw[:, u, t, :], ident[0:T, 0:T])
                last.then_inc(f_wt, 1)

            def bias_out(b, u):
                pe.wait_ge(f_wtc, b + 1)
                for t in range(2):
                    last = mm(psum[0:T, 7, t * D:(t + 1) * D], fwt[:, u, t * T:(t + 1) * T], bo_e[:, :], start=True, stop=True)
                last.then_inc(f_bo_done, 1)

            def e_body(b, u, last_block=False):
                for e in range(NX):
                    layer1(b, u, e)
                    if before(b, e, 1):
                        layer2(*before(b, e, 1))
                    if e == 1:
                        weights_t(b, u)
                    if before(b, e, 2):
                        layer3(*before(b, e, 2))
                    if e == 2:
                        bias_out(b, u)
                    if e == 6 and not last_block:
                        prelude(b + 1, 1 - u)
                    if e == 7 and not last_block:
                        router(b + 1, 1 - u)

            prelude(0, 0)
            router(0, 0)
            e_body(0, 0)
            e_body(1, 1)
            with pe.Fori(1, NB // 2) as it:
                e_body(it * 2, 0)
                e_body(it * 2 + 1, 1)
            e_body(NB - 1, 0, last_block=True)
            layer2(NB - 1, NX - 1)
            layer3(NB - 1, NX - 2)
            layer3(NB - 1, NX - 1)

        @block.scalar
        def _(act):
            copy, fn = nc.scalar.copy, nc.scalar.activation
            order = Order(act, act_o)

            def a_body(t, u):
                act.wait_ge(xn_turned, t + 1)
                wait(act, mkv_done, t - 1)
                if not (isinstance(t, int) and t < 2):
                    act.wait_ge(a_stored[u], (t - u) * 40)
                copy(xnt[:, u].rearrange("p c n -> p (c n)"), psum[:, u, 0:2 * T])
                copy(xnt_h[:, u].rearrange("p c n -> p (c n)"), psum[:, u, 0:2 * T]).then_inc(xnt_ready, 1)
                if not (isinstance(t, int) and t == 0):
                    phi_k(t - 1, 1 - u)

            def phi_k(t, u):
                act.wait_ge(kt_ready, t + 1)
                wait(act, kphi_ready, t - 1)
                fn(krelu[:, u, :], kt[:, u, :], ACT.Relu)
                fn(kexp[:, u, :], kt[:, u, :], ACT.Exp).then_inc(kexp_ready, 1)

            act.wait_ge(c_a, CONST_A)
            for half in range(2):
                cut = slice(half * 512, (half + 1) * 512)
                copy(wcat_p[0][:, :, cut], wcat[:, :, cut]).then_inc(wa_up, 1)
            copy(wmkv_p[0], wmkv).then_inc(wa_up, 1)
            twice(act, NT, a_body)
            phi_k(NT - 1, 1)

            act.wait_ge(state_ready, 1)
            act.wait_ge(c_a, CONST_A)
            act.wait_ge(c_walk, 32)
            act.wait_ge(walk_in, 64)
            act.wait_ge(jneg_ready, 1)
            act.wait_ge(c_b, CONST_B)
            copy(we_h[:, :], we[:, :]).then_inc(we_parts, 1)
            regs = [act.alloc_register(f"act_pair{s}") for s in range(SU)]

            def upper_att(k, s, turn_of):
                act.wait_ge(att_in[s % RA], turn_of * 32)
                wait(act, e_done, k - RP + 1)
                copy(att_parts[:, s % RP, :], att_b[:, s % RA, :]).then_inc(att_up, 1)

            def start_edges(k, s, reg):
                i = act.snap(reg, min_val=0, max_val=EP - 1)
                wait(act, red_done, k - RK + 1)
                copy(idx[:, s % RK, :], src_t[:, bass.ds(i * 2, 2)])
                act.wait_ge(e_done, k + 1)
                copy(kg[s % RK], psum[0:T, s % 2, :].rearrange("p (w d) -> p w d", w=2)).then_inc(e_copied, 1)

            def one_hot(k, s, turn_of):
                act.wait_ge(dstb_in[s % RA], turn_of * 16)
                wait(act, q_done, k - RA + 1)
                order(fn(hott[:, s % RA, :], dstb[:, s % RA, :], ACT.Abs, bias=jneg[:, bass.ds(k, 1)]))
                fn(hott[:, s % RA, :], hott[:, s % RA, :], ACT.Relu, bias=1.0, scale=-1.0).then_inc(hott_ready, 1)

            def mix(b, g):
                if g == "phi":
                    act.wait_ge(m_q, b + 1)
                    for c in range(2):
                        fn(mq[:, c, :], psum[:, 7, c * BN:(c + 1) * BN], ACT.Relu, bias=cols[:, C_BQ + c:C_BQ + c + 1])
                        last = fn(mqe[:, c, :], psum[:, 7, c * BN:(c + 1) * BN], ACT.Exp, bias=cols[:, C_BQ + c:C_BQ + c + 1])
                    last.then_inc(m_exp, 1)
                elif g == "turn":
                    act.wait_ge(m_att, b + 1)
                    copy(mat[:, :, :].rearrange("p c n -> p (c n)"), psum[:, 4, 0:2 * BN]).then_inc(m_at, 1)
                elif g == "turn1":
                    act.wait_ge(m_t, b + 1)
                    for c in range(2):
                        last = fn(mx1t[:, c, :], psum[:, 4, c * BN:(c + 1) * BN], ACT.Identity,
                                  scale=cols[:, C_G1 + c:C_G1 + c + 1], bias=cols[:, C_E1 + c:C_E1 + c + 1])
                    last.then_inc(m_tc, 1)
                else:
                    pair = g
                    act.wait_ge(m_h, b * 4 + pair + 1)
                    for o in range(2):
                        n = 2 * pair + o
                        last = fn(mh[:, n, :], psum[:, 5 + pair % 2, o * BN:(o + 1) * BN], ACT.Relu,
                                  bias=cols[:, C_B1 + n:C_B1 + n + 1])
                    last.then_inc(m_hr, 1)

            mix_at, late_at = {2: "phi", 10: "turn"}, {1: "turn1", 4: 0, 6: 1, 9: 2, 11: 3}

            def b_body(b, u):
                for s in range(SB):
                    k = b * SB + s
                    if s % SU == 0:
                        act.load(regs, walk[0:1, 0, bass.ds(k + LAGW, SU)])
                    start_edges(k, s, regs[s % SU])
                    if not (isinstance(b, int) and b == NB - 1 and s + AHEAD_UP >= SB):
                        upper_att(k + AHEAD_UP, s + AHEAD_UP, b * (SB // RA) + (s + AHEAD_UP) // RA + 1)
                    if s >= LAGD or not (isinstance(b, int) and b == 0):
                        one_hot(k - LAGD, (s - LAGD) % SB, b * (SB // RA) + s // RA)
                    if s in mix_at:
                        mix(b, mix_at[s])
                    if s in late_at and not (isinstance(b, int) and b == 0):
                        mix(b - 1, late_at[s])
                    if s == 14 and not (isinstance(b, int) and b < 2):
                        store_mix(act, b - 2)

            for s in range(AHEAD_UP):
                upper_att(s, s, s // RA + 1)
            twice(act, NB, b_body, (order,))
            for s in range(LAGD):
                one_hot(STEPS - LAGD + s, SB - LAGD + s, STEPS // RA)
            for g in late_at.values():
                mix(NB - 1, g)
            order.reset()

            act.wait_ge(score_done, STEPS)
            for bt in range(CT):
                act.wait_ge(turned, bt + 1)
                copy(sc_a[:, bt * T:(bt + 1) * T], psum[:, bt % 4, 0:T]).then_inc(turned_out, 1)
            act.wait_ge(shifted, 1)
            fn(sc_a, sc_a, ACT.Exp, scale=SCALE).then_inc(exped, 1)
            sview = rec[:, :, :].rearrange("p (b c) m -> p b c m", c=CH)
            for bt in range(CT):
                act.wait_ge(back, bt + 1)
                copy(sview[:, bt, :, 0:H], psum[0:T, bt % 4, 0:128].rearrange("p (c h) -> p c h", c=CH)).then_inc(back_out, 1)

            act.wait_ge(back_out, CT)
            act.wait_ge(rec_ready, 2)

            def d_body(it):
                act.load(regs, walk[0:1, 2, bass.ds(it * SU + LAGP, SU)])
                for s in range(SU):
                    k = it * SU + s
                    place = act.snap(regs[s], min_val=0, max_val=ET - CH - 1)
                    wait(act, sum_done, k - R + 1)
                    copy(pv[:, s, :, D:D + RW], tile_pair(rec, place))
                    act.wait_ge(ev_done, k + 1)
                    copy(vg[:, s, :, :], psum[0:T, s % 2 * 2:s % 2 * 2 + 2, 0:D]).then_inc(meta_ready, 1)

            d_body(0)
            with act.Fori(1, SI) as it:
                d_body(it)

            act.wait_ge(acc_done, STEPS)

            def turned_x(b, u):
                act.wait_ge(f_t, b + 1)
                if not (isinstance(b, int) and b < 2):
                    act.wait_ge(f_lg, b)
                    act.wait_ge(f_h1, (b - 1) * NX)
                copy(fxh[:, u].rearrange("p c n -> p (c n)"), psum[:, 6, 0:2 * BN]).then_inc(f_xh, 1)

            def upper_weights(e):
                for i in range(3):
                    copy(wxh[i][:, e].rearrange("p c n -> p (c n)"), wx[i][:, e].rearrange("p c n -> p (c n)")).then_inc(f_wh, 1)

            def relu(done, used, low, ready, bk, to, layer, b, e):
                n = b * NX + e
                act.wait_ge(done, n + 1)
                wait(act, low, n)
                for o in range(2):
                    col = e * 2 + o
                    last = fn(fh[:, layer, o, :], psum[:, bk + e % 2, o * BN:(o + 1) * BN], ACT.Relu,
                              bias=bns[:, layer, 1, col:col + 1], scale=bns[:, layer, 0, col:col + 1])
                order(last)
                wait(act, used, n - 1)
                copy(to[:, e % 2].rearrange("p c n -> p (c n)"), fh[:, layer].rearrange("p c n -> p (c n)")).then_inc(ready, 1)

            def e_body(b, u, last_block=False):
                for e in range(NX):
                    if isinstance(b, int) and b == 0 and e < NX - 2:
                        upper_weights(e + 2)
                    relu(f_h1, f_h2, f_r1, f_r1h, 0, fh1h, 0, b, e)
                    if e == 0:
                        act.wait_ge(f_sm, b + 1)
                        fn(fsm[:, u, 0:16], fsm[:, u, 0:16], ACT.Exp).then_inc(f_ex, 1)
                    if before(b, e, 1):
                        relu(f_h2, f_y, f_r2, f_r2h, 2, fh2h, 1, *before(b, e, 1))
                    if e == 1:
                        act.wait_ge(f_wt, b + 1)
                        copy(fwt[:, u, :], psum[0:NX, 7, 256:256 + BN]).then_inc(f_wtc, 1)
                    if e == 6 and not last_block:
                        turned_x(b + 1, 1 - u)

            act.wait_ge(c_ff, 48)
            copy(wr_h[:, :, :], wr[:, :, :]).then_inc(f_wh, 1)
            upper_weights(0)
            upper_weights(1)
            act.wait_ge(bn_ready, 2)
            turned_x(0, 0)
            e_body(0, 0)
            e_body(1, 1)
            order.reset()
            with act.Fori(1, NB // 2) as it:
                e_body(it * 2, 0)
                e_body(it * 2 + 1, 1)
                order.reset()
            e_body(NB - 1, 0, last_block=True)
            relu(f_h2, f_y, f_r2, f_r2h, 2, fh2h, 1, NB - 1, NX - 1)

        @block.vector
        def _(dve):
            tt, ts, stt = nc.vector.tensor_tensor, nc.vector.tensor_scalar, nc.vector.scalar_tensor_tensor
            order = Order(dve, dve_o)

            def signal(ins, sem, value):
                ins.then_inc(sem, 1)
                dve.wait_ge(sem, value)

            def root_start(x, eps, y):
                order(ts(x, x, eps, None, ALU.add))
                order(ts(y.bitcast(I32), x.bitcast(I32), 1, None, ALU.logical_shift_right))
                order(ts(y.bitcast(I32), y.bitcast(I32), -1.0, float(0x5F3759DF), ALU.mult, ALU.add))

            def root_step(x, y, t):
                order(stt(t, y, 0.5, y, ALU.mult, ALU.mult))
                order(tt(t, t, x, ALU.mult))
                order(stt(y, t, 1.5, y, ALU.subtract, ALU.mult, reverse0=True))

            def rsqrt(x, eps, y, t):
                root_start(x, eps, y)
                for _ in range(3):
                    root_step(x, y, t)

            var, root, scratch = stats[:, :, 7:8], stats[:, :, 8:9], stats[:, :, 9:10]

            def norm_stats(x):
                for t in range(2):
                    i = nc.vector.bn_stats(stats[:, t, 0:6], x[:, t, :])
                order(i)
                for t in range(2):
                    i = nc.vector.bn_aggr(stats[:, t, 6:8], stats[:, t, 0:6])
                order(i)

            def norm_apply(x, to):
                for t in range(2):
                    i = ts(to[:, t, :], x[:, t, :], stats[:, t, 6:7], stats[:, t, 8:9], ALU.subtract, ALU.mult)
                return i

            def norm2(x, to):
                norm_stats(x)
                rsqrt(var, LN_EPS, root, scratch)
                return norm_apply(x, to)

            def row2(at):
                return rows[:, at:at + D].unsqueeze(1).broadcast_to((T, 2, D))

            nc.vector.memset(zero, 0.0)
            nc.vector.memset(vone.rearrange("p u c n -> p (u c n)"), 1.0).then_inc(zero_ready, 1)
            dve.wait_ge(last_in, 16)
            dve.wait_ge(walk_steps, 4)
            nc.vector.tensor_copy(node[:, :], node_i[:, :])
            order(tt(wf, wz, wi, ALU.add))
            order(nc.vector.tensor_copy(walk_s[:, 0, :], walk_k[:, 0:SU]))
            for s in range(SU):
                order(ts(wl, wf, walk_s[:, 0, s:s + 1], 0.0, ALU.is_lt, ALU.add, accum_out=walk_s[:, 1, s:s + 1]))
            order(ts(walk_s[:, 2, :], walk_s[:, 1, :], float(EP - 1), float(T), ALU.min, ALU.mult))
            order(tt(walk_s[:, 3, :], walk_s[:, 0, :], walk_s[:, 2, :], ALU.subtract))
            order(ts(walk_s[:, 1, :], walk_s[:, 1, :], float(EP - 1), None, ALU.min))
            order(nc.vector.tensor_copy(walk_i[:, 0, :], walk_s[:, 1, :]))
            order(tt(walk_s[:, 4, :], walk_k[:, SU:2 * SU], walk_s[:, 1, :], ALU.subtract))
            order(ts(walk_s[:, 4, :], walk_s[:, 4, :], float(NT - 1), None, ALU.min))
            order(nc.vector.tensor_copy(walk_i[:, 1, :], walk_s[:, 4, :]))
            order(nc.vector.memset(walk_s[:, 5, :], 0.0))
            for c in range(1, CH):
                order(stt(walk_s[:, 5, :], walk_s[:, 1, :], float(CT // 2 * c), walk_s[:, 5, :], ALU.is_ge, ALU.add))
            order(ts(walk_s[:, 4, :], walk_s[:, 1, :], float(2 * CH), None, ALU.mult))
            order(stt(walk_s[:, 4, :], walk_s[:, 5, :], float(1 - CT * CH), walk_s[:, 4, :], ALU.mult, ALU.add))
            nc.vector.tensor_copy(walk_i[:, 2, :], walk_s[:, 4, :]).then_inc(walk_ready, 1)
            nc.vector.memset(walk.rearrange("p w n -> p (w n)"), 0).then_inc(walk_clear, 1)
            order.reset()

            def ln(t, u):
                wait(dve, xn_turned, t - 1)
                wait(dve, xnb_ready, t - 1)
                one, st = bass.ds(t, 1), xstat[:, bass.ds(t, 1), :].rearrange("p o k -> p (o k)")
                ts(xn[:, u, :], x_all[:, one, :].rearrange("p o d -> p (o d)"), st[:, 0:1], st[:, 2:3],
                   ALU.subtract, ALU.mult).then_inc(xn_ready, 1)

            def lower_xnt(t, u):
                dve.wait_ge(xnt_ready, t + 1)
                tt(xnt_l[:, u], xnt[:, u], xnt_h[:, u].bitcast(F32), ALU.subtract).then_inc(xnt_low, 1)

            def phi_k(t, u):
                dve.wait_ge(kexp_ready, t + 1)
                wait(dve, state_done, t - 1)
                stt(kphi[:, u, :], kexp[:, u, :], 1.0, krelu[:, u, :], ALU.min, ALU.add).then_inc(kphi_ready, 1)

            def tables(t, u, last_tile):
                dve.wait_ge(sq_done, t + 1)
                dve.wait_ge(xnb_ready, t + 1)
                if not (isinstance(t, int) and t < 2):
                    dve.wait_ge(a_stored[u], (t - u) * 40)
                x_t = x_all[:, bass.ds(t, 1), :].rearrange("p o d -> p (o d)")
                order(tt(skp[:, u, :], psum[0:T, 2, 0:D], x_t, ALU.add))
                tt(x_t, psum[0:T, 2, D:2 * D], rows[:, R_GNN + D:R_GNN + 2 * D], ALU.add).then_inc(sq_read, 1)
                dve.wait_ge(kv_done, t + 1)
                tt(kv[:, u, :], psum[0:T, 3, :], rows[:, R_GNN + 2 * D:R_GNN + 4 * D], ALU.add).then_inc(gnn_out, 1)
                if not last_tile:
                    lower_xnt(t + 1, 1 - u)
                dve.wait_ge(mkv_done, t + 1)
                wait(dve, state_done, t - 1)
                tt(kt[:, u, :], psum[0:T, 4 + u, 0:D], rows[:, R_MKV:R_MKV + D], ALU.add).then_inc(kt_ready, 1)
                order(tt(vone[:, u, :, 0:128], psum[0:T, 4 + u, D:2 * D].rearrange("p (c n) -> p c n", c=2),
                         rows[:, R_MKV + D:R_MKV + 2 * D].rearrange("p (c n) -> p c n", c=2), ALU.add))

            def a_body(t, u, last_tile=False):
                if not last_tile:
                    ln(t + 1, 1 - u)
                if not (isinstance(t, int) and t == 0):
                    phi_k(t - 1, 1 - u)
                tables(t, u, last_tile)

            for i in range(5):
                dve.wait_ge(x_in[i], 16)
                for t in range(10):
                    last = nc.vector.bn_stats(xsix[:, t, :], x_all[:, i * 10 + t, :])
                order(last)
                for t in range(10):
                    last = nc.vector.bn_aggr(xstat[:, i * 10 + t, 0:2], xsix[:, t, :])
                order(last)
            rsqrt(xstat[:, :, 1:2], LN_EPS, xstat[:, :, 2:3], xstat[:, :, 3:4])
            dve.wait_ge(c_a, CONST_A)
            tt(skip_row, skip_row, rows[:, R_E2:R_E2 + D], ALU.add).then_inc(skip_row_ready, 1)
            order(tt(rows[:, R_B2:R_B2 + D], rows[:, R_B2:R_B2 + D], rows[:, R_E1:R_E1 + D], ALU.add))
            ln(0, 0)
            for half in range(2):
                dve.wait_ge(wa_up, half + 1)
                cut = slice(half * 512, (half + 1) * 512)
                tt(wcat_p[1][:, :, cut], wcat[:, :, cut], wcat_p[0][:, :, cut].bitcast(F32), ALU.subtract).then_inc(wa_low, 1)
                if half == 0:
                    lower_xnt(0, 0)
            dve.wait_ge(wa_up, 3)
            tt(wmkv_p[1], wmkv, wmkv_p[0].bitcast(F32), ALU.subtract).then_inc(wa_low, 1)
            a_body(0, 0)
            a_body(1, 1)
            order.reset()
            with dve.Fori(1, NT // 2 - 1) as it:
                a_body(it * 2, 0)
                a_body(it * 2 + 1, 1)
                order.reset()
            a_body(NT - 2, 0)
            a_body(NT - 1, 1, last_tile=True)
            phi_k(NT - 1, 1)
            dve.wait_ge(state_done, NT + 1)
            for c in range(2):
                order(nc.vector.tensor_copy(ksum[:, c:c + 1], psum[:, 6 + c, 128:129]))
                tt(kvbd[:, c, 0:128], psum[:, 6 + c, 0:128], blockm[:, :], ALU.mult)
                last = ts(kvbd[:, c, 128:KV], blockm[:, ::C], ksum[:, c:c + 1], None, ALU.mult)
            last.then_inc(state_ready, 1)
            order.reset()

            dve.wait_ge(walk_in, 64)
            ts(jneg, jb_all, -1.0, node[:, 0:1], ALU.mult, ALU.subtract).then_inc(jneg_ready, 1)
            order(nc.vector.memset(scores, 0.0))
            order.reset()
            regs = [dve.alloc_register(f"dve_walk{s}") for s in range(SU)]
            score_rows = scores.rearrange("p (e h) -> p e h", h=H)

            dve.wait_ge(we_parts, 1)
            tt(we_l[:, :], we[:, :], we_h[:, :].bitcast(F32), ALU.subtract).then_inc(we_parts, 1)

            def lower_att(k, s):
                dve.wait_ge(att_up, k + 1)
                below = att_parts[ED:2 * ED, s % RP, :]
                tt(below, att_b[ED:2 * ED, s % RA, :], below.bitcast(F32), ALU.subtract).then_inc(att_low, 1)

            def multiply(k, s, turn_of):
                dve.wait_ge(gathered[s % RK], turn_of * 32)
                dve.wait_ge(q_done, k + 1)
                flat = kg[s % RK].rearrange("p w d -> p (w d)")
                tt(flat, flat, psum[0:T, 2 + s % 2, :], ALU.mult).then_inc(mult_done, 1)

            def total(k, s):
                dve.wait_ge(mult_done, k + 1)
                wait(dve, score_done, k - 2)
                nc.vector.tensor_reduce(part[:, s % 3, :], kg[s % RK].rearrange("p w (h c) -> p (w h) c", c=C),
                                        AX, ALU.add).then_inc(red_done, 1)

            def keep(k, s, reg):
                to = tile_pair(score_rows, dve.snap(reg, min_val=0, max_val=ET - CH - 1))
                dve.wait_ge(red_done, k + 1)
                wait(dve, score_done, k)
                tt(to, to, part[:, s % 3, :].rearrange("p (w h) -> p w h", w=2), ALU.add).then_inc(score_done, 1)

            def mix(b, u, g):
                if g == "phi":
                    dve.wait_ge(m_exp, b + 1)
                    stt(mqp, mqe, 1.0, mq, ALU.min, ALU.add).then_inc(m_phi, 1)
                elif g == "attend":
                    dve.wait_ge(m_nd, b + 1)
                    den = mden.rearrange("p o t h -> p (o t h)")
                    both = [psum[0:T, 4 + 3 * t, 0:2 * KV].rearrange("p (c n) -> p c n", c=2) for t in range(2)]
                    for t in range(2):
                        i = ts(mden[:, 0, t].rearrange("p (c h) -> p c h", c=2), both[t][:, :, 128:KV], Z_EPS, None, ALU.add)
                    order(i)
                    order(nc.vector.reciprocal(den[:, 2 * H:4 * H], den[:, 0:2 * H]))
                    for t in range(2):
                        i = tt(matn[:, t, :].rearrange("p (c h d) -> p c h d", c=2, d=C),
                               both[t][:, :, 0:128].rearrange("p c (h d) -> p c h d", d=C),
                               mden[:, 1, t, :].rearrange("p (c h) -> p c h", c=2).unsqueeze(3).broadcast_to((T, 2, H // 2, C)), ALU.mult)
                    i.then_inc(m_an, 1)
                elif g == "sum1":
                    dve.wait_ge(m_o, b + 1)
                    dve.wait_ge(m_xn_in[u], (b // 2 + 1) * 16 if isinstance(b, int) else (b - u) * 8 + 16)
                    order(tt(my[:, u], psum[0:T, 7, :].rearrange("p (t d) -> p t d", t=2), mxn[:, u], ALU.add))
                elif g == "stats1":
                    norm_stats(my[:, u])
                elif g == "norm1":
                    signal(norm_apply(my[:, u], mx1), m_x1, b + 1)
                elif g == "gain1":
                    order(tt(my[:, u], mx1, row2(R_G1), ALU.mult))
                elif g == "root":
                    root_start(var, LN_EPS, root)
                    root_step(var, root, scratch)
                elif g == "root2":
                    root_step(var, root, scratch)
                    root_step(var, root, scratch)
                elif g == "sum2":
                    dve.wait_ge(m_y, b + 1)
                    wait(dve, m_stored, b * 16)
                    signal(tt(mout[:, :, :], psum[0:T, 6, :].rearrange("p (t d) -> p t d", t=2), my[:, u], ALU.add), m_y_read, b + 1)
                    order(tt(mout[:, :, :], mout[:, :, :], row2(R_B2), ALU.add))
                elif g == "stats2":
                    norm_stats(mout)
                elif g == "norm2":
                    order(norm_apply(mout, mx2))
                elif g == "gain2":
                    order(tt(mx2[:, :, :], mx2[:, :, :], row2(R_G2), ALU.mult))
                elif g == "add2":
                    dve.wait_ge(m_res_in, (b + 1) * 16)
                    tt(mout[:, :, :], mx2[:, :, :], mres[:, :, :], ALU.add).then_inc(m_outr, 1)

            mix_at = {0: "phi", 3: "attend", 8: "sum1", 9: "stats1", 10: "root", 11: "root2", 12: "norm1", 13: "gain1"}
            late_at = {15: "sum2", 16: "stats2", 17: "root"}
            last_at = {1: "root2", 4: "norm2", 5: "gain2", 6: "add2"}

            def b_body(b, u):
                for s in range(SB):
                    k = b * SB + s
                    if s % SU == 0:
                        dve.load(regs, walk[0:1, 2, bass.ds(k, SU)])
                    if not (isinstance(b, int) and b == NB - 1 and s + AHEAD_LOW >= SB):
                        lower_att(k + AHEAD_LOW, s + AHEAD_LOW)
                    if s in last_at and not (isinstance(b, int) and b < 2):
                        mix(b - 2, u, last_at[s])
                    if s in late_at and not (isinstance(b, int) and b == 0):
                        mix(b - 1, 1 - u, late_at[s])
                    if s in mix_at:
                        mix(b, u, mix_at[s])
                    multiply(k, s, b * (SB // RK) + s // RK + 1)
                    if s >= 1 or not (isinstance(b, int) and b == 0):
                        total(k - 1, (s - 1) % SB)
                    if s >= LAGP or not (isinstance(b, int) and b == 0):
                        keep(k - LAGP, (s - LAGP) % SB, regs[s % SU])

            for s in range(AHEAD_LOW):
                lower_att(s, s)
            twice(dve, NB, b_body, (order,))
            total(STEPS - 1, SB - 1)
            dve.load(regs, walk[0:1, 2, STEPS:STEPS + SU])
            for s in range(LAGP):
                keep(STEPS - LAGP + s, SB - LAGP + s, regs[s])
            for g in last_at.values():
                mix(NB - 2, (NB - 2) % 2, g)
            order.reset()
            for layer in range(2):
                col = [cols[:, C_FF + (layer * 5 + i) * 16:C_FF + (layer * 5 + i + 1) * 16] for i in range(5)]
                b_, g_, be_, m_, v_ = col
                scale, bias = bns[:, layer, 0, :], bns[:, layer, 1, :]
                rsqrt(v_, BN_EPS, scale, bias)
                order(tt(scale, scale, g_, ALU.mult))
                order(tt(bias, b_, m_, ALU.subtract))
                order(tt(bias, bias, scale, ALU.mult))
                tt(bias, bias, be_, ALU.add).then_inc(bn_ready, 1)
            order.reset()

            dve.wait_ge(dst_in, 16 * 2 * CH)
            nc.vector.memset(sc_m[:, 0:1], 0.0)
            nc.vector.memset(sc_m[:, CE:CE + 1], 0.0)
            nc.vector.tensor_copy(ends[:, 2:3], sc_d[0][:, 0:1])
            nc.vector.tensor_copy(ends[:, 3:4], sc_d[1][:, CE - CUT:CE - CUT + 1])
            for piece, at in zip(sc_d, (1, CUT)):
                n = piece.shape[1] - 1
                last = tt(sc_m[:, at:at + n], piece[:, 1:n + 1], piece[:, 0:n], ALU.is_equal)
            last.then_inc(mask_ready, 1)
            dve.wait_ge(mask_ready, 1)
            order(ts(sc_m[:, 1:CE], sc_m[:, 1:CE], BIG, -BIG, ALU.mult, ALU.add))
            for g in [*late_at.values(), *last_at.values()]:
                mix(NB - 1, (NB - 1) % 2, g)
            order.reset()

            dve.wait_ge(turned_out, CT)
            dve.wait_ge(c_walk, 32)
            dve.wait_ge(turned, CT)
            by_place = rec[:, :, :].rearrange("p (b c) m -> p c b m", c=CH)
            nc.vector.tensor_copy(by_place[:, :, :, H], dst_t[:, :].rearrange("p (c b) -> p c b", c=CH)).then_inc(rec_ready, 1)
            nc.vector.tensor_copy(by_place[:, :, :, H + 1].bitcast(I32), src_t[:, :].rearrange("p (c b) -> p c b", c=CH)).then_inc(rec_ready, 1)
            nc.vector.memset(att_d[ED:2 * ED].rearrange("p r t -> p (r t)"), 0.0).then_inc(att_zero, 1)
            dve.wait_ge(m_stored, 16 * NB)
            scan = nc.vector.tensor_tensor_scan
            m_fwd, m_bwd = sc_m[:, 0:CE], sc_m[:, 1:CE + 1][:, ::-1]
            order(scan(sc_f, m_fwd, sc_a, -BIG, ALU.add, ALU.max))
            order(nc.vector.tensor_copy(ends[:, 0:1], sc_f[:, CE - 1:CE]))
            order(scan(sc_f[:, ::-1], m_bwd, sc_a[:, ::-1], -BIG, ALU.add, ALU.max))
            nc.vector.tensor_copy(ends[:, 1:2], sc_f[:, 0:1]).then_inc(ends_ready, 1)
            dve.wait_ge(fence_in, 16)
            nc.vector.memset(fence[:, 4, 0:1], 0.0)
            tt(fence[:, 4, 1:CH], fence[:, 2, 1:CH], fence[:, 3, 0:CH - 1], ALU.is_equal)
            order(tt(fence[:, 5, :], fence[:, 2, :], fence[:, 3, :], ALU.is_equal))
            order(ts(fence[:, 4:6, :], fence[:, 4:6, :], BIG, -BIG, ALU.mult, ALU.add))
            nc.vector.memset(fence[:, 8:10, :], -BIG)
            order(tt(fence[:, 6, :], fence[:, 4, :], fence[:, 5, :], ALU.add))
            order(scan(fence[:, 7, :], fence[:, 6, :], fence[:, 0, :], -BIG, ALU.add, ALU.max))
            order(tt(fence[:, 8, 1:CH], fence[:, 7, 0:CH - 1], fence[:, 4, 1:CH], ALU.add))
            order(nc.vector.memset(fence[:, 6, CH - 1:CH], -BIG))
            order(tt(fence[:, 6, 0:CH - 1], fence[:, 4, 1:CH], fence[:, 5, 0:CH - 1], ALU.add))
            order(scan(fence[:, 7, ::-1], fence[:, 6, ::-1], fence[:, 1, ::-1], -BIG, ALU.add, ALU.max))
            tt(fence[:, 9, 0:CH - 1], fence[:, 7, 1:CH], fence[:, 4, 1:CH], ALU.add).then_inc(carry_ready, 1)
            dve.wait_ge(fence_in, 32)
            order(scan(sc_f, m_fwd, sc_a, ends[:, 4:5], ALU.add, ALU.max))
            order(scan(sc_f[:, ::-1], m_bwd, sc_f[:, ::-1], ends[:, 5:6], ALU.add, ALU.max))
            tt(sc_a, sc_a, sc_f, ALU.subtract).then_inc(shifted, 1)

            dve.wait_ge(back, CT)
            order(nc.vector.memset(acc[:, 0:NT // 2, :], 0.0))
            order.reset()
            dve.wait_ge(acc_zero, 1)

            def add(k, s, reg):
                j = dve.snap(reg, min_val=0, max_val=NT - 1)
                dve.wait_ge(sum_done, k + 1)
                wait(dve, acc_done, k)
                to = acc[:, bass.ds(j, 1), :].rearrange("p o f -> p (o f)")
                tt(to, to, psum[0:T, 4 + s % 2, 0:PV], ALU.add).then_inc(acc_done, 1)

            def d_body(it):
                dve.load(regs, walk[0:1, 1, bass.ds(it * SU + LAGQ - LAG, SU)])
                for s in range(SU):
                    k = it * SU + s
                    dve.wait_ge(meta_ready, k + 1)
                    wait(dve, sum_done, k - RA + 1)
                    for w in range(2):
                        ts(hot[:, s % RA, w, :], iota[:, :], jb_all[:, bass.ds(k, 1)], pv[:, s, w, D + H:D + H + 1], ALU.add, ALU.is_equal)
                    dve.wait_ge(v_in[s], it * 32 + 32)
                    tt(pv[:, s, :, 0:D].rearrange("p w (h c) -> p w h c", h=H), vg[:, s].rearrange("p w (h c) -> p w h c", h=H),
                       pv[:, s, :, D:PV].unsqueeze(3).broadcast_to((T, 2, H, C)), ALU.mult).then_inc(pv_ready, 1)
                    if s >= LAG or not (isinstance(it, int) and it == 0):
                        add(k - LAG, s, regs[s])

            d_body(0)
            with dve.Fori(1, SI) as it:
                d_body(it)
            dve.load(regs, walk[0:1, 1, STEPS + LAGQ - LAG:STEPS + LAGQ - LAG + SU])
            for s in range(LAG):
                add(STEPS - LAG + s, s, regs[s])

            dve.wait_ge(acc_done, STEPS)

            def residual(b, u):
                dve.wait_ge(f_in[u], (b // 2 + 1) * 16 if isinstance(b, int) else (b - u) * 8 + 16)
                wait(dve, f_t, b)
                both = acc[:, bass.ds(b * 2, 2), :]
                rs = fsm[:, u, 16:32].rearrange("p (t h) -> p t h", t=2)
                order(ts(rs, both[:, :, D:PV], S_EPS, None, ALU.add))
                order(nc.vector.reciprocal(rs, rs))
                for t in range(2):
                    one = acc[:, bass.ds(b * 2 + t, 1), :].rearrange("p o f -> p (o f)")
                    i = tt(fgn[:, t, :].rearrange("p (h c) -> p h c", h=H), one[:, 0:D].rearrange("p (h c) -> p h c", h=H),
                           rs[:, t, :].unsqueeze(2).broadcast_to((T, H, C)), ALU.mult)
                order(i)
                order(tt(fx2[:, u], fgn, fres[:, u], ALU.add))
                norm_stats(fx2[:, u])

            def residual_norm(b, u):
                norm_apply(fx2[:, u], fxn).then_inc(f_xn, 1)

            def lower_x(b, u):
                dve.wait_ge(f_xh, b + 1)
                tt(fxl[:, u].rearrange("p c n -> p (c n)"), psum[:, 6, 0:2 * BN],
                   fxh[:, u].rearrange("p c n -> p (c n)").bitcast(F32), ALU.subtract).then_inc(f_tc, 1)

            def lower_weights(e):
                for i in range(3):
                    dve.wait_ge(f_wh, 1 + e * 3 + i + 1)
                    tt(wxl[i][:, e].rearrange("p c n -> p (c n)"), wx[i][:, e].rearrange("p c n -> p (c n)"),
                       wxh[i][:, e].rearrange("p c n -> p (c n)").bitcast(F32), ALU.subtract).then_inc(f_wl, 1)

            def lower(upper_ready, ready, used, up, low, layer, b, e):
                n = b * NX + e
                dve.wait_ge(upper_ready, n + 1)
                wait(dve, used, n - 1)
                tt(low[:, e % 2].rearrange("p c n -> p (c n)"), fh[:, layer].rearrange("p c n -> p (c n)"),
                   up[:, e % 2].rearrange("p c n -> p (c n)").bitcast(F32), ALU.subtract).then_inc(ready, 1)

            logits = [fsm[:, u, 0:16].rearrange("p (t e) -> p t e", t=2) for u in range(2)]
            mx = stats[:, :, 12:13]

            def router(b, u):
                dve.wait_ge(f_lg, b + 1)
                lg = logits[u]
                order(tt(lg, psum[0:T, 7, 0:16].rearrange("p (t e) -> p t e", t=2),
                         rows[:, R_BR:R_BR + NX].unsqueeze(1).broadcast_to((T, 2, NX)), ALU.add))
                order(nc.vector.tensor_reduce(mx, lg, AX, ALU.max))
                tt(lg, lg, mx.broadcast_to((T, 2, NX)), ALU.subtract).then_inc(f_sm, 1)

            def gates(b, u):
                dve.wait_ge(f_ex, b + 1)
                order(nc.vector.tensor_reduce(mx, logits[u], AX, ALU.add))
                order(nc.vector.reciprocal(mx, mx))
                signal(tt(fw[:, u], logits[u], mx.broadcast_to((T, 2, NX)), ALU.mult), f_w, b + 1)

            def bias_out(b, u):
                dve.wait_ge(f_bo_done, b + 1)
                if not (isinstance(b, int) and b < 2):
                    dve.wait_ge(f_stored[u], (b - u) * 8)
                signal(tt(fyb[:, u], psum[0:T, 7, :].rearrange("p (t d) -> p t d", t=2), fx2[:, u], ALU.add), f_bo, b + 1)

            def gate(b, e, u):
                n = b * NX + e
                dve.wait_ge(f_y, n + 1)
                for t in range(2):
                    i = stt(fyb[:, u, t, :], psum[0:T, 4 + e % 2, t * D:(t + 1) * D], fw[:, u, t, e:e + 1], fyb[:, u, t, :],
                            ALU.mult, ALU.add)
                signal(i, f_ya, n + 1)

            def e_body(b, u, last_block=False):
                for e in range(NX):
                    if before(b, e, 3):
                        gate(*before(b, e, 3), u if e >= 3 else 1 - u)
                    if e == 2 and before(b, e, 3):
                        stored(b - 1)
                    if e == 0:
                        router(b, u)
                    if isinstance(b, int) and b == 0 and e >= 1:
                        lower_weights(e)
                    lower(f_r1h, f_r1, f_h2, fh1h, fh1l, 0, b, e)
                    if e == 0:
                        gates(b, u)
                    if before(b, e, 1):
                        lower(f_r2h, f_r2, f_y, fh2h, fh2l, 1, *before(b, e, 1))
                    if e == 2:
                        bias_out(b, u)
                    if not last_block:
                        if e == 1:
                            residual(b + 1, 1 - u)
                        elif e == 3:
                            root_start(var, LN_EPS, root)
                            root_step(var, root, scratch)
                        elif e == 4:
                            root_step(var, root, scratch)
                            root_step(var, root, scratch)
                        elif e == 5:
                            residual_norm(b + 1, 1 - u)
                        elif e == 6:
                            lower_x(b + 1, 1 - u)

            def stored(b):
                dve.wait_ge(f_ya, b * NX + NX)
                dve.sem_inc(f_outr, 1)

            residual(0, 0)
            rsqrt(var, LN_EPS, root, scratch)
            residual_norm(0, 0)
            dve.wait_ge(f_wh, 1)
            tt(wr_l[:, :, :], wr[:, :, :], wr_h[:, :, :].bitcast(F32), ALU.subtract).then_inc(f_wl, 1)
            lower_weights(0)
            lower_x(0, 0)
            e_body(0, 0)
            e_body(1, 1)
            order.reset()
            with dve.Fori(1, NB // 2) as it:
                e_body(it * 2, 0)
                e_body(it * 2 + 1, 1)
                order.reset()
            e_body(NB - 1, 0, last_block=True)
            lower(f_r2h, f_r2, f_y, fh2h, fh2l, 1, NB - 1, NX - 1)
            for e in range(NX - 3, NX):
                gate(NB - 1, e, 0)
            stored(NB - 1)


_OUT = (N, D)


def kernel(**inputs):
    import concourse.bacc as bacc
    from concourse.bass_utils import run_bass_kernel_spmd

    g = {k: np.asarray(v) for k, v in inputs.items()}

    def gnn(n):
        return g["L0_gnn_" + n]

    def mix(n):
        return g["L0_mix_" + n]

    def ffn(n):
        return g["L0_ffn_" + n]

    def columns(v):
        return np.ascontiguousarray(v.reshape(-1, 128).T)

    row = np.concatenate([gnn("bskip"), gnn("bq"), gnn("bk"), gnn("bv"), mix("bk"), mix("bv"), mix("bo"), mix("b2"),
                          mix("ln1_g"), mix("ln1_b"), mix("ln2_g"), mix("ln2_b"), ffn("br")])
    dst = g["dst"].astype(np.int32, copy=False)
    src = g["src"].astype(np.int32, copy=False)

    def by_tile(v):
        return v.reshape(ET, T).T

    arrays = {
        "x": g["x"],
        "dst": dst,
        "src_t": by_tile(src),
        "dst_t": by_tile(dst),
        "dst_last": dst.reshape(EP, E2)[:, E2 - 1].reshape(1, EP),
        "attr_t": g["edge_attr_64"].T,
        "w_gnn": np.concatenate([gnn("Wskip").T, gnn("Wq").T, gnn("Wk").T, gnn("Wv").T], 1),
        "w_e": np.ascontiguousarray(gnn("We").T),
        "w_mkv": np.concatenate([mix("Wk"), mix("Wv")], 1),
        "w_mq": mix("Wq"), "w_mo": mix("Wo"), "w_m1": mix("W1"), "w_m2": mix("W2"),
        "w_x1": ffn("W1").reshape(NX * D, D), "w_x2": ffn("W2").reshape(NX * D, D), "w_xo": ffn("Wo").reshape(NX * D, D),
        "w_r": ffn("Wr"), "bo_e": ffn("bo"),
        "rows": np.ascontiguousarray(np.broadcast_to(row, (T, ROWS))),
        "cols": np.concatenate([columns(mix("bq")), columns(mix("b1")), columns(mix("ln1_g")), columns(mix("ln1_b"))]
                               + [columns(ffn(n + i)) for i in "12" for n in ("b", "g", "be", "m", "v")], 1),
        "ident": np.eye(128, dtype=np.float32),
        "blockm": np.kron(np.eye(128 // C, dtype=np.float32), np.ones((C, C), np.float32)),
        "iota": np.ascontiguousarray(np.broadcast_to(np.arange(T, dtype=np.float32), (T, T))),
    }
    arrays = {k: np.ascontiguousarray(v) for k, v in arrays.items()}
    from concourse import mybir as _mybir

    nc = bacc.Bacc("TRN2", target_bir_lowering=False, num_devices=1)
    aps = {n: nc.dram_tensor("in_" + n, v.shape, _mybir.dt.from_np(v.dtype), kind="ExternalInput").ap()
           for n, v in arrays.items()}
    out = nc.dram_tensor("out_0", _OUT, F32, kind="ExternalOutput").ap()
    build(nc, aps, out)
    r = run_bass_kernel_spmd(nc, [{"in_" + n: v for n, v in arrays.items()}], core_ids=[0])
    return r.results[0]["out_0"]
```
